# Optimizing a Trainium2 kernel written in Bass

```python
import numpy as np
import jax
import jax.numpy as jnp

def _softmax(x, axis=-1):
    return jax.nn.softmax(x, axis=axis)

def _gelu(x):
    return jax.nn.gelu(x, approximate=True)

def _silu(x):
    return jax.nn.silu(x)

def _sigmoid(x):
    return jax.nn.sigmoid(x)

def _layernorm(x, axis=-1, eps=1e-05):
    m = jnp.mean(x, axis=axis, keepdims=True)
    v = jnp.var(x, axis=axis, keepdims=True)
    return (x - m) / jnp.sqrt(v + eps)

def _scatter_add(tgt, idx, src, axis=0):
    return tgt.at[idx].add(src)

def _segment_sum(src, seg, n):
    return jax.ops.segment_sum(src, seg, n)
kernel_name = 'mk_xattn_seq_d2_seqx_r4_f9a3ee'

def setup_inputs(seed: int=0):
    np.random.seed(seed)
    _w = jnp.asarray

    def _rec_inputs():
        import jax
        import jax.numpy as jnp
        _rk = jax.random.key(seed)
        x = -0.0002928 + 1 * jax.random.normal(jax.random.fold_in(_rk, 1), (128, 128, 256), jnp.float32)
        _lenS = 128 - jax.random.randint(jax.random.fold_in(_rk, 7), (128,), 0, max(1, 128 // 4) + 1, jnp.int32)
        _lenS2 = 128 - jax.random.randint(jax.random.fold_in(_rk, 8), (128,), 0, max(1, 128 // 4) + 1, jnp.int32)
        _ctx_1024P = jax.random.normal(jax.random.fold_in(_rk, 11), (128, 16, 256), jnp.float32)
        _ctx_1024c = jax.random.dirichlet(jax.random.fold_in(_rk, 511), 0.3 * jnp.ones((16,), jnp.float32), (128, 128))
        _ctx_1024t = jnp.einsum('bsk,bkd->bsd', _ctx_1024c, _ctx_1024P)
        _ctx_1024t = _ctx_1024t * jax.lax.rsqrt(jnp.mean(jnp.square(_ctx_1024t)) + 1e-12) * 0.953939
        ctx_1024 = -1.39393e-06 + 0.999914 * (_ctx_1024t + 0.3 * jax.random.normal(jax.random.fold_in(_rk, 611), (128, 128, 256), jnp.float32))
        _validS = jnp.arange(128)[None, :] < _lenS[:, None]
        _validS2 = jnp.arange(128)[None, :] < _lenS2[:, None]
        _causal = jnp.tril(jnp.ones((128, 128), dtype=bool))
        mask_1x1xSxS2_fk1 = jnp.where(jnp.broadcast_to(_validS2[0:1, None, None, :], (1, 1, 128, 128)), 1.0, 0.0).astype(jnp.float32)
        mask_Bx1x1xS2_fk0 = jnp.where(jnp.broadcast_to(_validS2[:, None, None, :], (128, 1, 1, 128)), 0.0, 1.0).astype(jnp.float32)
        return (x, ctx_1024, mask_1x1xSxS2_fk1, mask_Bx1x1xS2_fk0)
    x, ctx_1024, mask_1x1xSxS2_fk1, mask_Bx1x1xS2_fk0 = _rec_inputs()

    def _L0_xattn_setup():
        import jax, jax.numpy as jnp
        import numpy as np
        H = 8
        LN_EPS = 1e-05

        def _gconv(x, w):
            xp = jnp.pad(x, ((0, 0), (0, 0), (1, 1)), mode='reflect')
            return jax.lax.conv_general_dilated(xp, w, window_strides=(1,), padding='VALID', feature_group_count=H, dimension_numbers=('NCH', 'OIH', 'NCH'))
        key = jax.random.key(seed)
        ks = jax.random.split(key, 5)
        B, C, L = (8, 128, 256)
        q = jax.random.normal(ks[0], (B, C, L), jnp.float32)
        k = jax.random.normal(ks[1], (B, C, L), jnp.float32)
        mask = jnp.triu(jnp.ones((L, L), jnp.float32), k=1)
        std = float(np.sqrt(2.0 / (C + C // H)))
        wq = jax.random.normal(ks[2], (C, C // H, 3), jnp.float32) * std
        wk = jax.random.normal(ks[3], (C, C // H, 3), jnp.float32) * std
        wv = jax.random.normal(ks[4], (C, C // H, 3), jnp.float32) * std
        gamma = jnp.ones((C,), jnp.float32)
        beta = jnp.zeros((C,), jnp.float32)
        return {'q': q, 'k': k, 'mask': mask, 'wq': wq, 'wk': wk, 'wv': wv, 'gamma': gamma, 'beta': beta}
    _L0_xattn_all = _L0_xattn_setup()
    _L0_xattn_in = {k: v for k, v in _L0_xattn_all.items() if k in ('mask', 'wq', 'wk', 'wv', 'gamma', 'beta')}
    del _L0_xattn_all

    def _L1_xattn_setup():
        import jax, jax.numpy as jnp
        import numpy as np
        D_MODEL = 256
        N_HEADS = 16
        DFF = 1024
        B, S = (2, 512)
        EPS = 1e-06

        def _dense_params(key, d_in, d_out):
            kw, kb = jax.random.split(key)
            w = jax.random.normal(kw, (d_in, d_out), jnp.float32) * 0.02
            b = jax.random.normal(kb, (d_out,), jnp.float32) * 0.02
            return (w, b)

        def _layernorm(x, g, b):
            mu = jnp.mean(x, axis=-1, keepdims=True)
            var = jnp.mean(jnp.square(x - mu), axis=-1, keepdims=True)
            return (x - mu) * jax.lax.rsqrt(var + EPS) * g + b

        def _mha(v, k, q, mask, wq, bq, wk, bk, wv, bv, wo, bo):
            Bq, Sq, D = q.shape
            depth = D // N_HEADS

            def split(t):
                return t.reshape(t.shape[0], -1, N_HEADS, depth).transpose(0, 2, 1, 3)
            qh = split(q @ wq + bq)
            kh = split(k @ wk + bk)
            vh = split(v @ wv + bv)
            logits = jnp.einsum('bhqd,bhkd->bhqk', qh, kh) / jnp.sqrt(jnp.float32(depth))
            if mask is not None:
                logits = logits + mask * -1000000000.0
            attn = jax.nn.softmax(logits, axis=-1)
            out = jnp.einsum('bhqk,bhkd->bhqd', attn, vh)
            out = out.transpose(0, 2, 1, 3).reshape(Bq, Sq, D)
            return out @ wo + bo
        key = jax.random.key(seed)
        ks = jax.random.split(key, 20)
        inp = {'x': jax.random.normal(ks[0], (B, S, D_MODEL), jnp.float32), 'enc_output': jax.random.normal(ks[1], (B, S, D_MODEL), jnp.float32), 'look_ahead_mask': jnp.triu(jnp.ones((S, S), jnp.float32), k=1)[None, None], 'padding_mask': (jax.random.uniform(ks[2], (B, 1, 1, S)) < 0.1).astype(jnp.float32)}
        names = ['mha1_wq', 'mha1_wk', 'mha1_wv', 'mha1_wo', 'mha2_wq', 'mha2_wk', 'mha2_wv', 'mha2_wo']
        for i, n in enumerate(names):
            w, b = _dense_params(ks[3 + i], D_MODEL, D_MODEL)
            inp[n] = w
            inp[n.replace('w', 'b')] = b
        inp['ffn_w1'], inp['ffn_b1'] = _dense_params(ks[11], D_MODEL, DFF)
        inp['ffn_w2'], inp['ffn_b2'] = _dense_params(ks[12], DFF, D_MODEL)
        for i, n in enumerate(['ln1', 'ln2', 'ln3']):
            inp[n + '_g'] = jnp.ones((D_MODEL,), jnp.float32)
            inp[n + '_b'] = jnp.zeros((D_MODEL,), jnp.float32)
        return inp
    _L1_xattn_all = _L1_xattn_setup()
    _L1_xattn_in = {k: v for k, v in _L1_xattn_all.items() if k in ('mha1_wq', 'mha1_bq', 'mha1_wk', 'mha1_bk', 'mha1_wv', 'mha1_bv', 'mha1_wo', 'mha1_bo', 'mha2_wq', 'mha2_bq', 'mha2_wk', 'mha2_bk', 'mha2_wv', 'mha2_bv', 'mha2_wo', 'mha2_bo', 'ffn_w1', 'ffn_b1', 'ffn_w2', 'ffn_b2', 'ln1_g', 'ln1_b', 'ln2_g', 'ln2_b', 'ln3_g', 'ln3_b')}
    del _L1_xattn_all
    return {'x': x, 'ctx_1024': ctx_1024, 'mask_1x1xSxS2_fk1': mask_1x1xSxS2_fk1, 'mask_Bx1x1xS2_fk0': mask_Bx1x1xS2_fk0, 'L0_xattn_mask': _L0_xattn_in['mask'], 'L0_xattn_wq': _L0_xattn_in['wq'], 'L0_xattn_wk': _L0_xattn_in['wk'], 'L0_xattn_wv': _L0_xattn_in['wv'], 'L0_xattn_gamma': _L0_xattn_in['gamma'], 'L0_xattn_beta': _L0_xattn_in['beta'], 'L1_xattn_mha1_wq': _L1_xattn_in['mha1_wq'], 'L1_xattn_mha1_bq': _L1_xattn_in['mha1_bq'], 'L1_xattn_mha1_wk': _L1_xattn_in['mha1_wk'], 'L1_xattn_mha1_bk': _L1_xattn_in['mha1_bk'], 'L1_xattn_mha1_wv': _L1_xattn_in['mha1_wv'], 'L1_xattn_mha1_bv': _L1_xattn_in['mha1_bv'], 'L1_xattn_mha1_wo': _L1_xattn_in['mha1_wo'], 'L1_xattn_mha1_bo': _L1_xattn_in['mha1_bo'], 'L1_xattn_mha2_wq': _L1_xattn_in['mha2_wq'], 'L1_xattn_mha2_bq': _L1_xattn_in['mha2_bq'], 'L1_xattn_mha2_wk': _L1_xattn_in['mha2_wk'], 'L1_xattn_mha2_bk': _L1_xattn_in['mha2_bk'], 'L1_xattn_mha2_wv': _L1_xattn_in['mha2_wv'], 'L1_xattn_mha2_bv': _L1_xattn_in['mha2_bv'], 'L1_xattn_mha2_wo': _L1_xattn_in['mha2_wo'], 'L1_xattn_mha2_bo': _L1_xattn_in['mha2_bo'], 'L1_xattn_ffn_w1': _L1_xattn_in['ffn_w1'], 'L1_xattn_ffn_b1': _L1_xattn_in['ffn_b1'], 'L1_xattn_ffn_w2': _L1_xattn_in['ffn_w2'], 'L1_xattn_ffn_b2': _L1_xattn_in['ffn_b2'], 'L1_xattn_ln1_g': _L1_xattn_in['ln1_g'], 'L1_xattn_ln1_b': _L1_xattn_in['ln1_b'], 'L1_xattn_ln2_g': _L1_xattn_in['ln2_g'], 'L1_xattn_ln2_b': _L1_xattn_in['ln2_b'], 'L1_xattn_ln3_g': _L1_xattn_in['ln3_g'], 'L1_xattn_ln3_b': _L1_xattn_in['ln3_b']}

def reference(x, ctx_1024, mask_1x1xSxS2_fk1, mask_Bx1x1xS2_fk0, L0_xattn_mask, L0_xattn_wq, L0_xattn_wk, L0_xattn_wv, L0_xattn_gamma, L0_xattn_beta, L1_xattn_mha1_wq, L1_xattn_mha1_bq, L1_xattn_mha1_wk, L1_xattn_mha1_bk, L1_xattn_mha1_wv, L1_xattn_mha1_bv, L1_xattn_mha1_wo, L1_xattn_mha1_bo, L1_xattn_mha2_wq, L1_xattn_mha2_bq, L1_xattn_mha2_wk, L1_xattn_mha2_bk, L1_xattn_mha2_wv, L1_xattn_mha2_bv, L1_xattn_mha2_wo, L1_xattn_mha2_bo, L1_xattn_ffn_w1, L1_xattn_ffn_b1, L1_xattn_ffn_w2, L1_xattn_ffn_b2, L1_xattn_ln1_g, L1_xattn_ln1_b, L1_xattn_ln2_g, L1_xattn_ln2_b, L1_xattn_ln3_g, L1_xattn_ln3_b):
    import jax
    import jax.numpy as jnp

    def _L0_xattn_ref(q, k, mask, wq, wk, wv, gamma, beta):
        import jax, jax.numpy as jnp
        import numpy as np
        H = 8
        LN_EPS = 1e-05

        def _gconv(x, w):
            xp = jnp.pad(x, ((0, 0), (0, 0), (1, 1)), mode='reflect')
            return jax.lax.conv_general_dilated(xp, w, window_strides=(1,), padding='VALID', feature_group_count=H, dimension_numbers=('NCH', 'OIH', 'NCH'))
        init = q
        B, C, L = q.shape
        D = C // H
        v = k
        qh = _gconv(q, wq).reshape(B, H, D, L)
        kh = _gconv(k, wk).reshape(B, H, D, L)
        vh = _gconv(v, wv).reshape(B, H, D, L)
        scores = jnp.einsum('bhdl,bhdm->bhlm', qh, kh) / jnp.sqrt(jnp.asarray(H, qh.dtype))
        scores = scores - 1000000000.0 * mask
        att = jax.nn.softmax(scores, axis=-1)
        o = jnp.einsum('bhlm,bhdm->blhd', att, vh).reshape(B, L, C)
        x = o + jnp.swapaxes(init, 1, 2)
        mu = jnp.mean(x, axis=-1, keepdims=True)
        var = jnp.mean(jnp.square(x - mu), axis=-1, keepdims=True)
        y = (x - mu) * jax.lax.rsqrt(var + LN_EPS) * gamma + beta
        return jnp.swapaxes(y, 1, 2)

    def _L1_xattn_ref(x, enc_output, look_ahead_mask, padding_mask, mha1_wq, mha1_bq, mha1_wk, mha1_bk, mha1_wv, mha1_bv, mha1_wo, mha1_bo, mha2_wq, mha2_bq, mha2_wk, mha2_bk, mha2_wv, mha2_bv, mha2_wo, mha2_bo, ffn_w1, ffn_b1, ffn_w2, ffn_b2, ln1_g, ln1_b, ln2_g, ln2_b, ln3_g, ln3_b):
        import jax, jax.numpy as jnp
        import numpy as np
        D_MODEL = 256
        N_HEADS = 16
        DFF = 1024
        B, S = (2, 512)
        EPS = 1e-06

        def _dense_params(key, d_in, d_out):
            kw, kb = jax.random.split(key)
            w = jax.random.normal(kw, (d_in, d_out), jnp.float32) * 0.02
            b = jax.random.normal(kb, (d_out,), jnp.float32) * 0.02
            return (w, b)

        def _layernorm(x, g, b):
            mu = jnp.mean(x, axis=-1, keepdims=True)
            var = jnp.mean(jnp.square(x - mu), axis=-1, keepdims=True)
            return (x - mu) * jax.lax.rsqrt(var + EPS) * g + b

        def _mha(v, k, q, mask, wq, bq, wk, bk, wv, bv, wo, bo):
            Bq, Sq, D = q.shape
            depth = D // N_HEADS

            def split(t):
                return t.reshape(t.shape[0], -1, N_HEADS, depth).transpose(0, 2, 1, 3)
            qh = split(q @ wq + bq)
            kh = split(k @ wk + bk)
            vh = split(v @ wv + bv)
            logits = jnp.einsum('bhqd,bhkd->bhqk', qh, kh) / jnp.sqrt(jnp.float32(depth))
            if mask is not None:
                logits = logits + mask * -1000000000.0
            attn = jax.nn.softmax(logits, axis=-1)
            out = jnp.einsum('bhqk,bhkd->bhqd', attn, vh)
            out = out.transpose(0, 2, 1, 3).reshape(Bq, Sq, D)
            return out @ wo + bo
        attn1 = _mha(x, x, x, look_ahead_mask, mha1_wq, mha1_bq, mha1_wk, mha1_bk, mha1_wv, mha1_bv, mha1_wo, mha1_bo)
        out1 = _layernorm(x + attn1, ln1_g, ln1_b)
        attn2 = _mha(enc_output, enc_output, out1, padding_mask, mha2_wq, mha2_bq, mha2_wk, mha2_bk, mha2_wv, mha2_bv, mha2_wo, mha2_bo)
        out2 = _layernorm(out1 + attn2, ln2_g, ln2_b)
        ffn = jax.nn.relu(out2 @ ffn_w1 + ffn_b1) @ ffn_w2 + ffn_b2
        return _layernorm(out2 + ffn, ln3_g, ln3_b)
    x = _L0_xattn_ref(x, ctx_1024, L0_xattn_mask, L0_xattn_wq, L0_xattn_wk, L0_xattn_wv, L0_xattn_gamma, L0_xattn_beta)
    x = _L1_xattn_ref(x, ctx_1024, mask_1x1xSxS2_fk1, mask_Bx1x1xS2_fk0, L1_xattn_mha1_wq, L1_xattn_mha1_bq, L1_xattn_mha1_wk, L1_xattn_mha1_bk, L1_xattn_mha1_wv, L1_xattn_mha1_bv, L1_xattn_mha1_wo, L1_xattn_mha1_bo, L1_xattn_mha2_wq, L1_xattn_mha2_bq, L1_xattn_mha2_wk, L1_xattn_mha2_bk, L1_xattn_mha2_wv, L1_xattn_mha2_bv, L1_xattn_mha2_wo, L1_xattn_mha2_bo, L1_xattn_ffn_w1, L1_xattn_ffn_b1, L1_xattn_ffn_w2, L1_xattn_ffn_b2, L1_xattn_ln1_g, L1_xattn_ln1_b, L1_xattn_ln2_g, L1_xattn_ln2_b, L1_xattn_ln3_g, L1_xattn_ln3_b)
    return x

_drawn_inputs = setup_inputs


def setup_inputs(seed=0):
    import zlib

    import numpy as np

    out = dict(_drawn_inputs(seed))
    spreads = {'L0_xattn_gamma': (1.0, 0.6),
     'L0_xattn_beta': (0.0, 2.0),
     'L1_xattn_ln1_g': (1.0, 0.2),
     'L1_xattn_ln1_b': (0.0, 0.1),
     'L1_xattn_ln2_g': (1.0, 0.2),
     'L1_xattn_ln2_b': (0.0, 0.1),
     'L1_xattn_ln3_g': (1.0, 0.2),
     'L1_xattn_ln3_b': (0.0, 0.1)}
    factors = {'L1_xattn_mha1_wv': 8.0,
     'L1_xattn_mha1_bv': 8.0,
     'L1_xattn_mha1_wo': 8.0,
     'L1_xattn_mha2_wq': 8.0,
     'L1_xattn_mha2_bq': 41.086,
     'L1_xattn_mha2_wk': 8.0,
     'L1_xattn_mha2_bk': 64.0,
     'L1_xattn_mha2_bv': 8.0,
     'L1_xattn_mha2_bo': 3.014,
     'L1_xattn_ffn_b1': 6.338,
     'L1_xattn_ffn_b2': 3.038,
     'L1_xattn_mha1_bo': 2.805}
    for name, (base, spread) in spreads.items():
        noise = np.random.default_rng([zlib.crc32(name.encode()), seed]).standard_normal(out[name].shape)
        drawn = base * np.exp(spread * noise) if base else spread * noise
        out[name] = jnp.asarray(drawn.astype(out[name].dtype))
    for name, factor in factors.items():
        out[name] = (out[name] * factor).astype(out[name].dtype)
    return out
```

```python
from contextlib import ExitStack

import concourse.bass as bass
from concourse import mybir

F32 = mybir.dt.float32
BF16 = mybir.dt.bfloat16
ALU = mybir.AluOpType
ACT = mybir.ActivationFunctionType

P = 128
D = 16
TILES = 4
TOK = TILES * P
CHUNKS = 16
HI, MID, LO = range(3)
SLOTS = [(HI, HI), (HI, MID), (HI, LO), (MID, HI), (MID, MID), (LO, HI)]
STACK = len(SLOTS) * D
STACKED = STACK + 3
MASKED = -1.0e9
LOWEST = -3.0e38
PV_LAG = 2
F_AT = (7, 8, 9, 11, 8, 10)


class Unit:

    def __init__(self, k, par):
        self.k, self.par = k, par
        self.u = 2 * k + par

    def plus(self, n):
        at = self.par + n
        return Unit(self.k + at // 2, at % 2)

    def number(self):
        return self.u if isinstance(self.u, int) else None


def wait_sp(sp, sem, value, passed):
    if isinstance(value, int):
        wait(sp, sem, value)
    else:
        wait_apart(sp, sem, value, passed)


def wait(eng, sem, value):
    if isinstance(value, int) and value <= 0:
        return
    eng.wait_ge(sem, value)


def wait_apart(eng, sem, value, passed):
    eng.wait_ge(sem, value).then_inc(passed, 1)


def iterations(eng, n, before, after, body):
    assert n % 2 == 0
    first = 1
    last = max(n // 2 - (before + 1) // 2, first)
    for t in range(-before, 2 * first):
        body(Unit(t // 2, t % 2))
    if last > first:
        with eng.Fori(first, last) as k:
            body(Unit(k, 0))
            body(Unit(k, 1))
    for t in range(2 * last, n + after):
        body(Unit(t // 2, t % 2))


def exists(unit, n):
    at = unit.number()
    return at is None or 0 <= at < n


def reset(nc, sems):
    with nc.Block() as block:
        @block.gpsimd
        def _(pool):
            for s in sems:
                pool.sem_clear(s)


def constants(nc, top, l0, io, c):
    def sb(name, shape, dt=F32):
        c[name] = top.enter_context(nc.sbuf_tensor(name, shape, dt))
        return c[name]

    def sb_l0(name, shape, dt=F32):
        c[name] = l0.enter_context(nc.sbuf_tensor(name, shape, dt))
        return c[name]

    L = io["x"].shape[2]
    LT = L // P
    NB = io["x"].shape[0]
    F = io["ffn_w1"].shape[1]

    ident = sb("ident", [P, P])
    identb = sb("identb", [P, P], BF16)
    mask1 = sb("mask1", [P, P])
    mask1t = sb("mask1t", [P, P])
    pad_bias = sb("pad_bias", [P, NB])
    rows = {n: sb(n, [P, L]) for n in ("ln1_g", "ln1_b", "ln2_g", "ln2_b", "ln3_g", "ln3_b",
                                       "mha1_bo", "mha2_bo", "ffn_b2")}
    bq = {m: sb(f"{m}_bq_s", [P, 2]) for m in ("mha1", "mha2")}
    bk = {m: sb(f"{m}_bk_s", [P, 2]) for m in ("mha1", "mha2")}
    bv = {m: sb(f"{m}_bv_s", [P, 2]) for m in ("mha1", "mha2")}
    c["bq"], c["bk"], c["bv"] = bq, bk, bv
    b1 = sb("ffn_b1_s", [P, F // P])
    cols = {n: sb(n, [P, 2]) for n in ("ln1_gc", "ln1_bc", "ln2_gc", "ln2_bc")}
    minus_half = sb("minus_half", [P, 1])
    conv = {n: sb_l0(f"conv_{n}", [P, 3, P]) for n in "qkv"}
    c["conv"] = conv
    mask0 = sb_l0("mask0", [P, LT, L])
    mask0t = sb_l0("mask0t", [P, LT, L])
    g0, b0 = sb_l0("g0", [P, P]), sb_l0("b0", [P, P])
    cols.update({n: sb_l0(n, [P, 1]) for n in ("g0_col", "b0_col")})

    with ExitStack() as ctx:
        dense = {n: ctx.enter_context(nc.sbuf_tensor(f"dense_{n}", [P, 3, P], F32)) for n in "qk"}
        pad = ctx.enter_context(nc.sbuf_tensor("pad_rows", [P, P], F32))
        wo = {m: ctx.enter_context(nc.sbuf_tensor(f"setup_wo_{m}", [P, 2, L], F32)) for m in ("mha1", "mha2")}
        bvw = ctx.enter_context(nc.sbuf_tensor("bv_wide", [P, 4, P], F32))
        ps = [ctx.enter_context(nc.psum_tensor(f"setup_ps{i}", [P, 512], F32)) for i in range(8)]
        zeroed = top.enter_context(nc.semaphore("zeroed"))
        ident_zero = top.enter_context(nc.semaphore("ident_zero"))
        ident_ready = top.enter_context(nc.semaphore("ident_ready"))
        loaded = top.enter_context(nc.semaphore("consts_loaded"))
        scaled = top.enter_context(nc.semaphore("masks_scaled"))
        turned = top.enter_context(nc.semaphore("masks_turned"))
        widened = top.enter_context(nc.semaphore("bv_widened"))
        bvwo = top.enter_context(nc.semaphore("bv_times_wo"))
        done = top.enter_context(nc.semaphore("consts_done"))
        block = ctx.enter_context(nc.Block())

        blocks = {"q": dense["q"], "k": dense["k"], "v": conv["v"]}
        loads = []
        for n in "qkv":
            for g in range(P // D):
                loads.append((blocks[n][g * D:(g + 1) * D, :, g * D:(g + 1) * D], io[f"conv_{n}"][g]))
        loads += [(mask0[:, t, :], io["mask0"][t * P:(t + 1) * P, :]) for t in range(LT)]
        loads += [(mask1[:, :], io["mask1"][0, 0]), (pad[0:NB, :], io["mask2"][:, 0, 0, :])]
        loads += [(g0[:, :], io["gamma"].partition_broadcast(P)), (b0[:, :], io["beta"].partition_broadcast(P))]
        loads += [(t[:, :], io[n].partition_broadcast(P)) for n, t in rows.items()]
        loads += [(t[:, :], io[f"{m}_{n}"]) for n, ts in (("bq", bq), ("bk", bk), ("bv", bv)) for m, t in ts.items()]
        loads += [(b1[:, :], io["ffn_b1"])] + [(t[:, :], io[n]) for n, t in cols.items()]
        loads += [(wo[m][:, :, :], io[f"{m}_wo"].rearrange("(k p) n -> p k n", p=P)) for m in wo]

        @block.gpsimd
        def _(pool):
            for t in (dense["q"], dense["k"], conv["v"], pad):
                nc.gpsimd.memset(t[:], 0.0).then_inc(zeroed, 1)
            nc.gpsimd.memset(minus_half[:, :], -0.5)
            nc.gpsimd.memset(ident[:, :], 0.0).then_inc(ident_zero, 1)
            nc.gpsimd.memset(identb[:, :], 0.0).then_inc(ident_zero, 1)
            pool.wait_ge(ident_zero, 2)
            for t in (ident, identb):
                nc.gpsimd.affine_select(out=t[:, :], in_=t[:, :], compare_op=ALU.not_equal, fill=1.0, base=0,
                                        pattern=[[-1, P]], channel_multiplier=1).then_inc(ident_ready, 1)

        @block.sync
        def _(sp):
            sp.wait_ge(zeroed, 4)
            for out, in_ in loads:
                sp.dma_start(out, in_).then_inc(loaded, 16)

        @block.vector
        def _(dve):
            dve.wait_ge(loaded, 16 * len(loads))
            for t in (mask0, mask1, pad):
                nc.vector.tensor_scalar(t[:], t[:], MASKED, None, ALU.mult).then_inc(scaled, 1)
            for n in "qk":
                nc.vector.tensor_copy(conv[n][:, :, :].rearrange("p t (d g) -> p t d g", d=D),
                                      dense[n][:, :, :].rearrange("p t (g d) -> p t d g", d=D))
            for m in bq:
                nc.vector.tensor_scalar(bq[m][:, :], bq[m][:, :], float(D) ** -0.5, None, ALU.mult)
            nc.vector.memset(bvw[:], 1.0).then_inc(widened, 1)
            dve.wait_ge(widened, 1)
            for i, m in enumerate(("mha1", "mha2")):
                for kt in range(2):
                    nc.vector.tensor_scalar(bvw[:, 2 * i + kt, :], bvw[:, 2 * i + kt, :], bv[m][:, kt:kt + 1],
                                            None, ALU.mult).then_inc(widened, 1)
            dve.wait_ge(bvwo, 2)
            for i, m in enumerate(("mha1", "mha2")):
                nc.vector.tensor_tensor(rows[f"{m}_bo"][:, :], rows[f"{m}_bo"][:, :], ps[i][:, 0:L], ALU.add)
            dve.wait_ge(turned, 3)
            for a in range(LT):
                nc.vector.tensor_copy(mask0t[:, a, :], ps[2 + a][:, 0:L])
            nc.vector.tensor_copy(mask1t[:, :], ps[4][:, 0:P])
            nc.vector.tensor_copy(pad_bias[:, 0:NB], ps[5][:, 0:NB]).then_inc(done, 1)

        @block.tensor
        def _(pe):
            pe.wait_ge(widened, 5)
            for i, m in enumerate(("mha1", "mha2")):
                for kt in range(2):
                    mm = nc.tensor.matmul(ps[i][:, 0:L], bvw[:, 2 * i + kt, :], wo[m][:, kt, :],
                                          start=(kt == 0), stop=(kt == 1))
                mm.then_inc(bvwo, 1)
            pe.wait_ge(ident_ready, 2)
            pe.wait_ge(scaled, 3)
            for a in range(LT):
                for b in range(LT):
                    mm = nc.tensor.transpose(ps[2 + a][:, b * P:(b + 1) * P], mask0[:, b, a * P:(a + 1) * P], ident[:, :])
            mm.then_inc(turned, 1)
            nc.tensor.transpose(ps[4][:, 0:P], mask1[:, :], ident[:, :]).then_inc(turned, 1)
            nc.tensor.transpose(ps[5][:, 0:P], pad[:, :], ident[:, :]).then_inc(turned, 1)

        @block.scalar
        def _(act):
            act.wait_ge(done, 1)


def attention(nc, top, c, io, phase):
    conv = phase == 0
    name = ("l0", "mha1", "mha2")[phase]
    H = 8 if conv else 16
    QUADS = H // 4
    KT = 2 if conv else 1
    BU = TILES // KT
    N = io["x"].shape[0] // BU
    GROUPS = H // 8
    HALVES = 2 * GROUPS
    VSTEPS = 1 if conv else 2
    W = P if conv else 2 * P
    SCALE = 8.0 ** -0.5 if conv else float(D) ** -0.5
    EPS = 1e-5 if conv else 1e-6
    L = io["x"].shape[2]
    KEYS = KT * P
    SH = 512 // KEYS
    TT = P // 1

    with ExitStack() as ctx:
        def sb(n, shape, dt=F32):
            return ctx.enter_context(nc.sbuf_tensor(f"{name}_{n}", shape, dt))

        sems = []

        def sem(n):
            sems.append(ctx.enter_context(nc.semaphore(f"{name}_{n}")))
            return sems[-1]

        if conv:
            x_pad = sb("x_pad", [P, 2, BU, L + 2])
            c_pad = sb("c_pad", [P, 2, BU, L + 2])
        else:
            xin = sb("xin", [P, 2, 2, TOK])
        if phase == 2:
            craw = sb("craw", [P, 2, TILES, L])
            cin = sb("cin", [P, 2, 2, TOK])
            pmask = sb("pmask", [P, 2, TILES, P])
        if not conv:
            wq, wk, wv, wo = (sb(n, [P, 2, L]) for n in ("wq", "wk", "wv", "wo"))
        resid = sb("resid", [P, 2, TILES * W])
        yproj = sb("yproj", [P, 2, TOK])
        parts = sb("parts", [P, 2, HALVES, 3, TOK], BF16)
        stack = sb("stack", [P, 2, 2, H, TOK], BF16)
        vals = sb("vals", [P, 2, TILES, H, 32])
        junk = sb("junk", [P, 2, 512], BF16)
        maxes = sb("maxes", [P, TILES, H])
        max_rest = sb("max_rest", [P, TILES, H])
        max_parts = sb("max_parts", [P, TILES, 3, H], BF16)
        max_rows = sb("max_rows", [3 * H, TOK], BF16)
        probs = sb("probs", [P, 4, 512])
        heads_out = sb("heads_out", [P, 2, QUADS * P])
        recips = sb("recips", [P, H])
        merged = sb("merged", [P, H * D])
        merged_t = sb("merged_t", [P, 2, P])
        z = sb("z", [P, 2, W])
        stats = sb("stats", [P, 2, 6])
        moments = sb("moments", [P, 2, 2])
        rstd = sb("rstd", [P, 2, 1])
        y = sb("y", [P, 2, TILES, W])
        y_t = sb("y_t", [P, 2, TILES * W])

        bank = [ctx.enter_context(nc.psum_tensor(f"{name}_bank{i}", [P, 512], F32)) for i in range(8)]
        work, sbank, tbank, pvbank, fbank = bank[0:2], bank[2:4], bank[4:6], bank[6], bank[7]

        const_ready, ones_ready = sem("const_ready"), sem("ones_ready")
        passed = {e: sem(f"passed_{e}") for e in ("pe", "act", "dve", "pool", "sp")}
        weights = sem("weights")
        xin_ld = [sem(f"xin_ld{i}") for i in range(2)]
        resid_ld = [sem(f"resid_ld{i}") for i in range(2)]
        pmask_ld = [sem(f"pmask_ld{i}") for i in range(2)]
        padded = sem("padded")
        pmask_ready = sem("pmask_ready")
        resid_ready = sem("resid_ready")
        ctx_mm, ctx_out = sem("ctx_mm"), sem("ctx_out")
        proj_mm, proj_out = sem("proj_mm"), sem("proj_out")
        mid_done = sem("mid_done")
        rest_step, split_done = sem("rest_step"), sem("split_done")
        val_mm, val_out = sem("val_mm"), sem("val_out")
        stack_in = [[sem(f"stack_in{p}{g}") for g in range(GROUPS)] for p in range(2)]
        score_mm, score_max = sem("score_mm"), sem("score_max")
        max_step, max_split = sem("max_step"), sem("max_split")
        max_mm, max_out = sem("max_mm"), sem("max_out")
        max_in = [sem(f"max_in{i}") for i in range(2)]
        att_mm, att_masked, att_exp, att_pv = sem("att_mm"), sem("att_masked"), sem("att_exp"), sem("att_pv")
        heads_done = sem("heads_done")
        turn_mm, recip_done, merged_done = sem("turn_mm"), sem("recip_done"), sem("merged_done")
        mt_mm, mt_out = sem("mt_mm"), sem("mt_out")
        out_mm = sem("out_mm")
        z_done, stats_done, moments_done, var_done, rstd_done = (
            sem("z_done"), sem("stats_done"), sem("moments_done"), sem("var_done"), sem("rstd_done"))
        normed, scaled, y_done = sem("normed"), sem("scaled"), sem("y_done")
        yt_mm, yt_out = sem("yt_mm"), sem("yt_out")
        stored = [sem(f"stored{i}") for i in range(2)]

        if conv:
            x_units = io["x"].rearrange("(u b) c l -> u c b l", b=BU)
            c_units = io["ctx"].rearrange("(u b) c l -> u c b l", b=BU)
            out_rows = io["x1"].rearrange("(u b) s d -> u s b d", b=BU)
            out_cols = io["x1t"].rearrange("(u b) k p s -> u p (b k) s", b=BU)
            res_units = x_units
            bo = None
            ln_g, ln_b, ln_gc, ln_bc = c["g0"], c["b0"], c["g0_col"], c["b0_col"]
        else:
            src_t, src, dst, dst_t = (("x1t", "x1", "o1", "o1t"), ("o1t", "o1", "o2", "o2t"))[phase - 1]
            xt_units = io[src_t].rearrange("(u b) k p s -> u p k b s", b=BU)
            res_units = io[src].rearrange("(u b) s d -> u s b d", b=BU)
            c_units = io["ctx"].rearrange("(u b) s d -> u s b d", b=BU)
            out_rows = io[dst].rearrange("(u b) s d -> u s b d", b=BU)
            out_cols = io[dst_t].rearrange("(u b) k p s -> u p k b s", b=BU)
            bo = c[f"{name}_bo"]
            ln_g, ln_b, ln_gc, ln_bc = (c[f"ln{phase}_{n}"] for n in ("g", "b", "gc", "bc"))
        mask2_units = io["mask2"].rearrange("(u b) i j m -> u (b i j m)", b=TILES) if phase == 2 else None
        XIN_LOADS = 2 if conv else (2 if phase == 1 else 3)
        HALF_SIDE = [(g, side) for g in range(GROUPS) for side in range(2)]

        def att_chunks():
            return [(j, q, kt) for j in range(TILES) for q in range(QUADS) for kt in range(KT)]

        def score_chunks():
            return [(j, h) for g in range(GROUPS) for j in range(TILES) for h in range(8 * g, 8 * g + 8, SH)]

        ATT, SCO = att_chunks(), score_chunks()
        assert len(ATT) == len(SCO) == CHUNKS
        SCORE_SLOT = [5 + i // 2 for i in range(CHUNKS)]
        MAX_SLOT = 14
        NORM_STEP = 4 if conv else 5
        V_SLOT = range(VSTEPS)
        C_SLOT = [2, 3]
        P_SLOT = [4, 5, 7, 9] if not conv else [2, 4]

        def finish_at(slot, step):
            for off in (0, -1):
                for j in range(TILES):
                    if 4 * j + F_AT[step] == slot - 16 * off:
                        return off, j
            return None

        def all_finish(n, t, slot, step):
            at = finish_at(slot, step)
            if at and exists(t.plus(at[0]), n):
                return t.plus(at[0]), at[1]
            return None

        def projected(u, i):
            return HALVES * u.u + i + 1

        running = ExitStack()
        block = running.enter_context(nc.Block())

        @block.sync
        def _(sp):
            if not conv:
                for t, n in ((wq, "wq"), (wk, "wk"), (wv, "wv"), (wo, "wo")):
                    sp.dma_start(t[:, :, :], io[f"{name}_{n}"].rearrange("(k p) n -> p k n", p=P)).then_inc(weights, 16)

            def load(u):
                wait_sp(sp, proj_mm, projected(u.plus(-2), HALVES - 1), passed["sp"])
                wait_sp(sp, val_mm, VSTEPS * (u.u - 1), passed["sp"])
                if conv:
                    sp.dma_start(x_pad[:, u.par, :, 1:L + 1], x_units[u.u]).then_inc(xin_ld[u.par], 16)
                    sp.dma_start(c_pad[:, u.par, :, 1:L + 1], c_units[u.u]).then_inc(xin_ld[u.par], 16)
                else:
                    for kt in range(2):
                        sp.dma_start(xin[:, u.par, kt, :].rearrange("p (b s) -> p b s", b=BU),
                                     xt_units[u.u][:, kt]).then_inc(xin_ld[u.par], 16)
                    if phase == 2:
                        sp.dma_start(craw[:, u.par, :, :], c_units[u.u]).then_inc(xin_ld[u.par], 16)

            def load_pmask(u):
                wait_sp(sp, score_max, CHUNKS * (u.u - 1), passed["sp"])
                sp.dma_start(pmask[:, u.par, :, :].rearrange("p b m -> p (b m)"),
                             mask2_units[u.u].partition_broadcast(P)).then_inc(pmask_ld[u.par], 16)

            def load_resid(u):
                if conv:
                    wait_sp(sp, turn_mm, TILES * (u.u - 1), passed["sp"])
                else:
                    wait_sp(sp, z_done, TILES * (u.u - 1), passed["sp"])
                sp.dma_start(resid[:, u.par, :].rearrange("p (b d) -> p b d", b=BU),
                             res_units[u.u]).then_inc(resid_ld[u.par], 16)

            def fill_stack(u):
                wait_sp(sp, att_mm, CHUNKS * (u.u - 1), passed["sp"])
                for i, (g, side) in enumerate(HALF_SIDE):
                    wait_sp(sp, split_done, projected(u, i), passed["sp"])
                    for s, pair in enumerate(SLOTS):
                        sp.dma_start(stack[s * D:(s + 1) * D, u.par, side, 8 * g:8 * g + 8, :],
                                     parts[:, u.par, i, pair[side], :]).then_inc(stack_in[u.par][g], 16)

            def store(u):
                wait_sp(sp, y_done, TILES * (u.u + 1), passed["sp"])
                if conv:
                    sp.dma_start(out_cols[u.u], y[:, u.par, :, :]).then_inc(stored[u.par], 16)
                else:
                    sp.dma_start(out_rows[u.u], y[:, u.par, :, :]).then_inc(stored[u.par], 16)
                wait_sp(sp, yt_out, TILES * (u.u + 1), passed["sp"])
                if conv:
                    sp.dma_start(out_rows[u.u], y_t[:, u.par, :].rearrange("p (b d) -> p b d", b=BU)
                                 ).then_inc(stored[u.par], 16)
                else:
                    for kt in range(2):
                        sp.dma_start(out_cols[u.u][:, kt],
                                     y_t[:, u.par, kt * TOK:(kt + 1) * TOK].rearrange("p (b s) -> p b s", b=BU)
                                     ).then_inc(stored[u.par], 16)

            def body(t):
                if exists(t.plus(1), N) :
                    fill_stack(t.plus(1))
                if exists(t, N):
                    load_resid(t)
                if phase == 2 and exists(t.plus(2), N):
                    load_pmask(t.plus(2))
                if exists(t.plus(3), N):
                    load(t.plus(3))
                if exists(t.plus(-1), N):
                    store(t.plus(-1))

            iterations(sp, N, 3, 1, body)
            STORES = 2 if conv else 3
            for p in range(2):
                sp.wait_ge(stored[p], 16 * STORES * (N // 2))

        @block.tensor
        def _(pe):
            if not conv:
                pe.wait_ge(weights, 16 * 4)
            pe.wait_ge(const_ready, 1)

            def context_step(u, i):
                if i == 0:
                    pe.wait_ge(xin_ld[u.par], 16 * XIN_LOADS * (u.k + 1))
                wait(pe, val_out, VSTEPS * (u.u - 1) + i + 1 if not isinstance(u.u, int) or u.u >= 1 else 0)
                for j in range(TILES):
                    mm = nc.tensor.transpose(work[i][:, j * P:(j + 1) * P], craw[:, u.par, j, i * P:(i + 1) * P],
                                             c["ident"][:, :])
                mm.then_inc(ctx_mm, 1)

            def project_step(u, i):
                g, side = HALF_SIDE[i]
                if i == 0:
                    if conv:
                        pe.wait_ge(padded, u.u + 1)
                    elif phase == 1:
                        pe.wait_ge(xin_ld[u.par], 16 * XIN_LOADS * (u.k + 1))
                if i >= 2:
                    pe.wait_ge(proj_out, projected(u, i - 2))
                elif phase == 2:
                    pe.wait_ge(ctx_out, 2 * u.u + i + 1)
                    if i == 0:
                        pe.wait_ge(ctx_out, 2 * u.u + 2)
                elif phase == 1:
                    wait(pe, val_out, VSTEPS * (u.u - 1) + i + 1 if u.number() != 0 else 0)
                elif i == 0:
                    wait(pe, val_out, u.u)
                else:
                    wait(pe, max_out, u.u - 1)
                if conv:
                    src = (x_pad, c_pad)[side]
                    for tap in range(3):
                        mm = nc.tensor.matmul(work[i % 2][:, :].rearrange("p (b l) -> p b l", b=BU),
                                              c["conv"]["qk"[side]][:, tap, :], src[:, u.par, :, tap:tap + L],
                                              start=(tap == 0), stop=(tap == 2))
                else:
                    w = (wq, wk)[side]
                    src = cin if phase == 2 and side == 1 else xin
                    for kt in range(2):
                        mm = nc.tensor.matmul(work[i % 2][:, :], w[:, kt, g * P:(g + 1) * P], src[:, u.par, kt, :],
                                              start=(kt == 0), stop=(kt == 1))
                mm.then_inc(proj_mm, 1)

            def value_step(u, i):
                if conv:
                    pe.wait_ge(proj_out, projected(u, 0))
                    for j in range(TILES):
                        for tap in range(3):
                            at = (j % 2) * P + tap
                            mm = nc.tensor.matmul(work[0][:, j * P:(j + 1) * P], c_pad[:, u.par, j // 2, at:at + P],
                                                  c["conv"]["v"][:, tap, :], start=(tap == 0), stop=(tap == 2))
                else:
                    pe.wait_ge(proj_out, projected(u, 2 + i))
                    if i == 1:
                        wait(pe, max_out, u.u)
                    src = cin if phase == 2 else xin
                    for j in range(2):
                        tile = 2 * i + j
                        for kt in range(2):
                            mm = nc.tensor.matmul(work[i][:, j * L:(j + 1) * L], src[:, u.par, kt, tile * P:(tile + 1) * P],
                                                  wv[:, kt, :], start=(kt == 0), stop=(kt == 1))
                mm.then_inc(val_mm, 1)

            def score_step(u, i):
                j, h0 = SCO[i]
                if j == 0 and h0 % 8 == 0:
                    g = h0 // 8
                    pe.wait_ge(stack_in[u.par][g], 16 * 2 * len(SLOTS) * (u.k + 1))
                wait(pe, score_max, CHUNKS * u.u + i - 1)
                first = (j // KT) * KT * P
                for s in range(SH):
                    mm = nc.tensor.matmul(sbank[i % 2][:, s * KEYS:(s + 1) * KEYS],
                                          stack[0:STACK, u.par, 0, h0 + s, j * P:(j + 1) * P],
                                          stack[0:STACK, u.par, 1, h0 + s, first:first + KEYS], start=True, stop=True)
                mm.then_inc(score_mm, 1)

            def max_turn(u):
                if exists(u.plus(1), N):
                    pe.wait_ge(proj_out, projected(u.plus(1), HALVES - 1))
                elif not conv:
                    pe.wait_ge(val_out, VSTEPS * (u.u + 1))
                else:
                    wait(pe, max_out, u.u)
                wait_apart(pe, max_split, u.u + 1, passed["pe"])
                for j in range(TILES):
                    mm = nc.tensor.transpose(work[1][0:3 * H, j * 64:(j + 1) * 64].bitcast(BF16),
                                             max_parts[:, j, :, :].rearrange("p a h -> p (a h)"), c["identb"][:, :])
                mm.then_inc(max_mm, 1)

            def attend_step(u, i):
                j, q, kt = ATT[i]
                if i == 0:
                    pe.wait_ge(max_in[u.par], 16 * (u.k + 1))
                    if u.number() == 0:
                        pe.wait_ge(ones_ready, 2)
                wait(pe, att_exp, CHUNKS * u.u + i - 1)
                key = ((j // KT) * KT + kt) * P
                for s in range(4):
                    h = 4 * q + s
                    mm = nc.tensor.matmul(tbank[i % 2][:, s * P:(s + 1) * P], stack[0:STACKED, u.par, 1, h, key:key + P],
                                          stack[0:STACKED, u.par, 0, h, j * P:(j + 1) * P], start=True, stop=True)
                mm.then_inc(att_mm, 1)

            def pv_step(u, i):
                j, q, kt = ATT[i]
                if i == 0:
                    pe.wait_ge(val_out, VSTEPS * (u.u + 1))
                if i % 4 == 0:
                    wait(pe, heads_done, TILES * u.u + j)
                pe.wait_ge(att_exp, CHUNKS * u.u + i + 1)
                for s in range(4):
                    mm = nc.tensor.matmul(pvbank[32 * s:32 * s + 32, q * P:(q + 1) * P],
                                          vals[:, u.par, (j // KT) * KT + kt, 4 * q + s, :],
                                          probs[:, i % 4, s * P:(s + 1) * P], start=(kt == 0), stop=(kt == KT - 1),
                                          tile_position=(0, 32 * s))
                mm.then_inc(att_pv, 1)

            def turn_heads(u, j):
                n = TILES * u.u + j
                pe.wait_ge(heads_done, n + 1)
                wait(pe, yt_out, n)
                if conv and j == 0:
                    pe.wait_ge(resid_ld[u.par], 16 * (u.k + 1))
                for q in range(QUADS):
                    mm = nc.tensor.transpose(fbank[:, q * P:(q + 1) * P], heads_out[:, j % 2, q * P:(q + 1) * P],
                                             c["ident"][:, :])
                if conv:
                    mm = nc.tensor.transpose(fbank[:, 2 * P:3 * P], resid[:, u.par, j * P:(j + 1) * P], c["ident"][:, :])
                mm.then_inc(turn_mm, 1)

            def turn_merged(u, j):
                pe.wait_ge(merged_done, TILES * u.u + j + 1)
                for a in range(2):
                    mm = nc.tensor.transpose(fbank[:, a * P:(a + 1) * P], merged[:, a * P:(a + 1) * P], c["ident"][:, :])
                mm.then_inc(mt_mm, 1)

            def output_step(u, j):
                pe.wait_ge(mt_out, TILES * u.u + j + 1)
                for a in range(2):
                    mm = nc.tensor.matmul(fbank[:, 0:L], merged_t[:, a, :], wo[:, a, :], start=(a == 0), stop=(a == 1))
                mm.then_inc(out_mm, 1)

            def turn_y(u, j):
                pe.wait_ge(normed, TILES * u.u + j + 1)
                for a in range(W // P):
                    mm = nc.tensor.transpose(fbank[:, a * P:(a + 1) * P], z[:, j % 2, a * P:(a + 1) * P],
                                             c["ident"][:, :])
                mm.then_inc(yt_mm, 1)

            def body(t):
                for slot in range(16):
                    if slot in V_SLOT and exists(t.plus(1), N):
                        value_step(t.plus(1), V_SLOT.index(slot))
                    if phase == 2 and slot in C_SLOT and exists(t.plus(2), N):
                        context_step(t.plus(2), C_SLOT.index(slot))
                    if slot in P_SLOT and exists(t.plus(2), N):
                        project_step(t.plus(2), P_SLOT.index(slot))
                    if exists(t.plus(1), N):
                        for i in range(CHUNKS):
                            if SCORE_SLOT[i] == slot:
                                score_step(t.plus(1), i)
                        if slot == MAX_SLOT:
                            max_turn(t.plus(1))
                    if exists(t, N):
                        attend_step(t, slot)
                        if slot >= PV_LAG:
                            pv_step(t, slot - PV_LAG)
                    if at := all_finish(N, t, slot, 3):
                        turn_y(*at)
                    if not conv:
                        if at := all_finish(N, t, slot, 2):
                            output_step(*at)
                        if at := all_finish(N, t, slot, 1):
                            turn_merged(*at)
                    if at := all_finish(N, t, slot, 0):
                        turn_heads(*at)
                if exists(t, N):
                    for i in range(CHUNKS - PV_LAG, CHUNKS):
                        pv_step(t, i)

            iterations(pe, N, 2, 1, body)

        @block.scalar
        def _(act):
            def context_out(u, i):
                act.wait_ge(ctx_mm, 2 * u.u + i + 1)
                nc.scalar.activation(cin[:, u.par, i, :], work[i][:, :], ACT.Copy).then_inc(ctx_out, 1)

            def project_out(u, i):
                g, side = HALF_SIDE[i]
                act.wait_ge(proj_mm, projected(u, i))
                wait(act, split_done, projected(u, i) - 2)
                if i == 0:
                    for gg in range(GROUPS):
                        wait(act, stack_in[u.par][gg], 16 * 2 * len(SLOTS) * u.k)
                args = {"scale": SCALE if side == 0 else 1.0}
                if not conv:
                    args["bias"] = ((c["bq"], c["bk"])[side])[name][:, g:g + 1]
                for out in (yproj[:, i % 2, :], parts[:, u.par, i, HI, :]):
                    last = nc.scalar.activation(out, work[i % 2][:, :], ACT.Identity, **args)
                last.then_inc(proj_out, 1)

            def value_out(u, i):
                act.wait_ge(val_mm, VSTEPS * u.u + i + 1)
                if i == 0:
                    wait(act, att_pv, CHUNKS * (u.u - 1))
                n = TILES // VSTEPS
                nc.scalar.activation(vals[:, u.par, i * n:(i + 1) * n, :, 0:D],
                                     work[i][:, :].rearrange("p (j h d) -> p j h d", j=n, d=D), ACT.Copy
                                     ).then_inc(val_out, 1)

            def max_rows_out(u):
                act.wait_ge(max_mm, u.u + 1)
                if u.number() != 0:
                    p = u.plus(-1)
                    act.wait_ge(max_in[p.par], 16 * (p.k + 1))
                nc.scalar.activation(max_rows[:, :], work[1][0:3 * H, 0:256].bitcast(BF16), ACT.Copy).then_inc(max_out, 1)
                act.wait_ge(max_out, u.u + 1)
                act.dma_start(stack[STACK:STACKED, u.par, 0, :, :], max_rows[:, :]).then_inc(max_in[u.par], 16)

            def exp_step(u, i):
                wait(act, att_pv, CHUNKS * u.u + i - 3)
                if phase == 2:
                    wait_apart(act, att_mm, CHUNKS * u.u + i + 1, passed["act"])
                else:
                    act.wait_ge(att_masked, CHUNKS * u.u + i + 1)
                if phase == 2:
                    b = TILES * u.u + ATT[i][0]
                    ins = nc.scalar.activation(probs[:, i % 4, :], tbank[i % 2][:, :], ACT.Exp,
                                               bias=c["pad_bias"][:, bass.ds(b, 1)])
                else:
                    ins = nc.scalar.activation(probs[:, i % 4, :], tbank[i % 2][:, :], ACT.Exp)
                ins.then_inc(att_exp, 1)

            def heads_copy(u, j):
                act.wait_ge(att_pv, CHUNKS * u.u + 4 * j + 4)
                wait(act, turn_mm, TILES * u.u + j - 1)
                nc.scalar.activation(heads_out[:, j % 2, :], pvbank[:, 0:QUADS * P], ACT.Copy).then_inc(heads_done, 1)

            def merged_out(u, j):
                act.wait_ge(mt_mm, TILES * u.u + j + 1)
                nc.scalar.activation(merged_t[:, :, :], fbank[:, 0:2 * P].rearrange("p (a s) -> p a s", a=2), ACT.Copy
                                     ).then_inc(mt_out, 1)

            def y_out(u, j):
                act.wait_ge(yt_mm, TILES * u.u + j + 1)
                if j == 0:
                    wait(act, stored[u.par], 16 * (2 if conv else 3) * u.k)
                for a in range(W // P):
                    last = nc.scalar.activation(y_t[:, u.par, a * TOK + j * P:a * TOK + (j + 1) * P],
                                                fbank[:, a * P:(a + 1) * P], ACT.Identity,
                                                scale=ln_gc[:, a:a + 1], bias=ln_bc[:, a:a + 1])
                last.then_inc(yt_out, 1)

            def body(t):
                for slot in range(16):
                    if slot in V_SLOT and exists(t.plus(1), N):
                        value_out(t.plus(1), V_SLOT.index(slot))
                    if phase == 2 and slot in C_SLOT and exists(t.plus(2), N):
                        context_out(t.plus(2), C_SLOT.index(slot))
                    if slot in P_SLOT and exists(t.plus(2), N):
                        project_out(t.plus(2), P_SLOT.index(slot))
                    if slot == MAX_SLOT and exists(t.plus(1), N):
                        max_rows_out(t.plus(1))
                    if exists(t, N):
                        exp_step(t, slot)
                        if slot >= PV_LAG + 3 and (slot - PV_LAG - 3) % 4 == 0:
                            heads_copy(t, (slot - PV_LAG - 3) // 4)
                    if at := all_finish(N, t, slot, 3):
                        y_out(*at)
                    if not conv:
                        if at := all_finish(N, t, slot, 1):
                            merged_out(*at)
                if exists(t, N):
                    heads_copy(t, TILES - 1)

            iterations(act, N, 2, 1, body)

        @block.vector
        def _(dve):
            nc.vector.memset(vals[:, :, :, :, D:32], 0.0).then_inc(max_step, 1)
            dve.wait_ge(max_step, 1)
            nc.vector.memset(vals[:, :, :, :, D:D + 1], 1.0).then_inc(const_ready, 1)

            def mid_part(u, i):
                n = HALVES * u.u + i
                dve.wait_ge(rest_step, n + 1)
                nc.vector.tensor_copy(parts[:, u.par, i, MID, :], yproj[:, i % 2, :]).then_inc(mid_done, 1)

            def max_of(u, i):
                j, h0 = SCO[i]
                if phase == 2 and i == 0:
                    dve.wait_ge(pmask_ready, u.u + 1)
                wait(dve, score_max, CHUNKS * u.u + i - 1)
                wait_apart(dve, score_mm, CHUNKS * u.u + i + 1, passed["dve"])
                mask = c["mask0"][:, j % 2, :] if conv else (c["mask1"][:, :] if phase == 1 else pmask[:, u.par, j, :])
                for s in range(SH):
                    cols = slice(s * KEYS, (s + 1) * KEYS)
                    ins = nc.vector.tensor_tensor_reduce(
                        out=junk[:, i % 2, cols], in0=sbank[i % 2][:, cols], in1=mask, scale=1.0, scalar=LOWEST,
                        op0=ALU.add, op1=ALU.max, accum_out=maxes[:, j, h0 + s:h0 + s + 1])
                ins.then_inc(score_max, 1)

            def split_max(u):
                dve.wait_ge(score_max, CHUNKS * (u.u + 1))
                wait(dve, max_mm, u.u)
                nc.vector.tensor_scalar(max_parts[:, :, HI, :], maxes[:, :, :], -1.0, None, ALU.mult).then_inc(max_step, 1)
                dve.wait_ge(max_step, 3 * u.u + 2)
                nc.vector.scalar_tensor_tensor(out=max_rest[:, :, :], in0=maxes[:, :, :], scalar=-1.0,
                                               in1=max_parts[:, :, HI, :], op0=ALU.mult, op1=ALU.subtract
                                               ).then_inc(max_step, 1)
                dve.wait_ge(max_step, 3 * u.u + 3)
                nc.vector.tensor_copy(max_parts[:, :, MID, :], max_rest[:, :, :]).then_inc(max_step, 1)
                dve.wait_ge(max_step, 3 * u.u + 4)
                nc.vector.tensor_tensor(max_parts[:, :, LO, :], max_rest[:, :, :], max_parts[:, :, MID, :], ALU.subtract
                                        ).then_inc(max_split, 1)

            def mask_scores(u, i):
                j, q, kt = ATT[i]
                dve.wait_ge(att_mm, CHUNKS * u.u + i + 1)
                if conv:
                    l0 = (j % 2) * P
                    mask = c["mask0t"][:, kt, l0:l0 + P]
                else:
                    mask = c["mask1t"][:, :]
                bank_ = tbank[i % 2][:, :].rearrange("p (s l) -> p s l", s=4)
                nc.vector.tensor_tensor(bank_, bank_, mask.unsqueeze(1).to_broadcast([P, 4, P]), ALU.add
                                        ).then_inc(att_masked, 1)

            def merge(u, j):
                n = TILES * u.u + j
                heads = fbank[:, 0:QUADS * P].rearrange("p (h e) -> p h e", e=32)
                dve.wait_ge(turn_mm, n + 1)
                nc.vector.reciprocal(recips[:, :].unsqueeze(2), heads[:, :, D:D + 1]).then_inc(recip_done, 1)
                dve.wait_ge(recip_done, n + 1)
                nc.vector.tensor_tensor(merged[:, :].rearrange("p (h d) -> p h d", d=D), heads[:, :, 0:D],
                                        recips[:, :].unsqueeze(2).to_broadcast([P, H, D]), ALU.mult
                                        ).then_inc(merged_done, 1)

            def norm(u, j):
                n = TILES * u.u + j
                r = j % 2
                wait(dve, yt_mm, n - 1)
                wait(dve, scaled, n - 1)
                if conv:
                    dve.wait_ge(merged_done, n + 1)
                    ins = nc.vector.tensor_tensor(z[:, r, :], fbank[:, 2 * P:3 * P], merged[:, :], ALU.add)
                else:
                    dve.wait_ge(out_mm, n + 1)
                    if j == 0:
                        dve.wait_ge(resid_ready, u.u + 1)
                    ins = nc.vector.tensor_tensor(z[:, r, :], fbank[:, 0:W], resid[:, u.par, j * W:(j + 1) * W], ALU.add)
                ins.then_inc(z_done, 1)
                dve.wait_ge(z_done, n + 1)
                nc.vector.bn_stats(stats[:, r, :], z[:, r, :]).then_inc(stats_done, 1)
                wait_apart(dve, stats_done, n + 1, passed["dve"])
                nc.vector.bn_aggr(moments[:, r, :], stats[:, r, :]).then_inc(moments_done, 1)
                dve.wait_ge(moments_done, n + 1)
                nc.vector.tensor_scalar(moments[:, r, 1:2], moments[:, r, 1:2], EPS, None, ALU.add).then_inc(var_done, 1)

            def normalise(u, j):
                n = TILES * u.u + j
                r = j % 2
                dve.wait_ge(rstd_done, n + 1)
                nc.vector.tensor_scalar(z[:, r, :], z[:, r, :], moments[:, r, 0:1], rstd[:, r, 0:1],
                                        ALU.subtract, ALU.mult).then_inc(normed, 1)

            def body(t):
                for slot in range(16):
                    if exists(t.plus(1), N):
                        for i in range(CHUNKS):
                            if SCORE_SLOT[i] == slot:
                                max_of(t.plus(1), i)
                        if slot == MAX_SLOT - 1:
                            split_max(t.plus(1))
                    if exists(t, N) and phase != 2:
                        mask_scores(t, slot)
                    if slot - 1 in P_SLOT and exists(t.plus(2), N):
                        mid_part(t.plus(2), P_SLOT.index(slot - 1))
                    if not conv:
                        if at := all_finish(N, t, slot, 2):
                            norm(*at)
                    if at := all_finish(N, t, slot, NORM_STEP):
                        normalise(*at)
                    if at := all_finish(N, t, slot, 0):
                        merge(*at)
                        if conv:
                            norm(*at)

            iterations(dve, N, 2, 1, body)

        @block.gpsimd
        def _(pool):
            def pad_edges(u):
                wait_apart(pool, xin_ld[u.par], 16 * XIN_LOADS * (u.k + 1), passed["pool"])
                for buf in (x_pad, c_pad):
                    ins = nc.gpsimd.tensor_copy(buf[:, u.par, :, 0:L + 2:L + 1], buf[:, u.par, :, 2:L:L - 3])
                ins.then_inc(padded, 1)

            def add_bias(u):
                pool.wait_ge(resid_ld[u.par], 16 * (u.k + 1))
                r = resid[:, u.par, :].rearrange("p (b d) -> p b d", b=TILES)
                nc.gpsimd.tensor_tensor(r, r, bo[:, :].unsqueeze(1).to_broadcast([P, TILES, L]), ALU.add
                                        ).then_inc(resid_ready, 1)

            def scale_pmask(u):
                wait_apart(pool, pmask_ld[u.par], 16 * (u.k + 1), passed["pool"])
                m = pmask[:, u.par, :, :]
                nc.gpsimd.tensor_scalar(m, m, MASKED, None, ALU.mult).then_inc(pmask_ready, 1)

            def first_rest(u, i):
                n = HALVES * u.u + i
                pool.wait_ge(proj_out, n + 1)
                rest = yproj[:, i % 2, :]
                nc.gpsimd.tensor_tensor(rest, rest, parts[:, u.par, i, HI, :], ALU.subtract).then_inc(rest_step, 1)

            def low_part(u, i):
                n = HALVES * u.u + i
                rest = yproj[:, i % 2, :]
                pool.wait_ge(mid_done, n + 1)
                nc.gpsimd.tensor_tensor(parts[:, u.par, i, LO, :], rest, parts[:, u.par, i, MID, :], ALU.subtract
                                        ).then_inc(split_done, 1)

            def power(u, j):
                n = TILES * u.u + j
                r = j % 2
                pool.wait_ge(var_done, n + 1)
                nc.gpsimd.tensor_tensor(rstd[:, r, :], moments[:, r, 1:2], c["minus_half"][:, :], ALU.pow
                                        ).then_inc(rstd_done, 1)

            def affine(u, j):
                n = TILES * u.u + j
                row = y[:, u.par, j, :]
                if j == 0:
                    wait(pool, stored[u.par], 16 * (2 if conv else 3) * u.k)
                pool.wait_ge(normed, n + 1)
                nc.gpsimd.tensor_tensor(row, z[:, j % 2, :], ln_g[:, 0:W], ALU.mult).then_inc(scaled, 1)
                pool.wait_ge(scaled, n + 1)
                nc.gpsimd.tensor_tensor(row, row, ln_b[:, 0:W], ALU.add).then_inc(y_done, 1)

            def body(t):
                if not conv and exists(t, N):
                    add_bias(t)
                for slot in range(16):
                    if slot in P_SLOT and exists(t.plus(2), N):
                        first_rest(t.plus(2), P_SLOT.index(slot))
                    if slot - 1 in P_SLOT and exists(t.plus(2), N):
                        low_part(t.plus(2), P_SLOT.index(slot - 1))
                    if at := all_finish(N, t, slot, 0 if conv else 2):
                        power(*at)
                    if at := all_finish(N, t, slot, NORM_STEP):
                        affine(*at)
                    if slot == 15 and phase == 2 and exists(t.plus(2), N):
                        scale_pmask(t.plus(2))
                    if slot == 15 and conv and exists(t.plus(3), N):
                        pad_edges(t.plus(3))

            for p in range(2):
                nc.gpsimd.memset(stack[STACK:STACKED, p, 1, :, :], 1.0).then_inc(ones_ready, 1)
                pool.wait_ge(ones_ready, p + 1)
            iterations(pool, N, 3, 1, body)

        running.close()
        reset(nc, sems)


def feed_forward(nc, top, c, io):
    NB, _, L = io["x"].shape
    F = io["ffn_w1"].shape[1]
    FT = F // P
    N = NB // TILES
    EPS = 1e-6
    with ExitStack() as ctx:
        def sb(n, shape, dt=F32):
            return ctx.enter_context(nc.sbuf_tensor(f"ffn_{n}", shape, dt))

        def sem(n):
            return ctx.enter_context(nc.semaphore(f"ffn_{n}"))

        w1, w2 = sb("w1", [P, 2, F]), sb("w2", [P, FT, L])
        xin = sb("xin", [P, 2, 2, TOK])
        resid = sb("resid", [P, 2, TILES, L])
        hidden = sb("hidden", [P, 2, FT, TOK])
        z = sb("z", [P, 2, L])
        stats, moments, rstd = sb("stats", [P, 2, 6]), sb("moments", [P, 2, 2]), sb("rstd", [P, 2, 1])
        y = sb("y", [P, 2, TILES, L])
        hbank = [ctx.enter_context(nc.psum_tensor(f"ffn_h{i}", [P, 512], F32)) for i in range(4)]
        obank = [ctx.enter_context(nc.psum_tensor(f"ffn_o{i}", [P, 512], F32)) for i in range(4)]
        weights = sem("weights")
        xin_ld = [sem(f"xin_ld{i}") for i in range(2)]
        resid_ld = [sem(f"resid_ld{i}") for i in range(2)]
        resid_ready = sem("resid_ready")
        h_mm, h_out = sem("h_mm"), sem("h_out")
        o_mm = sem("o_mm")
        z_done, stats_done, moments_done, var_done, rstd_done = (
            sem("z_done"), sem("stats_done"), sem("moments_done"), sem("var_done"), sem("rstd_done"))
        normed, scaled, y_done = sem("normed"), sem("scaled"), sem("y_done")
        passed, passed_sp = sem("passed_dve"), sem("passed_sp")
        stored = [sem(f"stored{i}") for i in range(2)]
        xt_units = io["o2t"].rearrange("(u b) k p s -> u p k b s", b=TILES)
        res_units = io["o2"].rearrange("(u b) s d -> u s b d", b=TILES)
        out_units = io["out"].rearrange("(u b) s d -> u s b d", b=TILES)
        block = ctx.enter_context(nc.Block())

        @block.sync
        def _(sp):
            sp.dma_start(w1[:, :, :], io["ffn_w1"].rearrange("(k p) n -> p k n", p=P)).then_inc(weights, 16)
            sp.dma_start(w2[:, :, :], io["ffn_w2"].rearrange("(k p) n -> p k n", p=P)).then_inc(weights, 16)

            def body(t):
                u = t.plus(1)
                if exists(u, N):
                    wait_sp(sp, h_mm, FT * (u.u - 1), passed_sp)
                    for kt in range(2):
                        sp.dma_start(xin[:, u.par, kt, :].rearrange("p (b s) -> p b s", b=TILES),
                                     xt_units[u.u][:, kt]).then_inc(xin_ld[u.par], 16)
                    wait_sp(sp, z_done, TILES * (u.u - 1), passed_sp)
                    sp.dma_start(resid[:, u.par, :, :], res_units[u.u]).then_inc(resid_ld[u.par], 16)
                if exists(t, N):
                    wait_sp(sp, y_done, TILES * (t.u + 1), passed_sp)
                    sp.dma_start(out_units[t.u], y[:, t.par, :, :]).then_inc(stored[t.par], 16)

            iterations(sp, N, 1, 0, body)
            for p in range(2):
                sp.wait_ge(stored[p], 16 * (N // 2))

        @block.tensor
        def _(pe):
            pe.wait_ge(weights, 32)

            def body(t):
                pe.wait_ge(xin_ld[t.par], 32 * (t.k + 1))
                for f in range(FT):
                    wait(pe, h_out, FT * t.u + f - 3)
                    for kt in range(2):
                        mm = nc.tensor.matmul(hbank[f % 4][:, :], w1[:, kt, f * P:(f + 1) * P], xin[:, t.par, kt, :],
                                              start=(kt == 0), stop=(kt == 1))
                    mm.then_inc(h_mm, 1)
                for j in range(TILES):
                    wait(pe, z_done, TILES * (t.u - 1) + j + 1 if t.number() != 0 else 0)
                    if j == 0:
                        pe.wait_ge(h_out, FT * (t.u + 1))
                    for f in range(FT):
                        mm = nc.tensor.matmul(obank[j][:, 0:L], hidden[:, t.par, f, j * P:(j + 1) * P], w2[:, f, :],
                                              start=(f == 0), stop=(f == FT - 1))
                    mm.then_inc(o_mm, 1)

            iterations(pe, N, 0, 0, body)

        @block.scalar
        def _(act):
            def body(t):
                wait(act, o_mm, TILES * (t.u - 1))
                for f in range(FT):
                    act.wait_ge(h_mm, FT * t.u + f + 1)
                    nc.scalar.activation(hidden[:, t.par, f, :], hbank[f % 4][:, :], ACT.Relu,
                                         bias=c["ffn_b1_s"][:, f:f + 1]).then_inc(h_out, 1)

            iterations(act, N, 0, 0, body)

        @block.vector
        def _(dve):
            def body(t):
                dve.wait_ge(resid_ready, t.u + 1)
                for j in range(TILES):
                    n = TILES * t.u + j
                    r = j % 2
                    wait(dve, scaled, n - 1)
                    dve.wait_ge(o_mm, n + 1)
                    nc.vector.tensor_tensor(z[:, r, :], obank[j][:, 0:L], resid[:, t.par, j, :], ALU.add).then_inc(z_done, 1)
                    dve.wait_ge(z_done, n + 1)
                    nc.vector.bn_stats(stats[:, r, :], z[:, r, :]).then_inc(stats_done, 1)
                    wait_apart(dve, stats_done, n + 1, passed)
                    nc.vector.bn_aggr(moments[:, r, :], stats[:, r, :]).then_inc(moments_done, 1)
                    dve.wait_ge(moments_done, n + 1)
                    nc.vector.tensor_scalar(moments[:, r, 1:2], moments[:, r, 1:2], EPS, None, ALU.add
                                            ).then_inc(var_done, 1)
                    dve.wait_ge(rstd_done, n + 1)
                    nc.vector.tensor_scalar(z[:, r, :], z[:, r, :], moments[:, r, 0:1], rstd[:, r, 0:1],
                                            ALU.subtract, ALU.mult).then_inc(normed, 1)

            iterations(dve, N, 0, 0, body)

        @block.gpsimd
        def _(pool):
            def body(t):
                pool.wait_ge(resid_ld[t.par], 16 * (t.k + 1))
                nc.gpsimd.tensor_tensor(resid[:, t.par, :, :], resid[:, t.par, :, :],
                                        c["ffn_b2"][:, :].unsqueeze(1).to_broadcast([P, TILES, L]), ALU.add
                                        ).then_inc(resid_ready, 1)
                for j in range(TILES):
                    n = TILES * t.u + j
                    r = j % 2
                    row = y[:, t.par, j, :]
                    pool.wait_ge(var_done, n + 1)
                    nc.gpsimd.tensor_tensor(rstd[:, r, :], moments[:, r, 1:2], c["minus_half"][:, :], ALU.pow
                                            ).then_inc(rstd_done, 1)
                    if j == 0:
                        wait(pool, stored[t.par], 16 * t.k)
                    pool.wait_ge(normed, n + 1)
                    nc.gpsimd.tensor_tensor(row, z[:, r, :], c["ln3_g"][:, :], ALU.mult).then_inc(scaled, 1)
                    pool.wait_ge(scaled, n + 1)
                    nc.gpsimd.tensor_tensor(row, row, c["ln3_b"][:, :], ALU.add).then_inc(y_done, 1)

            iterations(pool, N, 0, 0, body)


def build(nc, io):
    with ExitStack() as top:
        c = {}
        with ExitStack() as l0:
            constants(nc, top, l0, io, c)
            attention(nc, top, c, io, 0)
        attention(nc, top, c, io, 1)
        attention(nc, top, c, io, 2)
        feed_forward(nc, top, c, io)


def _laid_out(inputs):
    import numpy as np

    a = {k: np.asarray(v) for k, v in inputs.items()}
    out = {"x": a["x"], "ctx": a["ctx_1024"], "mask0": a["L0_xattn_mask"], "mask1": a["mask_1x1xSxS2_fk1"],
           "mask2": a["mask_Bx1x1xS2_fk0"], "gamma": a["L0_xattn_gamma"], "beta": a["L0_xattn_beta"]}
    for n in "qkv":
        out[f"conv_{n}"] = a[f"L0_xattn_w{n}"].reshape(8, 16, 16, 3).transpose(0, 2, 3, 1)
    for m in ("mha1", "mha2"):
        for n in "qk":
            out[f"{m}_w{n}"] = a[f"L1_xattn_{m}_w{n}"].reshape(256, 2, 8, 16).transpose(0, 1, 3, 2).reshape(256, 256)
            out[f"{m}_b{n}"] = a[f"L1_xattn_{m}_b{n}"].reshape(2, 8, 16).transpose(2, 1, 0).reshape(128, 2)
        out[f"{m}_wv"], out[f"{m}_wo"] = a[f"L1_xattn_{m}_wv"], a[f"L1_xattn_{m}_wo"]
        out[f"{m}_bv"] = a[f"L1_xattn_{m}_bv"].reshape(2, 128).T
        out[f"{m}_bo"] = a[f"L1_xattn_{m}_bo"]
    out["ffn_w1"], out["ffn_w2"], out["ffn_b2"] = (a[f"L1_xattn_ffn_{n}"] for n in ("w1", "w2", "b2"))
    out["ffn_b1"] = a["L1_xattn_ffn_b1"].reshape(8, 128).T
    for i in (1, 2, 3):
        for n in "gb":
            out[f"ln{i}_{n}"] = a[f"L1_xattn_ln{i}_{n}"]
    for i in (1, 2):
        for n in "gb":
            out[f"ln{i}_{n}c"] = out[f"ln{i}_{n}"].reshape(2, 128).T
    out["g0_col"], out["b0_col"] = out["gamma"].reshape(128, 1), out["beta"].reshape(128, 1)
    return {k: np.ascontiguousarray(v) for k, v in out.items()}


def kernel(**inputs):
    import concourse.bacc as bacc
    from concourse.bass_utils import run_bass_kernel_spmd

    nc = bacc.Bacc("TRN2", target_bir_lowering=False, num_devices=1)
    arrays, io = {}, {}
    for name, a in _laid_out(inputs).items():
        arrays[f"in_{name}"] = a
        io[name] = nc.dram_tensor(f"in_{name}", a.shape, mybir.dt.from_np(a.dtype), kind="ExternalInput").ap()
    NB, S, L = arrays["in_x"].shape
    for name in ("x1", "o1", "o2"):
        io[name] = nc.dram_tensor(f"rows_{name}", (NB, S, L), F32, kind="Internal").ap()
        io[f"{name}t"] = nc.dram_tensor(f"cols_{name}", (NB, 2, P, S), F32, kind="Internal").ap()
    io["out"] = nc.dram_tensor("out_0", (NB, S, L), F32, kind="ExternalOutput").ap()
    build(nc, io)
    r = run_bass_kernel_spmd(nc, [arrays], core_ids=[0])
    return r.results[0]["out_0"]
```

```python
from contextlib import ExitStack

import concourse.bass as bass
from concourse import mybir

F32 = mybir.dt.float32
BF16 = mybir.dt.bfloat16
ALU = mybir.AluOpType
ACT = mybir.ActivationFunctionType

P = 128
D = 16
TILES = 4
TOK = TILES * P
CHUNKS = 16
HI, MID, LO = range(3)
SLOTS = [(HI, HI), (HI, MID), (HI, LO), (MID, HI), (MID, MID), (LO, HI)]
STACK = len(SLOTS) * D
STACKED = STACK + 3
MASKED = -1.0e9
LOWEST = -3.0e38
PV_LAG = 2
FINISH = ({"turn": 6, "merge": 7, "norm": 7, "normalise": 9},
          {"turn": 6, "merge": 7, "turn_merged": 7, "output": 8, "norm": 9, "normalise": 11})
SCORE_SLOTS = ([5 + i * 13 // 15 for i in range(CHUNKS)], [6 + i * 12 // 15 for i in range(CHUNKS)],
               [6 + i * 12 // 15 for i in range(CHUNKS)])
WORK = (
    [((0,), "values", 1, 0), ((1,), "values", 1, 1), ((2,), "turn_y", -1, 2), ((4,), "max", 0, 1),
     ((6,), "turn_y", -1, 3), ((7, 8), "project", 2, 0), ((9, 10), "project", 2, 1), ((10,), "turn_y", 0, 0),
     ((13,), "max", 1, 0), ((14,), "turn_y", 0, 1)],
    [((0,), "values", 1, 0), ((2,), "values", 1, 1), ((4,), "turn_y", -1, 2), ((4,), "max", 0, 1),
     ((5,), "project", 2, 0), ((7,), "project", 2, 1), ((8,), "turn_y", -1, 3),
     ((9,), "project", 2, 2), ((11,), "project", 2, 3), ((12,), "turn_y", 0, 0), ((14,), "max", 1, 0),
     ((15,), "turn_y", 0, 1)],
    [((0,), "values", 1, 0), ((2,), "values", 1, 1), ((3,), "context", 2, 0), ((4,), "turn_y", -1, 2),
     ((4,), "max", 0, 1), ((5,), "project", 2, 0), ((6,), "context", 2, 1), ((7,), "project", 2, 1),
     ((8,), "turn_y", -1, 3), ((9,), "project", 2, 2), ((11,), "project", 2, 3), ((12,), "turn_y", 0, 0),
     ((14,), "max", 1, 0), ((15,), "turn_y", 0, 1)],
)


class Unit:

    def __init__(self, k, par):
        self.k, self.par = k, par
        self.u = 2 * k + par

    def plus(self, n):
        at = self.par + n
        return Unit(self.k + at // 2, at % 2)

    def number(self):
        return self.u if isinstance(self.u, int) else None


def wait_sp(sp, sem, value, passed):
    if isinstance(value, int):
        wait(sp, sem, value)
    else:
        wait_apart(sp, sem, value, passed)


def wait(eng, sem, value):
    if isinstance(value, int) and value <= 0:
        return
    eng.wait_ge(sem, value)


def wait_apart(eng, sem, value, passed):
    eng.wait_ge(sem, value).then_inc(passed, 1)


def iterations(eng, n, before, after, body):
    assert n % 2 == 0
    first = 1
    last = max(n // 2 - (before + 1) // 2, first)
    for t in range(-before, 2 * first):
        body(Unit(t // 2, t % 2))
    if last > first:
        with eng.Fori(first, last) as k:
            body(Unit(k, 0))
            body(Unit(k, 1))
    for t in range(2 * last, n + after):
        body(Unit(t // 2, t % 2))


class WorkBanks:

    def __init__(self, uses, n):
        self.uses, self.n = uses, n
        self.at = {(what, step): (i, off) for i, (_, what, off, step) in enumerate(uses)}
        assert len(uses) % 2 == 0

    def bank(self, what, step):
        return self.at[what, step][0] % 2

    def before(self, t, place):
        if t.number() is None:
            return len(self.uses) * t.u + place + self.before(Unit(1, 0), 0) - 2 * len(self.uses)
        return sum(0 <= i + off < self.n for i in range(-3, t.u + 1)
                   for p, (_, _, off, _) in enumerate(self.uses) if i < t.u or p < place)

    def number(self, u, what, step):
        place, off = self.at[what, step]
        return self.before(u.plus(-off), place)

    def free(self, u, what, step):
        place, off = self.at[what, step]
        t, place = u.plus(-off), place - 2
        while t.number() is None or t.number() >= -3:
            if place < 0:
                t, place = t.plus(-1), place + len(self.uses)
            elif exists(t.plus(self.uses[place][2]), self.n):
                return self.before(t, place) + 1
            else:
                place -= 2
        return 0

    def in_slot(self, t, slot):
        return [(t.plus(off), what, step, slots.index(slot), len(slots))
                for slots, what, off, step in self.uses if slot in slots and exists(t.plus(off), self.n)]


def exists(unit, n):
    at = unit.number()
    return at is None or 0 <= at < n


def reset(nc, sems):
    with nc.Block() as block:
        @block.gpsimd
        def _(pool):
            for s in sems:
                pool.sem_clear(s)


def constants(nc, top, l0, io, c):
    def sb(name, shape, dt=F32):
        c[name] = top.enter_context(nc.sbuf_tensor(name, shape, dt))
        return c[name]

    def sb_l0(name, shape, dt=F32):
        c[name] = l0.enter_context(nc.sbuf_tensor(name, shape, dt))
        return c[name]

    L = io["x"].shape[2]
    LT = L // P
    NB = io["x"].shape[0]
    F = io["ffn_w1"].shape[1]

    ident = sb("ident", [P, P])
    identb = sb("identb", [P, P], BF16)
    mask1 = sb("mask1", [P, P])
    mask1t = sb("mask1t", [P, P])
    pad_bias = sb("pad_bias", [P, NB])
    rows = {n: sb(n, [P, L]) for n in ("ln1_g", "ln1_b", "ln2_g", "ln2_b", "ln3_g", "ln3_b",
                                       "mha1_bo", "mha2_bo", "ffn_b2")}
    bq = {m: sb(f"{m}_bq_s", [P, 2]) for m in ("mha1", "mha2")}
    bk = {m: sb(f"{m}_bk_s", [P, 2]) for m in ("mha1", "mha2")}
    bv = {m: sb(f"{m}_bv_s", [P, 2]) for m in ("mha1", "mha2")}
    c["bq"], c["bk"], c["bv"] = bq, bk, bv
    b1 = sb("ffn_b1_s", [P, F // P])
    cols = {n: sb(n, [P, 2]) for n in ("ln1_gc", "ln1_bc", "ln2_gc", "ln2_bc")}
    minus_half = sb("minus_half", [P, 1])
    conv = {n: sb_l0(f"conv_{n}", [P, 3, P]) for n in "qkv"}
    c["conv"] = conv
    mask0 = sb_l0("mask0", [P, LT, L])
    mask0t = sb_l0("mask0t", [P, LT, L])
    g0, b0 = sb_l0("g0", [P, P]), sb_l0("b0", [P, P])
    cols.update({n: sb_l0(n, [P, 1]) for n in ("g0_col", "b0_col")})

    with ExitStack() as ctx:
        dense = {n: ctx.enter_context(nc.sbuf_tensor(f"dense_{n}", [P, 3, P], F32)) for n in "qk"}
        pad = ctx.enter_context(nc.sbuf_tensor("pad_rows", [P, P], F32))
        wo = {m: ctx.enter_context(nc.sbuf_tensor(f"setup_wo_{m}", [P, 2, L], F32)) for m in ("mha1", "mha2")}
        bvw = ctx.enter_context(nc.sbuf_tensor("bv_wide", [P, 4, P], F32))
        ps = [ctx.enter_context(nc.psum_tensor(f"setup_ps{i}", [P, 512], F32)) for i in range(8)]
        zeroed = top.enter_context(nc.semaphore("zeroed"))
        ident_zero = top.enter_context(nc.semaphore("ident_zero"))
        ident_ready = top.enter_context(nc.semaphore("ident_ready"))
        loaded = top.enter_context(nc.semaphore("consts_loaded"))
        scaled = top.enter_context(nc.semaphore("masks_scaled"))
        turned = top.enter_context(nc.semaphore("masks_turned"))
        widened = top.enter_context(nc.semaphore("bv_widened"))
        bvwo = top.enter_context(nc.semaphore("bv_times_wo"))
        done = top.enter_context(nc.semaphore("consts_done"))
        block = ctx.enter_context(nc.Block())

        blocks = {"q": dense["q"], "k": dense["k"], "v": conv["v"]}
        loads = []
        for n in "qkv":
            for g in range(P // D):
                loads.append((blocks[n][g * D:(g + 1) * D, :, g * D:(g + 1) * D], io[f"conv_{n}"][g]))
        loads += [(mask0[:, t, :], io["mask0"][t * P:(t + 1) * P, :]) for t in range(LT)]
        loads += [(mask1[:, :], io["mask1"][0, 0]), (pad[0:NB, :], io["mask2"][:, 0, 0, :])]
        loads += [(g0[:, :], io["gamma"].partition_broadcast(P)), (b0[:, :], io["beta"].partition_broadcast(P))]
        loads += [(t[:, :], io[n].partition_broadcast(P)) for n, t in rows.items()]
        loads += [(t[:, :], io[f"{m}_{n}"]) for n, ts in (("bq", bq), ("bk", bk), ("bv", bv)) for m, t in ts.items()]
        loads += [(b1[:, :], io["ffn_b1"])] + [(t[:, :], io[n]) for n, t in cols.items()]
        loads += [(wo[m][:, :, :], io[f"{m}_wo"].rearrange("(k p) n -> p k n", p=P)) for m in wo]

        @block.gpsimd
        def _(pool):
            for t in (dense["q"], dense["k"], conv["v"], pad):
                nc.gpsimd.memset(t[:], 0.0).then_inc(zeroed, 1)
            nc.gpsimd.memset(minus_half[:, :], -0.5)
            nc.gpsimd.memset(ident[:, :], 0.0).then_inc(ident_zero, 1)
            nc.gpsimd.memset(identb[:, :], 0.0).then_inc(ident_zero, 1)
            pool.wait_ge(ident_zero, 2)
            for t in (ident, identb):
                nc.gpsimd.affine_select(out=t[:, :], in_=t[:, :], compare_op=ALU.not_equal, fill=1.0, base=0,
                                        pattern=[[-1, P]], channel_multiplier=1).then_inc(ident_ready, 1)

        @block.sync
        def _(sp):
            sp.wait_ge(zeroed, 4)
            for out, in_ in loads:
                sp.dma_start(out, in_).then_inc(loaded, 16)

        @block.vector
        def _(dve):
            dve.wait_ge(loaded, 16 * len(loads))
            for t in (mask0, mask1, pad):
                nc.vector.tensor_scalar(t[:], t[:], MASKED, None, ALU.mult).then_inc(scaled, 1)
            for n in "qk":
                nc.vector.tensor_copy(conv[n][:, :, :].rearrange("p t (d g) -> p t d g", d=D),
                                      dense[n][:, :, :].rearrange("p t (g d) -> p t d g", d=D))
            for m in bq:
                nc.vector.tensor_scalar(bq[m][:, :], bq[m][:, :], float(D) ** -0.5, None, ALU.mult)
            nc.vector.memset(bvw[:], 1.0).then_inc(widened, 1)
            dve.wait_ge(widened, 1)
            for i, m in enumerate(("mha1", "mha2")):
                for kt in range(2):
                    nc.vector.tensor_scalar(bvw[:, 2 * i + kt, :], bvw[:, 2 * i + kt, :], bv[m][:, kt:kt + 1],
                                            None, ALU.mult).then_inc(widened, 1)
            dve.wait_ge(bvwo, 2)
            for i, m in enumerate(("mha1", "mha2")):
                nc.vector.tensor_tensor(rows[f"{m}_bo"][:, :], rows[f"{m}_bo"][:, :], ps[i][:, 0:L], ALU.add)
            dve.wait_ge(turned, 3)
            for a in range(LT):
                nc.vector.tensor_copy(mask0t[:, a, :], ps[2 + a][:, 0:L])
            nc.vector.tensor_copy(mask1t[:, :], ps[4][:, 0:P])
            nc.vector.tensor_copy(pad_bias[:, 0:NB], ps[5][:, 0:NB]).then_inc(done, 1)

        @block.tensor
        def _(pe):
            pe.wait_ge(widened, 5)
            for i, m in enumerate(("mha1", "mha2")):
                for kt in range(2):
                    mm = nc.tensor.matmul(ps[i][:, 0:L], bvw[:, 2 * i + kt, :], wo[m][:, kt, :],
                                          start=(kt == 0), stop=(kt == 1))
                mm.then_inc(bvwo, 1)
            pe.wait_ge(ident_ready, 2)
            pe.wait_ge(scaled, 3)
            for a in range(LT):
                for b in range(LT):
                    mm = nc.tensor.transpose(ps[2 + a][:, b * P:(b + 1) * P], mask0[:, b, a * P:(a + 1) * P], ident[:, :])
            mm.then_inc(turned, 1)
            nc.tensor.transpose(ps[4][:, 0:P], mask1[:, :], ident[:, :]).then_inc(turned, 1)
            nc.tensor.transpose(ps[5][:, 0:P], pad[:, :], ident[:, :]).then_inc(turned, 1)

        @block.scalar
        def _(act):
            act.wait_ge(done, 1)


def attention(nc, top, c, io, phase):
    conv = phase == 0
    name = ("l0", "mha1", "mha2")[phase]
    H = 8 if conv else 16
    QUADS = H // 4
    KT = 2 if conv else 1
    BU = TILES // KT
    N = io["x"].shape[0] // BU
    GROUPS = H // 8
    HALVES = 2 * GROUPS
    VSTEPS = 2
    W = P if conv else 2 * P
    SCALE = 8.0 ** -0.5 if conv else float(D) ** -0.5
    EPS = 1e-5 if conv else 1e-6
    L = io["x"].shape[2]
    KEYS = KT * P
    SH = 512 // KEYS

    with ExitStack() as ctx:
        def sb(n, shape, dt=F32):
            return ctx.enter_context(nc.sbuf_tensor(f"{name}_{n}", shape, dt))

        sems = []

        def sem(n):
            sems.append(ctx.enter_context(nc.semaphore(f"{name}_{n}")))
            return sems[-1]

        if conv:
            x_pad = sb("x_pad", [P, 2, BU, L + 2])
            c_pad = sb("c_pad", [P, 2, BU, L + 2])
        else:
            xin = sb("xin", [P, 2, 2, TOK])
        if phase == 2:
            craw = sb("craw", [P, 2, TILES, L])
            cin = sb("cin", [P, 2, 2, TOK])
            pmask = sb("pmask", [P, 2, TILES, P])
        if not conv:
            wq, wk, wv, wo = (sb(n, [P, 2, L]) for n in ("wq", "wk", "wv", "wo"))
        resid = sb("resid", [P, 2, TILES * W])
        yproj = sb("yproj", [P, 2, TOK])
        parts = sb("parts", [P, 2, HALVES, 3, TOK], BF16)
        stack = sb("stack", [P, 2, 2 * H, TOK], BF16)
        vals = sb("vals", [P, 2, TILES, H, 32])
        junk = sb("junk", [P, 2, 512], BF16)
        maxes = sb("maxes", [P, TILES, H])
        max_rest = sb("max_rest", [P, TILES, H])
        max_parts = sb("max_parts", [P, TILES, 3, H], BF16)
        max_rows = sb("max_rows", [3 * H, 2 * P], BF16)
        probs = sb("probs", [P, 4, 512])
        heads_out = sb("heads_out", [P, 2, QUADS * P])
        recips = sb("recips", [P, H])
        merged = sb("merged", [P, H * D])
        merged_t = sb("merged_t", [P, 2, P])
        z = sb("z", [P, 2, W])
        stats = sb("stats", [P, 2, 6])
        moments = sb("moments", [P, 2, 2])
        rstd = sb("rstd", [P, 2, 1])
        y = sb("y", [P, 2, TILES, W])
        y_t = sb("y_t", [P, 2, TILES * W])

        bank = [ctx.enter_context(nc.psum_tensor(f"{name}_bank{i}", [P, 512], F32)) for i in range(8)]
        work, sbank, tbank, pvbank, fbank = bank[0:2], bank[2:4], bank[4:6], bank[6], bank[7]

        const_ready, ones_ready = sem("const_ready"), sem("ones_ready")
        passed = {e: sem(f"passed_{e}") for e in ("pe", "act", "dve", "pool", "sp")}
        weights = sem("weights")
        xin_ld = [sem(f"xin_ld{i}") for i in range(2)]
        resid_ld = [sem(f"resid_ld{i}") for i in range(2)]
        pmask_ld = [sem(f"pmask_ld{i}") for i in range(2)]
        padded = sem("padded")
        pmask_ready = sem("pmask_ready")
        resid_ready = sem("resid_ready")
        work_mm, work_out = sem("work_mm"), sem("work_out")
        mid_done = sem("mid_done")
        rest_step, split_done = sem("rest_step"), sem("split_done")
        stack_in = [sem(f"stack_in{p}") for p in range(2)]
        score_mm, score_max = sem("score_mm"), sem("score_max")
        max_step, max_split = sem("max_step"), sem("max_split")
        max_in = [sem(f"max_in{i}") for i in range(2)]
        att_mm, att_masked, att_exp, att_pv = sem("att_mm"), sem("att_masked"), sem("att_exp"), sem("att_pv")
        heads_done = sem("heads_done")
        turn_mm, recip_done, merged_done = sem("turn_mm"), sem("recip_done"), sem("merged_done")
        mt_mm, mt_out = sem("mt_mm"), sem("mt_out")
        out_mm = sem("out_mm")
        z_done, stats_done, moments_done, var_done, rstd_done = (
            sem("z_done"), sem("stats_done"), sem("moments_done"), sem("var_done"), sem("rstd_done"))
        normed, scaled, y_done = sem("normed"), sem("scaled"), sem("y_done")
        stored = [sem(f"stored{i}") for i in range(2)]

        if conv:
            x_units = io["x"].rearrange("(u b) c l -> u c b l", b=BU)
            c_units = io["ctx"].rearrange("(u b) c l -> u c b l", b=BU)
            out_rows = io["x1"].rearrange("(u b) s d -> u s b d", b=BU)
            out_cols = io["x1t"].rearrange("(u b) k p s -> u p (b k) s", b=BU)
            res_units = x_units
            bo = None
            ln_g, ln_b, ln_gc, ln_bc = c["g0"], c["b0"], c["g0_col"], c["b0_col"]
        else:
            src_t, src, dst, dst_t = (("x1t", "x1", "o1", "o1t"), ("o1t", "o1", "o2", "o2t"))[phase - 1]
            xt_units = io[src_t].rearrange("(u b) k p s -> u p k b s", b=BU)
            res_units = io[src].rearrange("(u b) s d -> u s b d", b=BU)
            c_units = io["ctx"].rearrange("(u b) s d -> u s b d", b=BU)
            out_rows = io[dst].rearrange("(u b) s d -> u s b d", b=BU)
            out_cols = io[dst_t].rearrange("(u b) k p s -> u p k b s", b=BU)
            bo = c[f"{name}_bo"]
            ln_g, ln_b, ln_gc, ln_bc = (c[f"ln{phase}_{n}"] for n in ("g", "b", "gc", "bc"))
        mask2_units = io["mask2"].rearrange("(u b) i j m -> u (b i j m)", b=TILES) if phase == 2 else None
        XIN_LOADS = 2 if conv else (2 if phase == 1 else 3)
        HALF_SIDE = [(g, side) for side in range(2) for g in range(GROUPS)]
        FILLS = [(s, pair[0], (0, 1)) for s, pair in enumerate(SLOTS) if conv and pair[0] == pair[1]]
        FILLS += [(s, pair[side], (side,)) for s, pair in enumerate(SLOTS) for side in range(2)
                  if not (conv and pair[0] == pair[1])]

        def place(side, h):
            return 2 * h + side if conv else H * side + 2 * (h % 8) + h // 8

        def side_of(sides):
            if len(sides) == 2:
                return slice(0, 2 * H)
            return slice(sides[0], 2 * H, 2) if conv else slice(H * sides[0], H * sides[0] + H)

        def att_chunks():
            return [(j, q, kt) for j in range(TILES) for q in range(QUADS) for kt in range(KT)]

        ATT = att_chunks()
        SCO = [(j, h) for j in range(TILES) for h in range(0, H, SH)]
        assert len(ATT) == len(SCO) == CHUNKS
        SCORE_SLOT, finish = SCORE_SLOTS[phase], FINISH[not conv]
        banks = WorkBanks(WORK[phase], N)
        P_SLOT = [slots[-1] for slots, what, _, _ in WORK[phase] if what == "project"]

        def scores_in(t, slot):
            return [(t.plus(off), i) for off in (0, 1) for i in range(CHUNKS)
                    if SCORE_SLOT[i] == slot + 16 * (1 - off) and exists(t.plus(off), N)]

        def splits_in(t, slot):
            return [(t.plus(off), half) for off in (0, 1) for half in range(2)
                    if SCORE_SLOT[8 * half + 7] + 1 == slot + 16 * (1 - off) and exists(t.plus(off), N)]

        def finish_in(t, slot, step):
            return [(t.plus(off), j) for off in (0, -1) for j in range(TILES)
                    if 4 * j + finish[step] == slot - 16 * off and exists(t.plus(off), N)]

        def work_count(u, what, step):
            return banks.number(u, what, step) + 1

        def turned(u, j, back=0):
            v, i = u.plus((j - back) // TILES), (j - back) % TILES
            return work_count(v, "turn_y", i) if exists(v, N) else 0

        def projected(u, i):
            return HALVES * u.u + i + 1

        running = ExitStack()
        block = running.enter_context(nc.Block())

        @block.sync
        def _(sp):
            if not conv:
                for t, n in ((wq, "wq"), (wk, "wk"), (wv, "wv"), (wo, "wo")):
                    sp.dma_start(t[:, :, :], io[f"{name}_{n}"].rearrange("(k p) n -> p k n", p=P)).then_inc(weights, 16)

            def load(u):
                if exists(u.plus(-2), N):
                    wait_sp(sp, work_mm, work_count(u.plus(-2), "values", VSTEPS - 1), passed["sp"])
                if conv:
                    sp.dma_start(x_pad[:, u.par, :, 1:L + 1], x_units[u.u]).then_inc(xin_ld[u.par], 16)
                    sp.dma_start(c_pad[:, u.par, :, 1:L + 1], c_units[u.u]).then_inc(xin_ld[u.par], 16)
                else:
                    for kt in range(2):
                        sp.dma_start(xin[:, u.par, kt, :].rearrange("p (b s) -> p b s", b=BU),
                                     xt_units[u.u][:, kt]).then_inc(xin_ld[u.par], 16)
                    if phase == 2:
                        sp.dma_start(craw[:, u.par, :, :], c_units[u.u]).then_inc(xin_ld[u.par], 16)

            def load_pmask(u):
                wait_sp(sp, score_max, CHUNKS * (u.u - 1), passed["sp"])
                sp.dma_start(pmask[:, u.par, :, :].rearrange("p b m -> p (b m)"),
                             mask2_units[u.u].partition_broadcast(P)).then_inc(pmask_ld[u.par], 16)

            def load_resid(u):
                if conv:
                    wait_sp(sp, turn_mm, TILES * (u.u - 1), passed["sp"])
                else:
                    wait_sp(sp, z_done, TILES * (u.u - 1), passed["sp"])
                sp.dma_start(resid[:, u.par, :].rearrange("p (b d) -> p b d", b=BU),
                             res_units[u.u]).then_inc(resid_ld[u.par], 16)

            def fill_stack(u):
                wait_sp(sp, att_mm, CHUNKS * (u.u - 1), passed["sp"])
                wait_sp(sp, split_done, projected(u, HALVES - 1), passed["sp"])
                for s, part, sides in FILLS:
                    sp.dma_start(stack[s * D:(s + 1) * D, u.par, side_of(sides), :],
                                 parts[:, u.par, GROUPS * sides[0]:GROUPS * (sides[-1] + 1), part, :]
                                 ).then_inc(stack_in[u.par], 16)

            def store(u):
                wait_sp(sp, y_done, TILES * (u.u + 1), passed["sp"])
                if conv:
                    sp.dma_start(out_cols[u.u], y[:, u.par, :, :]).then_inc(stored[u.par], 16)
                else:
                    sp.dma_start(out_rows[u.u], y[:, u.par, :, :]).then_inc(stored[u.par], 16)
                wait_sp(sp, work_out, turned(u, TILES - 1), passed["sp"])
                if conv:
                    sp.dma_start(out_rows[u.u], y_t[:, u.par, :].rearrange("p (b d) -> p b d", b=BU)
                                 ).then_inc(stored[u.par], 16)
                else:
                    for kt in range(2):
                        sp.dma_start(out_cols[u.u][:, kt],
                                     y_t[:, u.par, kt * TOK:(kt + 1) * TOK].rearrange("p (b s) -> p b s", b=BU)
                                     ).then_inc(stored[u.par], 16)

            def body(t):
                if exists(t, N):
                    load_resid(t)
                if exists(t.plus(1), N):
                    fill_stack(t.plus(1))
                if phase == 2 and exists(t.plus(2), N):
                    load_pmask(t.plus(2))
                if exists(t.plus(3), N):
                    load(t.plus(3))
                if exists(t.plus(-1), N):
                    store(t.plus(-1))

            iterations(sp, N, 3, 1, body)
            STORES = 2 if conv else 3
            for p in range(2):
                sp.wait_ge(stored[p], 16 * STORES * (N // 2))

        @block.tensor
        def _(pe):
            if not conv:
                pe.wait_ge(weights, 16 * 4)
            pe.wait_ge(const_ready, 1)

            def context_step(u, i, bank_):
                if i == 0:
                    pe.wait_ge(xin_ld[u.par], 16 * XIN_LOADS * (u.k + 1))
                for j in range(TILES):
                    mm = nc.tensor.transpose(bank_[:, j * P:(j + 1) * P], craw[:, u.par, j, i * P:(i + 1) * P],
                                             c["ident"][:, :])
                mm.then_inc(work_mm, 1)

            def project_step(u, i, bank_, piece, pieces):
                g, side = HALF_SIDE[i]
                if piece == 0:
                    if i == 0 and conv:
                        pe.wait_ge(padded, u.u + 1)
                    elif i == 0 and phase == 1:
                        pe.wait_ge(xin_ld[u.par], 16 * XIN_LOADS * (u.k + 1))
                    elif side == 1 and g == 0 and phase == 2:
                        pe.wait_ge(work_out, work_count(u, "context", 1))
                taps = 3 if conv else 2
                for tap in range(taps * piece // pieces, taps * (piece + 1) // pieces):
                    if conv:
                        mm = nc.tensor.matmul(bank_[:, :].rearrange("p (b l) -> p b l", b=BU),
                                              c["conv"]["qk"[side]][:, tap, :],
                                              (x_pad, c_pad)[side][:, u.par, :, tap:tap + L],
                                              start=(tap == 0), stop=(tap == taps - 1))
                    else:
                        src = cin if phase == 2 and side == 1 else xin
                        mm = nc.tensor.matmul(bank_[:, :], (wq, wk)[side][:, tap, g * P:(g + 1) * P],
                                              src[:, u.par, tap, :], start=(tap == 0), stop=(tap == taps - 1))
                if piece == pieces - 1:
                    mm.then_inc(work_mm, 1)

            def value_step(u, i, bank_):
                for j in range(2):
                    if conv:
                        for tap in range(3):
                            at = j * P + tap
                            mm = nc.tensor.matmul(bank_[:, j * P:(j + 1) * P], c_pad[:, u.par, i, at:at + P],
                                                  c["conv"]["v"][:, tap, :], start=(tap == 0), stop=(tap == 2))
                    else:
                        at = (2 * i + j) * P
                        for kt in range(2):
                            mm = nc.tensor.matmul(bank_[:, j * L:(j + 1) * L],
                                                  (cin if phase == 2 else xin)[:, u.par, kt, at:at + P],
                                                  wv[:, kt, :], start=(kt == 0), stop=(kt == 1))
                mm.then_inc(work_mm, 1)

            def score_step(u, i):
                j, h0 = SCO[i]
                if i == 0:
                    pe.wait_ge(stack_in[u.par], 16 * len(FILLS) * (u.k + 1))
                wait(pe, score_max, CHUNKS * u.u + i - 1)
                first = (j // KT) * KT * P
                for s in range(SH):
                    h = h0 + s
                    mm = nc.tensor.matmul(sbank[i % 2][:, s * KEYS:(s + 1) * KEYS],
                                          stack[0:STACK, u.par, place(0, h), j * P:(j + 1) * P],
                                          stack[0:STACK, u.par, place(1, h), first:first + KEYS], start=True, stop=True)
                mm.then_inc(score_mm, 1)

            def max_turn(u, half, bank_):
                wait_apart(pe, max_split, 2 * u.u + half + 1, passed["pe"])
                for j in range(2):
                    mm = nc.tensor.transpose(bank_[0:3 * H, j * 64:(j + 1) * 64].bitcast(BF16),
                                             max_parts[:, 2 * half + j, :, :].rearrange("p a h -> p (a h)"),
                                             c["identb"][:, :])
                mm.then_inc(work_mm, 1)

            def attend_step(u, i):
                j, q, kt = ATT[i]
                if i % 8 == 0:
                    pe.wait_ge(max_in[i // 8], 16 * (u.u + 1))
                    if u.number() == 0 and i == 0:
                        pe.wait_ge(ones_ready, 2)
                wait(pe, att_exp, CHUNKS * u.u + i - 1)
                key = ((j // KT) * KT + kt) * P
                for s in range(4):
                    h = 4 * q + s
                    mm = nc.tensor.matmul(tbank[i % 2][:, s * P:(s + 1) * P],
                                          stack[0:STACKED, u.par, place(1, h), key:key + P],
                                          stack[0:STACKED, u.par, place(0, h), j * P:(j + 1) * P], start=True, stop=True)
                mm.then_inc(att_mm, 1)

            def pv_step(u, i):
                j, q, kt = ATT[i]
                if i == 0:
                    pe.wait_ge(work_out, work_count(u, "values", VSTEPS - 1))
                if i % 4 == 0:
                    wait(pe, heads_done, TILES * u.u + j)
                pe.wait_ge(att_exp, CHUNKS * u.u + i + 1)
                for s in range(4):
                    mm = nc.tensor.matmul(pvbank[32 * s:32 * s + 32, q * P:(q + 1) * P],
                                          vals[:, u.par, (j // KT) * KT + kt, 4 * q + s, :],
                                          probs[:, i % 4, s * P:(s + 1) * P], start=(kt == 0), stop=(kt == KT - 1),
                                          tile_position=(0, 32 * s))
                mm.then_inc(att_pv, 1)

            def turn_heads(u, j):
                n = TILES * u.u + j
                pe.wait_ge(heads_done, n + 1)
                wait(pe, z_done, n)
                if conv and j == 0:
                    pe.wait_ge(resid_ld[u.par], 16 * (u.k + 1))
                for q in range(QUADS):
                    mm = nc.tensor.transpose(fbank[:, q * P:(q + 1) * P], heads_out[:, j % 2, q * P:(q + 1) * P],
                                             c["ident"][:, :])
                if conv:
                    mm = nc.tensor.transpose(fbank[:, 2 * P:3 * P], resid[:, u.par, j * P:(j + 1) * P], c["ident"][:, :])
                mm.then_inc(turn_mm, 1)

            def turn_merged(u, j):
                pe.wait_ge(merged_done, TILES * u.u + j + 1)
                for a in range(2):
                    mm = nc.tensor.transpose(fbank[:, a * P:(a + 1) * P], merged[:, a * P:(a + 1) * P], c["ident"][:, :])
                mm.then_inc(mt_mm, 1)

            def output_step(u, j):
                pe.wait_ge(mt_out, TILES * u.u + j + 1)
                for a in range(2):
                    mm = nc.tensor.matmul(fbank[:, 0:L], merged_t[:, a, :], wo[:, a, :], start=(a == 0), stop=(a == 1))
                mm.then_inc(out_mm, 1)

            def turn_y(u, j, bank_):
                pe.wait_ge(normed, TILES * u.u + j + 1)
                for a in range(W // P):
                    mm = nc.tensor.transpose(bank_[:, a * P:(a + 1) * P], z[:, j % 2, a * P:(a + 1) * P],
                                             c["ident"][:, :])
                mm.then_inc(work_mm, 1)

            def body(t):
                for slot in range(16):
                    if exists(t, N):
                        attend_step(t, slot)
                        if slot >= PV_LAG:
                            pv_step(t, slot - PV_LAG)
                    for u, i in scores_in(t, slot):
                        score_step(u, i)
                    for u, what, step, piece, pieces in banks.in_slot(t, slot):
                        bank_ = work[banks.bank(what, step)]
                        if piece == 0:
                            wait(pe, work_out, banks.free(u, what, step))
                        if what == "project":
                            project_step(u, step, bank_, piece, pieces)
                        elif what == "values":
                            value_step(u, step, bank_)
                        elif what == "context":
                            context_step(u, step, bank_)
                        elif what == "max":
                            max_turn(u, step, bank_)
                        else:
                            turn_y(u, step, bank_)
                    if not conv:
                        for at in finish_in(t, slot, "output"):
                            output_step(*at)
                        for at in finish_in(t, slot, "turn_merged"):
                            turn_merged(*at)
                    for at in finish_in(t, slot, "turn"):
                        turn_heads(*at)
                if exists(t, N):
                    for i in range(CHUNKS - PV_LAG, CHUNKS):
                        pv_step(t, i)

            iterations(pe, N, 2, 1, body)

        @block.scalar
        def _(act):
            def context_out(u, i, bank_):
                nc.scalar.activation(cin[:, u.par, i, :], bank_[:, :], ACT.Copy).then_inc(work_out, 1)

            def project_out(u, i, bank_):
                g, side = HALF_SIDE[i]
                wait(act, split_done, projected(u, i) - 2)
                if i == 0:
                    wait(act, stack_in[u.par], 16 * len(FILLS) * u.k)
                args = {"scale": SCALE if side == 0 else 1.0}
                if not conv:
                    args["bias"] = ((c["bq"], c["bk"])[side])[name][:, g:g + 1]
                for out in (yproj[:, i % 2, :], parts[:, u.par, i, HI, :]):
                    last = nc.scalar.activation(out, bank_[:, :], ACT.Identity, **args)
                last.then_inc(work_out, 1)

            def value_out(u, i, bank_):
                if i == 0:
                    wait(act, att_pv, CHUNKS * (u.u - 1))
                nc.scalar.activation(vals[:, u.par, 2 * i:2 * i + 2, :, 0:D],
                                     bank_[:, 0:2 * H * D].rearrange("p (j h d) -> p j h d", j=2, d=D), ACT.Copy
                                     ).then_inc(work_out, 1)

            def max_rows_out(u, half, bank_):
                if half == 1:
                    act.wait_ge(max_in[0], 16 * (u.u + 1))
                else:
                    wait(act, max_in[1], 16 * u.u)
                nc.scalar.activation(max_rows[:, :], bank_[0:3 * H, 0:P].bitcast(BF16), ACT.Copy).then_inc(work_out, 1)
                act.wait_ge(work_out, work_count(u, "max", half))
                act.dma_start(stack[STACK:STACKED, u.par, side_of((0,)), 2 * half * P:2 * (half + 1) * P], max_rows[:, :]
                              ).then_inc(max_in[half], 16)

            def exp_step(u, i):
                wait(act, att_pv, CHUNKS * u.u + i - 3)
                if phase == 2:
                    wait_apart(act, att_mm, CHUNKS * u.u + i + 1, passed["act"])
                else:
                    act.wait_ge(att_masked, CHUNKS * u.u + i + 1)
                if phase == 2:
                    b = TILES * u.u + ATT[i][0]
                    ins = nc.scalar.activation(probs[:, i % 4, :], tbank[i % 2][:, :], ACT.Exp,
                                               bias=c["pad_bias"][:, bass.ds(b, 1)])
                else:
                    ins = nc.scalar.activation(probs[:, i % 4, :], tbank[i % 2][:, :], ACT.Exp)
                ins.then_inc(att_exp, 1)

            def heads_copy(u, j):
                act.wait_ge(att_pv, CHUNKS * u.u + 4 * j + 4)
                wait(act, turn_mm, TILES * u.u + j - 1)
                nc.scalar.activation(heads_out[:, j % 2, :], pvbank[:, 0:QUADS * P], ACT.Copy
                                     ).then_inc(heads_done, 1)

            def merged_out(u, j):
                act.wait_ge(mt_mm, TILES * u.u + j + 1)
                nc.scalar.activation(merged_t[:, :, :], fbank[:, 0:2 * P].rearrange("p (a s) -> p a s", a=2), ACT.Copy
                                     ).then_inc(mt_out, 1)

            def y_out(u, j, bank_):
                if j == 0:
                    wait(act, stored[u.par], 16 * (2 if conv else 3) * u.k)
                for a in range(W // P):
                    last = nc.scalar.activation(y_t[:, u.par, a * TOK + j * P:a * TOK + (j + 1) * P],
                                                bank_[:, a * P:(a + 1) * P], ACT.Identity,
                                                scale=ln_gc[:, a:a + 1], bias=ln_bc[:, a:a + 1])
                last.then_inc(work_out, 1)

            def body(t):
                for slot in range(16):
                    if exists(t, N):
                        if slot >= PV_LAG + 3 and (slot - PV_LAG - 3) % 4 == 0:
                            heads_copy(t, (slot - PV_LAG - 3) // 4)
                        exp_step(t, slot)
                    if not conv:
                        for at in finish_in(t, slot, "turn_merged"):
                            merged_out(*at)
                    for u, what, step, piece, pieces in banks.in_slot(t, slot):
                        if piece == pieces - 1:
                            bank_ = work[banks.bank(what, step)]
                            act.wait_ge(work_mm, work_count(u, what, step))
                            {"project": project_out, "values": value_out, "context": context_out,
                             "max": max_rows_out, "turn_y": y_out}[what](u, step, bank_)
                if exists(t, N):
                    heads_copy(t, TILES - 1)

            iterations(act, N, 2, 1, body)

        @block.vector
        def _(dve):
            nc.vector.memset(vals[:, :, :, :, D:32], 0.0).then_inc(max_step, 1)
            dve.wait_ge(max_step, 1)
            nc.vector.memset(vals[:, :, :, :, D:D + 1], 1.0).then_inc(const_ready, 1)

            def mid_part(u, i):
                n = HALVES * u.u + i
                dve.wait_ge(rest_step, n + 1)
                nc.vector.tensor_copy(parts[:, u.par, i, MID, :], yproj[:, i % 2, :]).then_inc(mid_done, 1)

            def max_of(u, i):
                j, h0 = SCO[i]
                if phase == 2 and i == 0:
                    dve.wait_ge(pmask_ready, u.u + 1)
                wait(dve, score_max, CHUNKS * u.u + i - 1)
                wait_apart(dve, score_mm, CHUNKS * u.u + i + 1, passed["dve"])
                mask = c["mask0"][:, j % 2, :] if conv else (c["mask1"][:, :] if phase == 1 else pmask[:, u.par, j, :])
                for s in range(SH):
                    cols = slice(s * KEYS, (s + 1) * KEYS)
                    h = h0 + s
                    col = (h % 8) * GROUPS + h // 8
                    ins = nc.vector.tensor_tensor_reduce(
                        out=junk[:, i % 2, cols], in0=sbank[i % 2][:, cols], in1=mask, scale=1.0, scalar=LOWEST,
                        op0=ALU.add, op1=ALU.max, accum_out=maxes[:, j, col:col + 1])
                ins.then_inc(score_max, 1)

            def split_max(u, half):
                steps = 3 * (2 * u.u + half) + 1
                m, rest = maxes[:, 2 * half:2 * half + 2, :], max_rest[:, 2 * half:2 * half + 2, :]
                hi, mid, lo = (max_parts[:, 2 * half:2 * half + 2, part, :] for part in range(3))
                dve.wait_ge(score_max, CHUNKS * u.u + 8 * half + 8)
                if exists(u.plus(-1), N):
                    dve.wait_ge(work_mm, work_count(u.plus(-1), "max", half))
                nc.vector.tensor_scalar(hi, m, -1.0, None, ALU.mult).then_inc(max_step, 1)
                dve.wait_ge(max_step, steps + 1)
                nc.vector.scalar_tensor_tensor(out=rest, in0=m, scalar=-1.0, in1=hi, op0=ALU.mult, op1=ALU.subtract
                                               ).then_inc(max_step, 1)
                dve.wait_ge(max_step, steps + 2)
                nc.vector.tensor_copy(mid, rest).then_inc(max_step, 1)
                dve.wait_ge(max_step, steps + 3)
                nc.vector.tensor_tensor(lo, rest, mid, ALU.subtract).then_inc(max_split, 1)

            def mask_scores(u, i):
                j, q, kt = ATT[i]
                dve.wait_ge(att_mm, CHUNKS * u.u + i + 1)
                if conv:
                    l0 = (j % 2) * P
                    mask = c["mask0t"][:, kt, l0:l0 + P]
                else:
                    mask = c["mask1t"][:, :]
                bank_ = tbank[i % 2][:, :].rearrange("p (s l) -> p s l", s=4)
                nc.vector.tensor_tensor(bank_, bank_, mask.unsqueeze(1).to_broadcast([P, 4, P]), ALU.add
                                        ).then_inc(att_masked, 1)

            def merge(u, j):
                n = TILES * u.u + j
                heads = fbank[:, 0:QUADS * P].rearrange("p (h e) -> p h e", e=32)
                dve.wait_ge(turn_mm, n + 1)
                nc.vector.reciprocal(recips[:, :].unsqueeze(2), heads[:, :, D:D + 1]).then_inc(recip_done, 1)
                dve.wait_ge(recip_done, n + 1)
                nc.vector.tensor_tensor(merged[:, :].rearrange("p (h d) -> p h d", d=D), heads[:, :, 0:D],
                                        recips[:, :].unsqueeze(2).to_broadcast([P, H, D]), ALU.mult
                                        ).then_inc(merged_done, 1)

            def norm(u, j):
                n = TILES * u.u + j
                r = j % 2
                wait(dve, work_mm, turned(u, j, 2))
                wait(dve, scaled, n - 1)
                if conv:
                    dve.wait_ge(merged_done, n + 1)
                    ins = nc.vector.tensor_tensor(z[:, r, :], fbank[:, 2 * P:3 * P], merged[:, :], ALU.add)
                else:
                    dve.wait_ge(out_mm, n + 1)
                    if j == 0:
                        dve.wait_ge(resid_ready, u.u + 1)
                    ins = nc.vector.tensor_tensor(z[:, r, :], fbank[:, 0:W], resid[:, u.par, j * W:(j + 1) * W], ALU.add)
                ins.then_inc(z_done, 1)
                dve.wait_ge(z_done, n + 1)
                nc.vector.bn_stats(stats[:, r, :], z[:, r, :]).then_inc(stats_done, 1)
                wait_apart(dve, stats_done, n + 1, passed["dve"])
                nc.vector.bn_aggr(moments[:, r, :], stats[:, r, :]).then_inc(moments_done, 1)
                dve.wait_ge(moments_done, n + 1)
                nc.vector.tensor_scalar(moments[:, r, 1:2], moments[:, r, 1:2], EPS, None, ALU.add).then_inc(var_done, 1)

            def normalise(u, j):
                n = TILES * u.u + j
                r = j % 2
                dve.wait_ge(rstd_done, n + 1)
                nc.vector.tensor_scalar(z[:, r, :], z[:, r, :], moments[:, r, 0:1], rstd[:, r, 0:1],
                                        ALU.subtract, ALU.mult).then_inc(normed, 1)

            def body(t):
                for slot in range(16):
                    if exists(t, N) and phase != 2:
                        mask_scores(t, slot)
                    for at in splits_in(t, slot):
                        split_max(*at)
                    for at in finish_in(t, slot, "merge"):
                        merge(*at)
                    for at in finish_in(t, slot, "norm"):
                        norm(*at)
                    for at in finish_in(t, slot, "normalise"):
                        normalise(*at)
                    for u, i in scores_in(t, slot):
                        max_of(u, i)
                    if slot - 1 in P_SLOT and exists(t.plus(2), N):
                        mid_part(t.plus(2), P_SLOT.index(slot - 1))

            iterations(dve, N, 2, 1, body)

        @block.gpsimd
        def _(pool):
            def pad_edges(u):
                wait_apart(pool, xin_ld[u.par], 16 * XIN_LOADS * (u.k + 1), passed["pool"])
                for buf in (x_pad, c_pad):
                    ins = nc.gpsimd.tensor_copy(buf[:, u.par, :, 0:L + 2:L + 1], buf[:, u.par, :, 2:L:L - 3])
                ins.then_inc(padded, 1)

            def add_bias(u):
                pool.wait_ge(resid_ld[u.par], 16 * (u.k + 1))
                r = resid[:, u.par, :].rearrange("p (b d) -> p b d", b=TILES)
                nc.gpsimd.tensor_tensor(r, r, bo[:, :].unsqueeze(1).to_broadcast([P, TILES, L]), ALU.add
                                        ).then_inc(resid_ready, 1)

            def scale_pmask(u):
                wait_apart(pool, pmask_ld[u.par], 16 * (u.k + 1), passed["pool"])
                m = pmask[:, u.par, :, :]
                nc.gpsimd.tensor_scalar(m, m, MASKED, None, ALU.mult).then_inc(pmask_ready, 1)

            def first_rest(u, i):
                n = HALVES * u.u + i
                pool.wait_ge(work_out, work_count(u, "project", i))
                rest = yproj[:, i % 2, :]
                nc.gpsimd.tensor_tensor(rest, rest, parts[:, u.par, i, HI, :], ALU.subtract).then_inc(rest_step, 1)

            def low_part(u, i):
                n = HALVES * u.u + i
                rest = yproj[:, i % 2, :]
                pool.wait_ge(mid_done, n + 1)
                nc.gpsimd.tensor_tensor(parts[:, u.par, i, LO, :], rest, parts[:, u.par, i, MID, :], ALU.subtract
                                        ).then_inc(split_done, 1)

            def power(u, j):
                n = TILES * u.u + j
                r = j % 2
                pool.wait_ge(var_done, n + 1)
                nc.gpsimd.tensor_tensor(rstd[:, r, :], moments[:, r, 1:2], c["minus_half"][:, :], ALU.pow
                                        ).then_inc(rstd_done, 1)

            def affine(u, j):
                n = TILES * u.u + j
                row = y[:, u.par, j, :]
                if j == 0:
                    wait(pool, stored[u.par], 16 * (2 if conv else 3) * u.k)
                pool.wait_ge(normed, n + 1)
                nc.gpsimd.tensor_tensor(row, z[:, j % 2, :], ln_g[:, 0:W], ALU.mult).then_inc(scaled, 1)
                pool.wait_ge(scaled, n + 1)
                nc.gpsimd.tensor_tensor(row, row, ln_b[:, 0:W], ALU.add).then_inc(y_done, 1)

            def body(t):
                if not conv and exists(t, N):
                    add_bias(t)
                for slot in range(16):
                    for at in finish_in(t, slot, "norm"):
                        power(*at)
                    if slot in P_SLOT and exists(t.plus(2), N):
                        first_rest(t.plus(2), P_SLOT.index(slot))
                    if slot - 1 in P_SLOT and exists(t.plus(2), N):
                        low_part(t.plus(2), P_SLOT.index(slot - 1))
                    for at in finish_in(t, slot, "normalise"):
                        affine(*at)
                    if slot == 15 and phase == 2 and exists(t.plus(2), N):
                        scale_pmask(t.plus(2))
                    if slot == 15 and conv and exists(t.plus(3), N):
                        pad_edges(t.plus(3))

            for p in range(2):
                nc.gpsimd.memset(stack[STACK:STACKED, p, side_of((1,)), :], 1.0).then_inc(ones_ready, 1)
                pool.wait_ge(ones_ready, p + 1)
            iterations(pool, N, 3, 1, body)

        running.close()
        reset(nc, sems)


def feed_forward(nc, top, c, io):
    NB, _, L = io["x"].shape
    F = io["ffn_w1"].shape[1]
    FT = F // P
    N = NB // TILES
    EPS = 1e-6
    with ExitStack() as ctx:
        def sb(n, shape, dt=F32):
            return ctx.enter_context(nc.sbuf_tensor(f"ffn_{n}", shape, dt))

        def sem(n):
            return ctx.enter_context(nc.semaphore(f"ffn_{n}"))

        w1, w2 = sb("w1", [P, 2, F]), sb("w2", [P, FT, L])
        xin = sb("xin", [P, 2, 2, TOK])
        resid = sb("resid", [P, 2, TILES, L])
        hidden = sb("hidden", [P, 2, FT, TOK])
        z = sb("z", [P, 2, L])
        stats, moments, rstd = sb("stats", [P, 2, 6]), sb("moments", [P, 2, 2]), sb("rstd", [P, 2, 1])
        y = sb("y", [P, 2, TILES, L])
        hbank = [ctx.enter_context(nc.psum_tensor(f"ffn_h{i}", [P, 512], F32)) for i in range(4)]
        obank = [ctx.enter_context(nc.psum_tensor(f"ffn_o{i}", [P, 512], F32)) for i in range(4)]
        weights = sem("weights")
        xin_ld = [sem(f"xin_ld{i}") for i in range(2)]
        resid_ld = [sem(f"resid_ld{i}") for i in range(2)]
        resid_ready = sem("resid_ready")
        h_mm, h_out = sem("h_mm"), sem("h_out")
        o_mm = sem("o_mm")
        z_done, stats_done, moments_done, var_done, rstd_done = (
            sem("z_done"), sem("stats_done"), sem("moments_done"), sem("var_done"), sem("rstd_done"))
        normed, scaled, y_done = sem("normed"), sem("scaled"), sem("y_done")
        passed, passed_sp = sem("passed_dve"), sem("passed_sp")
        stored = [sem(f"stored{i}") for i in range(2)]
        xt_units = io["o2t"].rearrange("(u b) k p s -> u p k b s", b=TILES)
        res_units = io["o2"].rearrange("(u b) s d -> u s b d", b=TILES)
        out_units = io["out"].rearrange("(u b) s d -> u s b d", b=TILES)
        block = ctx.enter_context(nc.Block())

        @block.sync
        def _(sp):
            sp.dma_start(w1[:, :, :], io["ffn_w1"].rearrange("(k p) n -> p k n", p=P)).then_inc(weights, 16)
            sp.dma_start(w2[:, :, :], io["ffn_w2"].rearrange("(k p) n -> p k n", p=P)).then_inc(weights, 16)

            def body(t):
                u = t.plus(1)
                if exists(u, N):
                    wait_sp(sp, h_mm, FT * (u.u - 1), passed_sp)
                    for kt in range(2):
                        sp.dma_start(xin[:, u.par, kt, :].rearrange("p (b s) -> p b s", b=TILES),
                                     xt_units[u.u][:, kt]).then_inc(xin_ld[u.par], 16)
                    wait_sp(sp, z_done, TILES * (u.u - 1), passed_sp)
                    sp.dma_start(resid[:, u.par, :, :], res_units[u.u]).then_inc(resid_ld[u.par], 16)
                if exists(t, N):
                    wait_sp(sp, y_done, TILES * (t.u + 1), passed_sp)
                    sp.dma_start(out_units[t.u], y[:, t.par, :, :]).then_inc(stored[t.par], 16)

            iterations(sp, N, 1, 0, body)
            for p in range(2):
                sp.wait_ge(stored[p], 16 * (N // 2))

        @block.tensor
        def _(pe):
            pe.wait_ge(weights, 32)

            def body(t):
                pe.wait_ge(xin_ld[t.par], 32 * (t.k + 1))
                for f in range(FT):
                    wait(pe, h_out, FT * t.u + f - 3)
                    for kt in range(2):
                        mm = nc.tensor.matmul(hbank[f % 4][:, :], w1[:, kt, f * P:(f + 1) * P], xin[:, t.par, kt, :],
                                              start=(kt == 0), stop=(kt == 1))
                    mm.then_inc(h_mm, 1)
                for j in range(TILES):
                    wait(pe, z_done, TILES * (t.u - 1) + j + 1 if t.number() != 0 else 0)
                    if j == 0:
                        pe.wait_ge(h_out, FT * (t.u + 1))
                    for f in range(FT):
                        mm = nc.tensor.matmul(obank[j][:, 0:L], hidden[:, t.par, f, j * P:(j + 1) * P], w2[:, f, :],
                                              start=(f == 0), stop=(f == FT - 1))
                    mm.then_inc(o_mm, 1)

            iterations(pe, N, 0, 0, body)

        @block.scalar
        def _(act):
            def body(t):
                wait(act, o_mm, TILES * (t.u - 1))
                for f in range(FT):
                    act.wait_ge(h_mm, FT * t.u + f + 1)
                    nc.scalar.activation(hidden[:, t.par, f, :], hbank[f % 4][:, :], ACT.Relu,
                                         bias=c["ffn_b1_s"][:, f:f + 1]).then_inc(h_out, 1)

            iterations(act, N, 0, 0, body)

        @block.vector
        def _(dve):
            def body(t):
                dve.wait_ge(resid_ready, t.u + 1)
                for j in range(TILES):
                    n = TILES * t.u + j
                    r = j % 2
                    wait(dve, scaled, n - 1)
                    dve.wait_ge(o_mm, n + 1)
                    nc.vector.tensor_tensor(z[:, r, :], obank[j][:, 0:L], resid[:, t.par, j, :], ALU.add).then_inc(z_done, 1)
                    dve.wait_ge(z_done, n + 1)
                    nc.vector.bn_stats(stats[:, r, :], z[:, r, :]).then_inc(stats_done, 1)
                    wait_apart(dve, stats_done, n + 1, passed)
                    nc.vector.bn_aggr(moments[:, r, :], stats[:, r, :]).then_inc(moments_done, 1)
                    dve.wait_ge(moments_done, n + 1)
                    nc.vector.tensor_scalar(moments[:, r, 1:2], moments[:, r, 1:2], EPS, None, ALU.add
                                            ).then_inc(var_done, 1)
                    dve.wait_ge(rstd_done, n + 1)
                    nc.vector.tensor_scalar(z[:, r, :], z[:, r, :], moments[:, r, 0:1], rstd[:, r, 0:1],
                                            ALU.subtract, ALU.mult).then_inc(normed, 1)

            iterations(dve, N, 0, 0, body)

        @block.gpsimd
        def _(pool):
            def body(t):
                pool.wait_ge(resid_ld[t.par], 16 * (t.k + 1))
                nc.gpsimd.tensor_tensor(resid[:, t.par, :, :], resid[:, t.par, :, :],
                                        c["ffn_b2"][:, :].unsqueeze(1).to_broadcast([P, TILES, L]), ALU.add
                                        ).then_inc(resid_ready, 1)
                for j in range(TILES):
                    n = TILES * t.u + j
                    r = j % 2
                    row = y[:, t.par, j, :]
                    pool.wait_ge(var_done, n + 1)
                    nc.gpsimd.tensor_tensor(rstd[:, r, :], moments[:, r, 1:2], c["minus_half"][:, :], ALU.pow
                                            ).then_inc(rstd_done, 1)
                    if j == 0:
                        wait(pool, stored[t.par], 16 * t.k)
                    pool.wait_ge(normed, n + 1)
                    nc.gpsimd.tensor_tensor(row, z[:, r, :], c["ln3_g"][:, :], ALU.mult).then_inc(scaled, 1)
                    pool.wait_ge(scaled, n + 1)
                    nc.gpsimd.tensor_tensor(row, row, c["ln3_b"][:, :], ALU.add).then_inc(y_done, 1)

            iterations(pool, N, 0, 0, body)


def build(nc, io):
    with ExitStack() as top:
        c = {}
        with ExitStack() as l0:
            constants(nc, top, l0, io, c)
            attention(nc, top, c, io, 0)
        attention(nc, top, c, io, 1)
        attention(nc, top, c, io, 2)
        feed_forward(nc, top, c, io)


def _laid_out(inputs):
    import numpy as np

    a = {k: np.asarray(v) for k, v in inputs.items()}
    out = {"x": a["x"], "ctx": a["ctx_1024"], "mask0": a["L0_xattn_mask"], "mask1": a["mask_1x1xSxS2_fk1"],
           "mask2": a["mask_Bx1x1xS2_fk0"], "gamma": a["L0_xattn_gamma"], "beta": a["L0_xattn_beta"]}
    for n in "qkv":
        out[f"conv_{n}"] = a[f"L0_xattn_w{n}"].reshape(8, 16, 16, 3).transpose(0, 2, 3, 1)
    for m in ("mha1", "mha2"):
        for n in "qk":
            out[f"{m}_w{n}"] = a[f"L1_xattn_{m}_w{n}"].reshape(256, 2, 8, 16).transpose(0, 1, 3, 2).reshape(256, 256)
            out[f"{m}_b{n}"] = a[f"L1_xattn_{m}_b{n}"].reshape(2, 8, 16).transpose(2, 1, 0).reshape(128, 2)
        out[f"{m}_wv"], out[f"{m}_wo"] = a[f"L1_xattn_{m}_wv"], a[f"L1_xattn_{m}_wo"]
        out[f"{m}_bv"] = a[f"L1_xattn_{m}_bv"].reshape(2, 128).T
        out[f"{m}_bo"] = a[f"L1_xattn_{m}_bo"]
    out["ffn_w1"], out["ffn_w2"], out["ffn_b2"] = (a[f"L1_xattn_ffn_{n}"] for n in ("w1", "w2", "b2"))
    out["ffn_b1"] = a["L1_xattn_ffn_b1"].reshape(8, 128).T
    for i in (1, 2, 3):
        for n in "gb":
            out[f"ln{i}_{n}"] = a[f"L1_xattn_ln{i}_{n}"]
    for i in (1, 2):
        for n in "gb":
            out[f"ln{i}_{n}c"] = out[f"ln{i}_{n}"].reshape(2, 128).T
    out["g0_col"], out["b0_col"] = out["gamma"].reshape(128, 1), out["beta"].reshape(128, 1)
    return {k: np.ascontiguousarray(v) for k, v in out.items()}


def kernel(**inputs):
    import concourse.bacc as bacc
    from concourse.bass_utils import run_bass_kernel_spmd

    nc = bacc.Bacc("TRN2", target_bir_lowering=False, num_devices=1)
    arrays, io = {}, {}
    for name, a in _laid_out(inputs).items():
        arrays[f"in_{name}"] = a
        io[name] = nc.dram_tensor(f"in_{name}", a.shape, mybir.dt.from_np(a.dtype), kind="ExternalInput").ap()
    NB, S, L = arrays["in_x"].shape
    for name in ("x1", "o1", "o2"):
        io[name] = nc.dram_tensor(f"rows_{name}", (NB, S, L), F32, kind="Internal").ap()
        io[f"{name}t"] = nc.dram_tensor(f"cols_{name}", (NB, 2, P, S), F32, kind="Internal").ap()
    io["out"] = nc.dram_tensor("out_0", (NB, S, L), F32, kind="ExternalOutput").ap()
    build(nc, io)
    r = run_bass_kernel_spmd(nc, [arrays], core_ids=[0])
    return r.results[0]["out_0"]
```

```python
from contextlib import ExitStack

import concourse.bass as bass
from concourse import mybir

F32 = mybir.dt.float32
BF16 = mybir.dt.bfloat16
F32R = mybir.dt.float32r
ALU = mybir.AluOpType
ACT = mybir.ActivationFunctionType

P = 128
D = 16
TILES = 4
TOK = TILES * P
CHUNKS = 16
HI, MID, LO = range(3)
SLOTS = [(HI, HI), (HI, MID), (HI, LO), (MID, HI), (MID, MID), (LO, HI)]
STACK = len(SLOTS) * D
STACKED = STACK + 3
PRODUCTS = ((0, 0), (0, 1), (1, 0))
MASKED = -1.0e9
LOWEST = -3.0e38
PLANS = (
    dict(
        score=[5, 5, 7, 7, 9, 9, 10, 10, 12, 12, 13, 14, 14, 15, 16, 17],
        pv_lag=2,
        steps={"turn": 6, "normalise": 10},
        dve_steps={"recip": (7, 0),
                   "merge": (7, 1),
                   "add": (7, 1),
                   "stats": (8, 0),
                   "moments": (8, 2),
                   "epsilon": (9, 0)},
        pe_masks=(1, 4, 6, 9, 12, 13),
        work=[((0,), "values", 1, 0), ((0, 1), "values", 1, 1), ((3,), "turn_y", -1, 2), ((4,), "max", 0, 1),
              ((7,), "turn_y", -1, 3), ((7, 8), "project", 2, 0), ((9, 10), "project", 2, 1),
              ((11,), "turn_y", 0, 0), ((12,), "max", 1, 0), ((15,), "turn_y", 0, 1)],
        split_slot=15,
    ),
    dict(
        score=[4, 5, 6, 7, 8, 9, 9, 10, 11, 12, 12, 13, 14, 15, 15, 16],
        pv_lag=2,
        steps={"turn": 6, "turn_merged": 7, "output": 8, "normalise": 10},
        dve_steps={"recip": (6, 1),
                   "merge": (7, 0),
                   "add": (8, 2),
                   "stats": (9, 0),
                   "moments": (9, 1),
                   "epsilon": (9, 2)},
        work=[((0,), "turn_y", -1, 1), ((1,), "values", 1, 0), ((2, 3), "project", 2, 0),
              ((3,), "values", 1, 1), ((5,), "max", 0, 1), ((5,), "turn_y", -1, 2), ((7,), "project", 2, 1),
              ((9,), "project", 2, 2), ((9,), "turn_y", -1, 3), ((11,), "project", 2, 3), ((13,), "max", 1, 0),
              ((13,), "turn_y", 0, 0)],
        pe_masks=(),
        split_slot=15,
    ),
    dict(
        score=[4, 4, 5, 6, 8, 8, 9, 10, 11, 12, 13, 15, 15, 16, 17, 17],
        pv_lag=2,
        steps={"turn": 6, "turn_merged": 7, "output": 8, "normalise": 9},
        dve_steps={"recip": (5, 2),
                   "merge": (5, 2),
                   "add": (8, 2),
                   "stats": (8, 2),
                   "moments": (9, 1),
                   "epsilon": (9, 1)},
        work=[((0,), "values", 1, 0), ((2,), "context", 2, 0), ((3,), "values", 1, 1), ((4,), "turn_y", -1, 2),
              ((5,), "max", 0, 1), ((5,), "project", 2, 0), ((6,), "context", 2, 1), ((7,), "project", 2, 1),
              ((8,), "turn_y", -1, 3), ((9,), "project", 2, 2), ((11,), "project", 2, 3),
              ((12,), "turn_y", 0, 0), ((13,), "max", 1, 0), ((15,), "turn_y", 0, 1)],
        pe_masks=(),
    ),
)


class Unit:

    def __init__(self, k, par):
        self.k, self.par = k, par
        self.u = 2 * k + par

    def plus(self, n):
        at = self.par + n
        return Unit(self.k + at // 2, at % 2)

    def number(self):
        return self.u if isinstance(self.u, int) else None


def wait_sp(sp, sem, value, passed):
    if isinstance(value, int):
        wait(sp, sem, value)
    else:
        wait_apart(sp, sem, value, passed)


def wait(eng, sem, value):
    if isinstance(value, int) and value <= 0:
        return
    eng.wait_ge(sem, value)


def wait_apart(eng, sem, value, passed):
    eng.wait_ge(sem, value).then_inc(passed, 1)


def iterations(eng, n, before, after, body):
    assert n % 2 == 0
    first = 1
    last = max(n // 2 - (before + 1) // 2, first)
    for t in range(-before, 2 * first):
        body(Unit(t // 2, t % 2))
    if last > first:
        with eng.Fori(first, last) as k:
            body(Unit(k, 0))
            body(Unit(k, 1))
    for t in range(2 * last, n + after):
        body(Unit(t // 2, t % 2))


class WorkBanks:

    def __init__(self, uses, n):
        self.uses, self.n = uses, n
        self.at = {(what, step): (i, off) for i, (_, what, off, step) in enumerate(uses)}
        assert len(uses) % 2 == 0
        assert [u[0][-1] for u in uses] == sorted(u[0][-1] for u in uses)

    def bank(self, what, step):
        return self.at[what, step][0] % 2

    def before(self, t, place):
        if t.number() is None:
            return len(self.uses) * t.u + place + self.before(Unit(1, 0), 0) - 2 * len(self.uses)
        return sum(0 <= i + off < self.n for i in range(-3, t.u + 1)
                   for p, (_, _, off, _) in enumerate(self.uses) if i < t.u or p < place)

    def number(self, u, what, step):
        place, off = self.at[what, step]
        return self.before(u.plus(-off), place)

    def free(self, u, what, step):
        place, off = self.at[what, step]
        t, place = u.plus(-off), place - 2
        while t.number() is None or t.number() >= -3:
            if place < 0:
                t, place = t.plus(-1), place + len(self.uses)
            elif exists(t.plus(self.uses[place][2]), self.n):
                return self.before(t, place) + 1
            else:
                place -= 2
        return 0

    def in_slot(self, t, slot):
        return [(t.plus(off), what, step, slots.index(slot), len(slots))
                for slots, what, off, step in self.uses if slot in slots and exists(t.plus(off), self.n)]


def exists(unit, n):
    at = unit.number()
    return at is None or 0 <= at < n


def reset(nc, sems):
    with nc.Block() as block:
        @block.gpsimd
        def _(pool):
            for s in sems:
                pool.sem_clear(s)


def constants(nc, top, l0, io, c):
    def sb(name, shape, dt=F32):
        c[name] = top.enter_context(nc.sbuf_tensor(name, shape, dt))
        return c[name]

    def sb_l0(name, shape, dt=F32):
        c[name] = l0.enter_context(nc.sbuf_tensor(name, shape, dt))
        return c[name]

    L = io["x"].shape[2]
    LT = L // P
    NB = io["x"].shape[0]
    F = io["ffn_w1"].shape[1]

    ident = sb("ident", [P, P])
    identb = sb("identb", [P, P], BF16)
    mask1 = sb("mask1", [P, P])
    mask1t = sb("mask1t", [P, P])
    pad_bias = sb("pad_bias", [P, NB])
    rows = {n: sb(n, [P, L]) for n in ("ln1_g", "ln1_b", "ln2_g", "ln2_b", "ln3_g", "ln3_b",
                                       "mha1_bo", "mha2_bo", "ffn_b2")}
    bq = {m: sb(f"{m}_bq_s", [P, 2]) for m in ("mha1", "mha2")}
    bk = {m: sb(f"{m}_bk_s", [P, 2]) for m in ("mha1", "mha2")}
    bv = {m: sb(f"{m}_bv_s", [P, 2]) for m in ("mha1", "mha2")}
    c["bq"], c["bk"], c["bv"] = bq, bk, bv
    b1 = sb("ffn_b1_s", [P, F // P])
    cols = {n: sb(n, [P, 2]) for n in ("ln1_gc", "ln1_bc", "ln2_gc", "ln2_bc")}
    minus_half = sb("minus_half", [P, 1])
    c["weights"] = {m: {n: sb(f"{m}_{n}", [P, 2, L]) for n in ("wq", "wk", "wv", "wo")} for m in ("mha1", "mha2")}
    c["weights_in"] = top.enter_context(nc.semaphore("weights_in"))
    conv = {n: sb_l0(f"conv_{n}", [P, 3, P]) for n in "qkv"}
    c["conv"] = conv
    mask0 = sb_l0("mask0", [P, LT, L])
    mask0t = sb_l0("mask0t", [P, LT, L])
    mask0t_parts = sb_l0("mask0t_parts", [P, 2, LT, L], F32R)
    ident_r = sb_l0("ident_r", [P, P], F32R)
    g0, b0 = sb_l0("g0", [P, P]), sb_l0("b0", [P, P])
    cols.update({n: sb_l0(n, [P, 1]) for n in ("g0_col", "b0_col")})

    with ExitStack() as ctx:
        taps = {n: ctx.enter_context(nc.sbuf_tensor(f"taps_{n}", [P, 3, D], F32)) for n in "qkv"}
        group_of = ctx.enter_context(nc.sbuf_tensor("group_of", [P, P // D], F32))
        pad = ctx.enter_context(nc.sbuf_tensor("pad_rows", [P, P], F32))
        wo = {m: ctx.enter_context(nc.sbuf_tensor(f"setup_wo_{m}", [P, 2, L], F32)) for m in ("mha1", "mha2")}
        bvw = ctx.enter_context(nc.sbuf_tensor("bv_wide", [P, 4, P], F32))
        ps = [ctx.enter_context(nc.psum_tensor(f"setup_ps{i}", [P, 512], F32)) for i in range(8)]
        grouped = top.enter_context(nc.semaphore("grouped"))
        zeroed = top.enter_context(nc.semaphore("zeroed"))
        ident_zero = top.enter_context(nc.semaphore("ident_zero"))
        ident_ready = top.enter_context(nc.semaphore("ident_ready"))
        loaded = top.enter_context(nc.semaphore("consts_loaded"))
        scaled = top.enter_context(nc.semaphore("masks_scaled"))
        turned = top.enter_context(nc.semaphore("masks_turned"))
        widened = top.enter_context(nc.semaphore("bv_widened"))
        bvwo = top.enter_context(nc.semaphore("bv_times_wo"))
        parted = top.enter_context(nc.semaphore("mask_parts"))
        done = top.enter_context(nc.semaphore("consts_done"))
        block = ctx.enter_context(nc.Block())

        loads = [(taps[n][:, :, :], io[f"conv_{n}"].rearrange("g i t o -> (g i) t o")) for n in "qkv"]
        loads += [(mask0[:, t, :], io["mask0"][t * P:(t + 1) * P, :]) for t in range(LT)]
        loads += [(mask1[:, :], io["mask1"][0, 0]), (pad[0:NB, :], io["mask2"][:, 0, 0, :])]
        loads += [(g0[:, :], io["gamma"].partition_broadcast(P)), (b0[:, :], io["beta"].partition_broadcast(P))]
        loads += [(t[:, :], io[n].partition_broadcast(P)) for n, t in rows.items()]
        loads += [(t[:, :], io[f"{m}_{n}"]) for n, ts in (("bq", bq), ("bk", bk), ("bv", bv)) for m, t in ts.items()]
        loads += [(b1[:, :], io["ffn_b1"])] + [(t[:, :], io[n]) for n, t in cols.items()]
        loads += [(wo[m][:, :, :], io[f"{m}_wo"].rearrange("(k p) n -> p k n", p=P)) for m in wo]

        @block.gpsimd
        def _(pool):
            nc.gpsimd.memset(pad[:], 0.0).then_inc(zeroed, 1)
            nc.gpsimd.memset(minus_half[:, :], -0.5)
            nc.gpsimd.memset(ident[:, :], 0.0).then_inc(ident_zero, 1)
            nc.gpsimd.memset(identb[:, :], 0.0).then_inc(ident_zero, 1)
            pool.wait_ge(ident_zero, 2)
            for t in (ident, identb):
                nc.gpsimd.affine_select(out=t[:, :], in_=t[:, :], compare_op=ALU.not_equal, fill=1.0, base=0,
                                        pattern=[[-1, P]], channel_multiplier=1).then_inc(ident_ready, 1)

        @block.sync
        def _(sp):
            sp.wait_ge(zeroed, 1)
            for out, in_ in loads:
                sp.dma_start(out, in_).then_inc(loaded, 16)

        @block.vector
        def _(dve):
            dve.wait_ge(loaded, 16 * len(loads))
            for t in (mask0, mask1, pad):
                nc.vector.tensor_scalar(t[:], t[:], MASKED, None, ALU.mult).then_inc(scaled, 1)
            dve.wait_ge(ident_ready, 2)
            nc.vector.tensor_reduce(group_of[:, :], ident[:, :].rearrange("p (g o) -> p g o", o=D),
                                    op=ALU.add, axis=mybir.AxisListType.X).then_inc(grouped, 1)
            dve.wait_ge(grouped, 1)
            for n in "qkv":
                for tap in range(3):
                    out = conv[n][:, tap, :].rearrange("p (g o) -> p g o" if n == "v" else "p (o g) -> p g o", o=D)
                    nc.vector.tensor_tensor(out, taps[n][:, tap, :].unsqueeze(1).to_broadcast([P, P // D, D]),
                                            group_of[:, :].unsqueeze(2).to_broadcast([P, P // D, D]), ALU.mult)
            for m in bq:
                nc.vector.tensor_scalar(bq[m][:, :], bq[m][:, :], float(D) ** -0.5, None, ALU.mult)
            nc.vector.memset(bvw[:], 1.0).then_inc(widened, 1)
            dve.wait_ge(widened, 1)
            for i, m in enumerate(("mha1", "mha2")):
                for kt in range(2):
                    nc.vector.tensor_scalar(bvw[:, 2 * i + kt, :], bvw[:, 2 * i + kt, :], bv[m][:, kt:kt + 1],
                                            None, ALU.mult).then_inc(widened, 1)
            dve.wait_ge(bvwo, 2)
            for i, m in enumerate(("mha1", "mha2")):
                nc.vector.tensor_tensor(rows[f"{m}_bo"][:, :], rows[f"{m}_bo"][:, :], ps[i][:, 0:L], ALU.add)
            dve.wait_ge(turned, 3)
            for a in range(LT):
                nc.vector.tensor_copy(mask0t[:, a, :], ps[2 + a][:, 0:L]).then_inc(parted, 1)
            nc.vector.tensor_copy(ident_r[:, :], ident[:, :])
            dve.wait_ge(parted, LT)
            nc.vector.tensor_copy(mask0t_parts[:, 0, :, :], mask0t[:, :, :]).then_inc(parted, 1)
            dve.wait_ge(parted, LT + 1)
            nc.vector.tensor_tensor(mask0t_parts[:, 1, :, :], mask0t[:, :, :], mask0t_parts[:, 0, :, :], ALU.subtract)
            nc.vector.tensor_copy(mask1t[:, :], ps[4][:, 0:P])
            nc.vector.tensor_copy(pad_bias[:, 0:NB], ps[5][:, 0:NB]).then_inc(done, 1)

        @block.tensor
        def _(pe):
            pe.wait_ge(widened, 5)
            for i, m in enumerate(("mha1", "mha2")):
                for kt in range(2):
                    mm = nc.tensor.matmul(ps[i][:, 0:L], bvw[:, 2 * i + kt, :], wo[m][:, kt, :],
                                          start=(kt == 0), stop=(kt == 1))
                mm.then_inc(bvwo, 1)
            pe.wait_ge(ident_ready, 2)
            pe.wait_ge(scaled, 3)
            for a in range(LT):
                for b in range(LT):
                    mm = nc.tensor.transpose(ps[2 + a][:, b * P:(b + 1) * P], mask0[:, b, a * P:(a + 1) * P], ident[:, :])
            mm.then_inc(turned, 1)
            nc.tensor.transpose(ps[4][:, 0:P], mask1[:, :], ident[:, :]).then_inc(turned, 1)
            nc.tensor.transpose(ps[5][:, 0:P], pad[:, :], ident[:, :]).then_inc(turned, 1)

        @block.scalar
        def _(act):
            act.wait_ge(done, 1)


def attention(nc, top, c, io, phase):
    conv = phase == 0
    name = ("l0", "mha1", "mha2")[phase]
    H = 8 if conv else 16
    QUADS = H // 4
    KT = 2 if conv else 1
    BU = TILES // KT
    N = io["x"].shape[0] // BU
    GROUPS = H // 8
    HALVES = 2 * GROUPS
    VSTEPS = 2
    W = P if conv else 2 * P
    SCALE = 8.0 ** -0.5 if conv else float(D) ** -0.5
    EPS = 1e-5 if conv else 1e-6
    L = io["x"].shape[2]
    KEYS = KT * P
    SH = 512 // KEYS

    with ExitStack() as ctx:
        def sb(n, shape, dt=F32):
            return ctx.enter_context(nc.sbuf_tensor(f"{name}_{n}", shape, dt))

        sems = []

        def sem(n):
            sems.append(ctx.enter_context(nc.semaphore(f"{name}_{n}")))
            return sems[-1]

        if conv:
            x_pad = sb("x_pad", [P, 2, BU, L + 2])
            c_pad = sb("c_pad", [P, 2, BU, L + 2])
        else:
            xin = sb("xin", [P, 2, 2, TOK])
        if phase == 2:
            craw = sb("craw", [P, 2, TILES, L])
            cin = sb("cin", [P, 2, 2, TOK])
            pmask = sb("pmask", [P, 2, TILES, P])
        if phase == 0:
            x_parts = [sb(f"{n}_parts", [P, 2, 2, BU, L + 2], F32R) for n in ("x", "c")]
        elif phase == 1:
            x_rounded = sb("x_rounded", [P, 2, 2, TOK], F32R)
        if not conv:
            wq, wk, wv, wo = (c["weights"][name][n] for n in ("wq", "wk", "wv", "wo"))
        w_split = [] if phase == 2 else [(w, sb(f"w{n}_parts", [P, 2, w.shape[1], w.shape[2]], F32R))
                                         for n, w in enumerate([c["conv"]["q"], c["conv"]["k"]] if conv else [wq, wk, wv])]
        raw = [x_pad, c_pad] if conv else [xin]

        def x_part(n, par, part):
            if conv:
                return x_parts[n][:, par, part, :, :]
            return xin[:, par, :, :].bitcast(F32R) if part else x_rounded[:, par, :, :]

        resid = sb("resid", [P, 2, TILES * W])
        yproj = sb("yproj", [P, 2, TOK])
        parts = sb("parts", [P, 2, HALVES, 3, TOK], BF16)
        stack = sb("stack", [P, 2, 2 * H, TOK], BF16)
        vals = sb("vals", [P, 2, TILES, H, 32])
        junk = sb("junk", [P, 2, 512], BF16)
        maxes = sb("maxes", [P, TILES, H])
        max_rest = sb("max_rest", [P, TILES, H])
        max_parts = sb("max_parts", [P, TILES, 3, H], BF16)
        max_rows = sb("max_rows", [3 * H, 2 * P], BF16)
        probs = sb("probs", [P, 4, 512])
        heads_out = sb("heads_out", [P, 2, QUADS * P])
        recips = sb("recips", [P, H])
        merged = sb("merged", [P, H * D])
        merged_t = sb("merged_t", [P, 2, P])
        z = sb("z", [P, 2, W])
        stats = sb("stats", [P, 2, 6])
        moments = sb("moments", [P, 2, 2])
        rstd = sb("rstd", [P, 2, 1])
        shift = sb("shift", [P, 2, 1])
        y = sb("y", [P, 2, TILES, W])
        y_t = sb("y_t", [P, 2, TILES * W])

        bank = [ctx.enter_context(nc.psum_tensor(f"{name}_bank{i}", [P, 512], F32)) for i in range(8)]
        work, sbank, tbank, pvbank, fbank = bank[0:2], bank[2:4], bank[4:6], bank[6], bank[7]

        const_ready, ones_ready = sem("const_ready"), sem("ones_ready")
        passed = {e: sem(f"passed_{e}") for e in ("pe", "act", "dve", "pool", "sp")}
        xin_ld = [sem(f"xin_ld{i}") for i in range(2)]
        resid_ld = [sem(f"resid_ld{i}") for i in range(2)]
        pmask_ld = [sem(f"pmask_ld{i}") for i in range(2)]
        padded = sem("padded")
        pmask_ready = sem("pmask_ready")
        resid_ready = sem("resid_ready")
        w_hi, w_lo = sem("w_hi"), sem("w_lo")
        x_hi, x_lo = sem("x_hi"), sem("x_lo")
        work_mm, work_out = sem("work_mm"), sem("work_out")
        mid_done = sem("mid_done")
        rest_step, split_done = sem("rest_step"), sem("split_done")
        stack_in = [[sem(f"stack_in{p}{half}") for half in range(2)] for p in range(2)]
        score_mm, score_max = sem("score_mm"), sem("score_max")
        max_step, max_split = sem("max_step"), sem("max_split")
        max_in = [sem(f"max_in{i}") for i in range(2)]
        att_mm, att_masked, att_exp, att_pv = sem("att_mm"), sem("att_masked"), sem("att_exp"), sem("att_pv")
        heads_done = sem("heads_done")
        turn_mm, recip_done, merged_done = sem("turn_mm"), sem("recip_done"), sem("merged_done")
        mt_mm, mt_out = sem("mt_mm"), sem("mt_out")
        out_mm = sem("out_mm")
        z_done, stats_done, moments_done, var_done, rstd_done = (
            sem("z_done"), sem("stats_done"), sem("moments_done"), sem("var_done"), sem("rstd_done"))
        normed, scaled, y_done = sem("normed"), sem("scaled"), sem("y_done")
        stored = [sem(f"stored{i}") for i in range(2)]

        if conv:
            x_units = io["x"].rearrange("(u b) c l -> u c b l", b=BU)
            c_units = io["ctx"].rearrange("(u b) c l -> u c b l", b=BU)
            out_rows = io["x1"].rearrange("(u b) s d -> u s b d", b=BU)
            out_cols = io["x1t"].rearrange("(u b) k p s -> u p (b k) s", b=BU)
            res_units = x_units
            bo = None
            ln_g, ln_b, ln_gc, ln_bc = c["g0"], c["b0"], c["g0_col"], c["b0_col"]
        else:
            src_t, src, dst, dst_t = (("x1t", "x1", "o1", "o1t"), ("o1t", "o1", "o2", "o2t"))[phase - 1]
            xt_units = io[src_t].rearrange("(u b) k p s -> u p k b s", b=BU)
            res_units = io[src].rearrange("(u b) s d -> u s b d", b=BU)
            c_units = io["ctx"].rearrange("(u b) s d -> u s b d", b=BU)
            out_rows = io[dst].rearrange("(u b) s d -> u s b d", b=BU)
            out_cols = io[dst_t].rearrange("(u b) k p s -> u p k b s", b=BU)
            bo = c[f"{name}_bo"]
            ln_g, ln_b, ln_gc, ln_bc = (c[f"ln{phase}_{n}"] for n in ("g", "b", "gc", "bc"))
        mask2_units = io["mask2"].rearrange("(u b) i j m -> u (b i j m)", b=TILES) if phase == 2 else None
        XIN_LOADS = 2 if conv else (2 if phase == 1 else 3)
        HALF_SIDE = [(g, side) for side in range(2) for g in range(GROUPS)]
        FILLS = [(s, pair[0], (0, 1)) for s, pair in enumerate(SLOTS) if conv and pair[0] == pair[1]]
        FILLS += [(s, pair[side], (side,)) for s, pair in enumerate(SLOTS) for side in range(2)
                  if not (conv and pair[0] == pair[1])]

        def place(side, h):
            return 2 * h + side if conv else H * side + 2 * (h % 8) + h // 8

        def side_of(sides):
            if len(sides) == 2:
                return slice(0, 2 * H)
            return slice(sides[0], 2 * H, 2) if conv else slice(H * sides[0], H * sides[0] + H)

        def att_chunks():
            return [(j, q, kt) for j in range(TILES) for q in range(QUADS) for kt in range(KT)]

        ATT = att_chunks()
        SCO = [(j, h) for j in range(TILES) for h in range(0, H, SH)]
        assert len(ATT) == len(SCO) == CHUNKS
        plan = PLANS[phase]
        SCORE_SLOT, PV_LAG = plan["score"], plan["pv_lag"]
        SPLIT_SLOT = plan.get("split_slot")
        DVE_MASKS = [i for i in range(CHUNKS) if phase != 2 and i not in plan["pe_masks"]]
        banks = WorkBanks(plan["work"], N)
        P_SLOT = [slots[-1] for slots, what, _, _ in plan["work"] if what == "project"]

        def scores_in(t, slot):
            return [(t.plus(off), i) for off in (0, 1) for i in range(CHUNKS)
                    if SCORE_SLOT[i] == slot + 16 * (1 - off) and exists(t.plus(off), N)]

        def products_in(t, slot):
            u, i = (t, slot - PV_LAG) if slot >= PV_LAG else (t.plus(-1), slot - PV_LAG + CHUNKS)
            return [(u, i)] if exists(u, N) else []

        def splits_in(t, slot, pos):
            return [(t.plus(off), half, step) for off in (0, 1) for half in range(2) for step in range(4)
                    if SCORE_SLOT[8 * half + 7] + 1 + step // 3 == slot + 16 * (1 - off) and step % 3 == pos
                    and exists(t.plus(off), N)]

        def finish_in(t, slot, step):
            return [(t.plus(off), j) for off in (0, -1) for j in range(TILES)
                    if 4 * j + plan["steps"][step] == slot - 16 * off and exists(t.plus(off), N)]

        def vector_in(t, slot, pos):
            return [(t.plus(off), j, step) for off in (0, -1) for j in range(TILES) for step, at in plan["dve_steps"].items()
                    if (4 * j + at[0], at[1]) == (slot - 16 * off, pos)
                    and exists(t.plus(off), N)]

        def work_count(u, what, step):
            return banks.number(u, what, step) + 1

        def turned(u, j, back=0):
            v, i = u.plus((j - back) // TILES), (j - back) % TILES
            return work_count(v, "turn_y", i) if exists(v, N) else 0

        def projected(u, i):
            return HALVES * u.u + i + 1

        running = ExitStack()
        block = running.enter_context(nc.Block())

        @block.sync
        def _(sp):
            def load(u):
                if exists(u.plus(-2), N):
                    wait_sp(sp, work_mm, work_count(u.plus(-2), "values", VSTEPS - 1), passed["sp"])
                if conv:
                    sp.dma_start(x_pad[:, u.par, :, 1:L + 1], x_units[u.u]).then_inc(xin_ld[u.par], 16)
                    sp.dma_start(c_pad[:, u.par, :, 1:L + 1], c_units[u.u]).then_inc(xin_ld[u.par], 16)
                else:
                    for kt in range(2):
                        sp.dma_start(xin[:, u.par, kt, :].rearrange("p (b s) -> p b s", b=BU),
                                     xt_units[u.u][:, kt]).then_inc(xin_ld[u.par], 16)
                    if phase == 2:
                        sp.dma_start(craw[:, u.par, :, :], c_units[u.u]).then_inc(xin_ld[u.par], 16)

            def load_pmask(u):
                wait_sp(sp, score_max, CHUNKS * (u.u - 1), passed["sp"])
                sp.dma_start(pmask[:, u.par, :, :].rearrange("p b m -> p (b m)"),
                             mask2_units[u.u].partition_broadcast(P)).then_inc(pmask_ld[u.par], 16)

            def load_resid(u):
                if conv:
                    wait_sp(sp, turn_mm, TILES * (u.u - 1), passed["sp"])
                else:
                    wait_sp(sp, z_done, TILES * (u.u - 1), passed["sp"])
                sp.dma_start(resid[:, u.par, :].rearrange("p (b d) -> p b d", b=BU),
                             res_units[u.u]).then_inc(resid_ld[u.par], 16)

            def fill_stack(u, half):
                wait_sp(sp, att_mm, CHUNKS * (u.u - 2) + 8 * (half + 1) if u.number() not in (0, 1) else 0,
                        passed["sp"])
                wait_sp(sp, split_done, projected(u, HALVES - 1), passed["sp"])
                tokens = slice(2 * half * P, 2 * (half + 1) * P)
                for s, part, sides in FILLS:
                    sp.dma_start(stack[s * D:(s + 1) * D, u.par, side_of(sides), tokens],
                                 parts[:, u.par, GROUPS * sides[0]:GROUPS * (sides[-1] + 1), part, tokens]
                                 ).then_inc(stack_in[u.par][half], 16)

            def store(u):
                wait_sp(sp, y_done, TILES * (u.u + 1), passed["sp"])
                if conv:
                    sp.dma_start(out_cols[u.u], y[:, u.par, :, :]).then_inc(stored[u.par], 16)
                else:
                    sp.dma_start(out_rows[u.u], y[:, u.par, :, :]).then_inc(stored[u.par], 16)
                wait_sp(sp, work_out, turned(u, TILES - 1), passed["sp"])
                if conv:
                    sp.dma_start(out_rows[u.u], y_t[:, u.par, :].rearrange("p (b d) -> p b d", b=BU)
                                 ).then_inc(stored[u.par], 16)
                else:
                    for kt in range(2):
                        sp.dma_start(out_cols[u.u][:, kt],
                                     y_t[:, u.par, kt * TOK:(kt + 1) * TOK].rearrange("p (b s) -> p b s", b=BU)
                                     ).then_inc(stored[u.par], 16)

            def body(t):
                if exists(t.plus(1), N):
                    fill_stack(t.plus(1), 1)
                if phase == 2 and exists(t.plus(2), N):
                    load_pmask(t.plus(2))
                if exists(t.plus(3), N):
                    load(t.plus(3))
                if exists(t.plus(-1), N):
                    store(t.plus(-1))
                if exists(t.plus(1), N):
                    load_resid(t.plus(1))
                if exists(t.plus(2), N):
                    fill_stack(t.plus(2), 0)
                if conv and t.number() == 0:
                    for m, ts in c["weights"].items():
                        for n, w in ts.items():
                            sp.dma_start(w[:, :, :], io[f"{m}_{n}"].rearrange("(k p) n -> p k n", p=P)
                                         ).then_inc(c["weights_in"], 16)

            iterations(sp, N, 3, 1, body)
            STORES = 2 if conv else 3
            for p in range(2):
                sp.wait_ge(stored[p], 16 * STORES * (N // 2))

        @block.tensor
        def _(pe):
            if not conv:
                pe.wait_ge(c["weights_in"], 16 * 8)
            pe.wait_ge(const_ready, 1)

            def context_step(u, i, bank_):
                if i == 0:
                    pe.wait_ge(xin_ld[u.par], 16 * XIN_LOADS * (u.k + 1))
                for j in range(TILES):
                    mm = nc.tensor.transpose(bank_[:, j * P:(j + 1) * P], craw[:, u.par, j, i * P:(i + 1) * P],
                                             c["ident"][:, :])
                mm.then_inc(work_mm, 1)

            def project_step(u, i, bank_, piece, pieces):
                g, side = HALF_SIDE[i]
                if piece == 0:
                    if i == 0 and phase != 2:
                        pe.wait_ge(x_lo, u.u + 1)
                        if u.number() == 0:
                            pe.wait_ge(w_lo, len(w_split))
                    elif side == 1 and g == 0 and phase == 2:
                        pe.wait_ge(work_out, work_count(u, "context", 1))
                taps = 3 if conv else 2
                for tap in range(taps * piece // pieces, taps * (piece + 1) // pieces):
                    for a, b in PRODUCTS if phase != 2 else [(0, 0)]:
                        flags = dict(start=tap == 0 and (a, b) == (0, 0),
                                     stop=tap == taps - 1 and (phase == 2 or (a, b) == PRODUCTS[-1]))
                        if conv:
                            mm = nc.tensor.matmul(bank_[:, :].rearrange("p (b l) -> p b l", b=BU),
                                                  w_split[side][1][:, a, tap, :],
                                                  x_part(side, u.par, b)[:, :, tap:tap + L], **flags)
                        elif phase == 1:
                            mm = nc.tensor.matmul(bank_[:, :], w_split[side][1][:, a, tap, g * P:(g + 1) * P],
                                                  x_part(0, u.par, b)[:, tap, :], **flags)
                        else:
                            mm = nc.tensor.matmul(bank_[:, :], (wq, wk)[side][:, tap, g * P:(g + 1) * P],
                                                  (xin, cin)[side][:, u.par, tap, :], **flags)
                if piece == pieces - 1:
                    mm.then_inc(work_mm, 1)

            def value_step(u, i, bank_, piece, pieces):
                for j in range(2 * piece // pieces, 2 * (piece + 1) // pieces):
                    if conv:
                        for tap in range(3):
                            at = j * P + tap
                            mm = nc.tensor.matmul(bank_[:, j * P:(j + 1) * P], c_pad[:, u.par, i, at:at + P],
                                                  c["conv"]["v"][:, tap, :], start=(tap == 0), stop=(tap == 2))
                    elif phase == 1:
                        at = (2 * i + j) * P
                        for kt in range(2):
                            for a, b in PRODUCTS:
                                mm = nc.tensor.matmul(bank_[:, j * L:(j + 1) * L], x_part(0, u.par, b)[:, kt, at:at + P],
                                                      w_split[2][1][:, a, kt, :], start=(kt, a, b) == (0, 0, 0),
                                                      stop=(kt, a, b) == (1, *PRODUCTS[-1]))
                    else:
                        at = (2 * i + j) * P
                        for kt in range(2):
                            mm = nc.tensor.matmul(bank_[:, j * L:(j + 1) * L], cin[:, u.par, kt, at:at + P],
                                                  wv[:, kt, :], start=(kt == 0), stop=(kt == 1))
                if piece == pieces - 1:
                    mm.then_inc(work_mm, 1)

            def score_step(u, i):
                j, h0 = SCO[i]
                if i % 8 == 0:
                    pe.wait_ge(stack_in[u.par][i // 8], 16 * len(FILLS) * (u.k + 1))
                wait(pe, score_max, CHUNKS * u.u + i - 1)
                first = (j // KT) * KT * P
                for s in range(SH):
                    h = h0 + s
                    mm = nc.tensor.matmul(sbank[i % 2][:, s * KEYS:(s + 1) * KEYS],
                                          stack[0:STACK, u.par, place(0, h), j * P:(j + 1) * P],
                                          stack[0:STACK, u.par, place(1, h), first:first + KEYS], start=True, stop=True)
                mm.then_inc(score_mm, 1)

            def max_turn(u, half, bank_):
                wait_apart(pe, max_split, 2 * u.u + half + 1, passed["pe"])
                for j in range(2):
                    mm = nc.tensor.transpose(bank_[0:3 * H, j * 64:(j + 1) * 64].bitcast(BF16),
                                             max_parts[:, 2 * half + j, :, :].rearrange("p a h -> p (a h)"),
                                             c["identb"][:, :])
                mm.then_inc(work_mm, 1)

            def attend_step(u, i):
                j, q, kt = ATT[i]
                if i % 8 == 0:
                    pe.wait_ge(max_in[i // 8], 16 * (u.u + 1))
                    if u.number() == 0 and i == 0:
                        pe.wait_ge(ones_ready, 2)
                wait(pe, att_exp, CHUNKS * u.u + i - 1)
                key = ((j // KT) * KT + kt) * P
                masked = i in plan["pe_masks"]
                if masked:
                    for part in range(2):
                        mask = c["mask0t_parts"][:, part, kt, (j % 2) * P:(j % 2 + 1) * P]
                        nc.tensor.matmul(tbank[i % 2][:, :].rearrange("p (s l) -> p s l", s=4), c["ident_r"][:, :],
                                         mask.unsqueeze(1).to_broadcast([P, 4, P]), start=part == 0, stop=False)
                for s in range(4):
                    h = 4 * q + s
                    mm = nc.tensor.matmul(tbank[i % 2][:, s * P:(s + 1) * P],
                                          stack[0:STACKED, u.par, place(1, h), key:key + P],
                                          stack[0:STACKED, u.par, place(0, h), j * P:(j + 1) * P],
                                          start=not masked, stop=not masked or s == 3)
                mm.then_inc(att_mm, 1)

            def pv_step(u, i):
                j, q, kt = ATT[i]
                if i == 0:
                    pe.wait_ge(work_out, work_count(u, "values", VSTEPS - 1))
                if i % 4 == 0:
                    wait(pe, heads_done, TILES * u.u + j)
                pe.wait_ge(att_exp, CHUNKS * u.u + i + 1)
                for s in range(4):
                    mm = nc.tensor.matmul(pvbank[32 * s:32 * s + 32, q * P:(q + 1) * P],
                                          vals[:, u.par, (j // KT) * KT + kt, 4 * q + s, :],
                                          probs[:, i % 4, s * P:(s + 1) * P], start=(kt == 0), stop=(kt == KT - 1),
                                          tile_position=(0, 32 * s))
                mm.then_inc(att_pv, 1)

            def turn_heads(u, j):
                n = TILES * u.u + j
                pe.wait_ge(heads_done, n + 1)
                wait(pe, z_done, n)
                if conv and j == 0:
                    pe.wait_ge(resid_ld[u.par], 16 * (u.k + 1))
                for q in range(QUADS):
                    mm = nc.tensor.transpose(fbank[:, q * P:(q + 1) * P], heads_out[:, j % 2, q * P:(q + 1) * P],
                                             c["ident"][:, :])
                if conv:
                    mm = nc.tensor.transpose(fbank[:, 2 * P:3 * P], resid[:, u.par, j * P:(j + 1) * P], c["ident"][:, :])
                mm.then_inc(turn_mm, 1)

            def turn_merged(u, j):
                pe.wait_ge(merged_done, TILES * u.u + j + 1)
                for a in range(2):
                    mm = nc.tensor.transpose(fbank[:, a * P:(a + 1) * P], merged[:, a * P:(a + 1) * P], c["ident"][:, :])
                mm.then_inc(mt_mm, 1)

            def output_step(u, j):
                pe.wait_ge(mt_out, TILES * u.u + j + 1)
                for a in range(2):
                    mm = nc.tensor.matmul(fbank[:, 0:L], merged_t[:, a, :], wo[:, a, :], start=(a == 0), stop=(a == 1))
                mm.then_inc(out_mm, 1)

            def turn_y(u, j, bank_):
                pe.wait_ge(normed, TILES * u.u + j + 1)
                for a in range(W // P):
                    mm = nc.tensor.transpose(bank_[:, a * P:(a + 1) * P], z[:, j % 2, a * P:(a + 1) * P],
                                             c["ident"][:, :])
                mm.then_inc(work_mm, 1)

            def body(t):
                for slot in range(16):
                    if exists(t, N):
                        attend_step(t, slot)
                    for at in products_in(t, slot):
                        pv_step(*at)
                    for u, i in scores_in(t, slot):
                        score_step(u, i)
                    for u, what, step, piece, pieces in banks.in_slot(t, slot):
                        bank_ = work[banks.bank(what, step)]
                        if piece == 0:
                            wait(pe, work_out, banks.free(u, what, step))
                        if what == "project":
                            project_step(u, step, bank_, piece, pieces)
                        elif what == "values":
                            value_step(u, step, bank_, piece, pieces)
                        elif what == "context":
                            context_step(u, step, bank_)
                        elif what == "max":
                            max_turn(u, step, bank_)
                        else:
                            turn_y(u, step, bank_)
                    if not conv:
                        for at in finish_in(t, slot, "output"):
                            output_step(*at)
                        for at in finish_in(t, slot, "turn_merged"):
                            turn_merged(*at)
                    for at in finish_in(t, slot, "turn"):
                        turn_heads(*at)

            iterations(pe, N, 2, 1, body)

        @block.scalar
        def _(act):
            def context_out(u, i, bank_):
                nc.scalar.activation(cin[:, u.par, i, :], bank_[:, :], ACT.Copy).then_inc(work_out, 1)

            def project_out(u, i, bank_):
                g, side = HALF_SIDE[i]
                wait(act, split_done, projected(u, i) - 2)
                if i == 0:
                    for half in range(2):
                        wait(act, stack_in[u.par][half], 16 * len(FILLS) * u.k)
                args = {"scale": SCALE if side == 0 else 1.0}
                if not conv:
                    args["bias"] = ((c["bq"], c["bk"])[side])[name][:, g:g + 1]
                for out in (yproj[:, i % 2, :], parts[:, u.par, i, HI, :]):
                    last = nc.scalar.activation(out, bank_[:, :], ACT.Identity, **args)
                last.then_inc(work_out, 1)

            def value_out(u, i, bank_):
                if i == 0:
                    wait(act, att_pv, CHUNKS * (u.u - 1))
                nc.scalar.activation(vals[:, u.par, 2 * i:2 * i + 2, :, 0:D],
                                     bank_[:, 0:2 * H * D].rearrange("p (j h d) -> p j h d", j=2, d=D), ACT.Copy
                                     ).then_inc(work_out, 1)

            def max_rows_out(u, half, bank_):
                if half == 1:
                    act.wait_ge(max_in[0], 16 * (u.u + 1))
                else:
                    wait(act, max_in[1], 16 * u.u)
                nc.scalar.activation(max_rows[:, :], bank_[0:3 * H, 0:P].bitcast(BF16), ACT.Copy).then_inc(work_out, 1)
                act.wait_ge(work_out, work_count(u, "max", half))
                act.dma_start(stack[STACK:STACKED, u.par, side_of((0,)), 2 * half * P:2 * (half + 1) * P], max_rows[:, :]
                              ).then_inc(max_in[half], 16)

            def exp_step(u, i):
                wait(act, att_pv, CHUNKS * u.u + i - 3)
                if phase == 2:
                    wait_apart(act, att_mm, CHUNKS * u.u + i + 1, passed["act"])
                elif i in plan["pe_masks"]:
                    act.wait_ge(att_mm, CHUNKS * u.u + i + 1)
                else:
                    act.wait_ge(att_masked, len(DVE_MASKS) * u.u + DVE_MASKS.index(i) + 1)
                if phase == 2:
                    b = TILES * u.u + ATT[i][0]
                    ins = nc.scalar.activation(probs[:, i % 4, :], tbank[i % 2][:, :], ACT.Exp,
                                               bias=c["pad_bias"][:, bass.ds(b, 1)])
                else:
                    ins = nc.scalar.activation(probs[:, i % 4, :], tbank[i % 2][:, :], ACT.Exp)
                ins.then_inc(att_exp, 1)

            def heads_copy(u, j):
                act.wait_ge(att_pv, CHUNKS * u.u + 4 * j + 4)
                wait(act, turn_mm, TILES * u.u + j - 1)
                nc.scalar.activation(heads_out[:, j % 2, :], pvbank[:, 0:QUADS * P], ACT.Copy
                                     ).then_inc(heads_done, 1)

            def merged_out(u, j):
                act.wait_ge(mt_mm, TILES * u.u + j + 1)
                nc.scalar.activation(merged_t[:, :, :], fbank[:, 0:2 * P].rearrange("p (a s) -> p a s", a=2), ACT.Copy
                                     ).then_inc(mt_out, 1)

            def y_out(u, j, bank_):
                if j == 0:
                    wait(act, stored[u.par], 16 * (2 if conv else 3) * u.k)
                for a in range(W // P):
                    last = nc.scalar.activation(y_t[:, u.par, a * TOK + j * P:a * TOK + (j + 1) * P],
                                                bank_[:, a * P:(a + 1) * P], ACT.Identity,
                                                scale=ln_gc[:, a:a + 1], bias=ln_bc[:, a:a + 1])
                last.then_inc(work_out, 1)

            def round_x(u):
                if conv:
                    act.wait_ge(padded, u.u + 1)
                else:
                    act.wait_ge(xin_ld[u.par], 16 * XIN_LOADS * (u.k + 1))
                if exists(u.plus(-2), N):
                    act.wait_ge(work_mm, work_count(u.plus(-2), "values", VSTEPS - 1))
                for n, x in enumerate(raw):
                    last = nc.scalar.activation(x_part(n, u.par, 0), x[:, u.par, :, :], ACT.Copy)
                last.then_inc(x_hi, 1)

            def mid_part(u, i):
                act.wait_ge(rest_step, HALVES * u.u + i + 1)
                nc.scalar.activation(parts[:, u.par, i, MID, :], yproj[:, i % 2, :], ACT.Copy).then_inc(mid_done, 1)

            def normalise(u, j):
                r = j % 2
                act.wait_ge(rstd_done, 3 * (TILES * u.u + j + 1))
                nc.scalar.activation(z[:, r, :], z[:, r, :], ACT.Identity, scale=rstd[:, r, 0:1], bias=shift[:, r, 0:1]
                                     ).then_inc(normed, 1)

            def body(t):
                for slot in range(16):
                    for u, i in products_in(t, slot):
                        if i % 4 == 3:
                            heads_copy(u, i // 4)
                    if exists(t, N):
                        exp_step(t, slot)
                    if phase != 2:
                        for at in finish_in(t, slot, "normalise"):
                            normalise(*at)
                    if not conv:
                        for at in finish_in(t, slot, "turn_merged"):
                            merged_out(*at)
                    if phase != 2 and slot - 1 in P_SLOT and exists(t.plus(2), N):
                        mid_part(t.plus(2), P_SLOT.index(slot - 1))
                    for u, what, step, piece, pieces in banks.in_slot(t, slot):
                        if piece == pieces - 1:
                            bank_ = work[banks.bank(what, step)]
                            act.wait_ge(work_mm, work_count(u, what, step))
                            {"project": project_out, "values": value_out, "context": context_out,
                             "max": max_rows_out, "turn_y": y_out}[what](u, step, bank_)
                    if slot == SPLIT_SLOT and phase != 2 and exists(t.plus(3), N):
                        round_x(t.plus(3))
            if phase == 1:
                act.wait_ge(c["weights_in"], 16 * 8)
            for w, w_parts in w_split:
                nc.scalar.activation(w_parts[:, 0, :, :], w[:, :, :], ACT.Copy).then_inc(w_hi, 1)
            iterations(act, N, 3, 1, body)

        @block.vector
        def _(dve):
            nc.vector.memset(vals[:, :, :, :, D:32], 0.0).then_inc(max_step, 1)
            dve.wait_ge(max_step, 1)
            nc.vector.memset(vals[:, :, :, :, D:D + 1], 1.0).then_inc(const_ready, 1)
            for p in range(2):
                nc.vector.memset(stack[STACK:STACKED, p, side_of((1,)), :], 1.0).then_inc(ones_ready, 1)
            for i, (w, w_parts) in enumerate(w_split):
                dve.wait_ge(w_hi, i + 1)
                nc.vector.tensor_tensor(w_parts[:, 1, :, :], w[:, :, :], w_parts[:, 0, :, :], ALU.subtract
                                        ).then_inc(w_lo, 1)

            def max_of(u, i, piece):
                j, h0 = SCO[i]
                if phase == 2 and i == 0 and piece == 0:
                    dve.wait_ge(pmask_ready, u.u + 1)
                if piece == 0:
                    wait(dve, score_max, CHUNKS * u.u + i - 1)
                    wait_apart(dve, score_mm, CHUNKS * u.u + i + 1, passed["dve"])
                mask = c["mask0"][:, j % 2, :] if conv else (c["mask1"][:, :] if phase == 1 else pmask[:, u.par, j, :])
                for s in range(piece * SH // 2, (piece + 1) * SH // 2):
                    cols = slice(s * KEYS, (s + 1) * KEYS)
                    h = h0 + s
                    col = (h % 8) * GROUPS + h // 8
                    ins = nc.vector.tensor_tensor_reduce(
                        out=junk[:, i % 2, cols], in0=sbank[i % 2][:, cols], in1=mask, scale=1.0, scalar=LOWEST,
                        op0=ALU.add, op1=ALU.max, accum_out=maxes[:, j, col:col + 1])
                if piece == 1:
                    ins.then_inc(score_max, 1)

            def split_max(u, half, step):
                done = 3 * (2 * u.u + half) + 1
                m, rest = maxes[:, 2 * half:2 * half + 2, :], max_rest[:, 2 * half:2 * half + 2, :]
                hi, mid, lo = (max_parts[:, 2 * half:2 * half + 2, part, :] for part in range(3))
                if step == 0:
                    dve.wait_ge(score_max, CHUNKS * u.u + 8 * half + 8)
                    if exists(u.plus(-1), N):
                        dve.wait_ge(work_mm, work_count(u.plus(-1), "max", half))
                    nc.vector.tensor_scalar(hi, m, -1.0, None, ALU.mult).then_inc(max_step, 1)
                else:
                    dve.wait_ge(max_step, done + step)
                if step == 1:
                    nc.vector.scalar_tensor_tensor(out=rest, in0=m, scalar=-1.0, in1=hi, op0=ALU.mult,
                                                   op1=ALU.subtract).then_inc(max_step, 1)
                elif step == 2:
                    nc.vector.tensor_copy(mid, rest).then_inc(max_step, 1)
                elif step == 3:
                    nc.vector.tensor_tensor(lo, rest, mid, ALU.subtract).then_inc(max_split, 1)

            def mask_scores(u, i):
                j, q, kt = ATT[i]
                dve.wait_ge(att_mm, CHUNKS * u.u + i + 1)
                if conv:
                    l0 = (j % 2) * P
                    mask = c["mask0t"][:, kt, l0:l0 + P]
                else:
                    mask = c["mask1t"][:, :]
                bank_ = tbank[i % 2][:, :].rearrange("p (s l) -> p s l", s=4)
                nc.vector.tensor_tensor(bank_, bank_, mask.unsqueeze(1).to_broadcast([P, 4, P]), ALU.add
                                        ).then_inc(att_masked, 1)

            def mid_part(u, i):
                dve.wait_ge(rest_step, HALVES * u.u + i + 1)
                nc.vector.tensor_copy(parts[:, u.par, i, MID, :], yproj[:, i % 2, :]).then_inc(mid_done, 1)

            def normalise(u, j):
                r = j % 2
                dve.wait_ge(rstd_done, TILES * u.u + j + 1)
                nc.vector.tensor_scalar(z[:, r, :], z[:, r, :], moments[:, r, 0:1], rstd[:, r, 0:1],
                                        ALU.subtract, ALU.mult).then_inc(normed, 1)

            def recip(u, j):
                heads = fbank[:, 0:QUADS * P].rearrange("p (h e) -> p h e", e=32)
                dve.wait_ge(turn_mm, TILES * u.u + j + 1)
                nc.vector.reciprocal(recips[:, :].unsqueeze(2), heads[:, :, D:D + 1]).then_inc(recip_done, 1)

            def merge(u, j):
                n = TILES * u.u + j
                heads = fbank[:, 0:QUADS * P].rearrange("p (h e) -> p h e", e=32)
                dve.wait_ge(recip_done, n + 1)
                nc.vector.tensor_tensor(merged[:, :].rearrange("p (h d) -> p h d", d=D), heads[:, :, 0:D],
                                        recips[:, :].unsqueeze(2).to_broadcast([P, H, D]), ALU.mult
                                        ).then_inc(merged_done, 1)

            def add(u, j):
                n = TILES * u.u + j
                wait(dve, work_mm, turned(u, j, 2))
                wait(dve, scaled, n - 1)
                if conv:
                    dve.wait_ge(merged_done, n + 1)
                    ins = nc.vector.tensor_tensor(z[:, j % 2, :], fbank[:, 2 * P:3 * P], merged[:, :], ALU.add)
                else:
                    dve.wait_ge(out_mm, n + 1)
                    if j == 0:
                        dve.wait_ge(resid_ready, u.u + 1)
                    ins = nc.vector.tensor_tensor(z[:, j % 2, :], fbank[:, 0:W], resid[:, u.par, j * W:(j + 1) * W],
                                                  ALU.add)
                ins.then_inc(z_done, 1)

            def stats_of(u, j):
                dve.wait_ge(z_done, TILES * u.u + j + 1)
                nc.vector.bn_stats(stats[:, j % 2, :], z[:, j % 2, :]).then_inc(stats_done, 1)

            def moments_of(u, j):
                wait_apart(dve, stats_done, TILES * u.u + j + 1, passed["dve"])
                nc.vector.bn_aggr(moments[:, j % 2, :], stats[:, j % 2, :]).then_inc(moments_done, 1)

            def epsilon(u, j):
                dve.wait_ge(moments_done, TILES * u.u + j + 1)
                var = moments[:, j % 2, 1:2]
                nc.vector.tensor_scalar(var, var, EPS, None, ALU.add).then_inc(var_done, 1)

            STEP = {"recip": recip, "merge": merge, "add": add, "stats": stats_of, "moments": moments_of,
                    "epsilon": epsilon}

            def body(t):
                for slot in range(16):
                    if exists(t, N) and slot in DVE_MASKS:
                        mask_scores(t, slot)
                    for pos in range(3):
                        for at in splits_in(t, slot, pos):
                            split_max(*at)
                        for u, j, step in vector_in(t, slot, pos):
                            STEP[step](u, j)
                        if pos < 2:
                            for u, i in scores_in(t, slot):
                                max_of(u, i, pos)
                    if phase == 2:
                        for at in finish_in(t, slot, "normalise"):
                            normalise(*at)
                        if slot - 1 in P_SLOT and exists(t.plus(2), N):
                            mid_part(t.plus(2), P_SLOT.index(slot - 1))

            iterations(dve, N, 2, 1, body)

        @block.gpsimd
        def _(pool):
            def pad_edges(u):
                wait_apart(pool, xin_ld[u.par], 16 * XIN_LOADS * (u.k + 1), passed["pool"])
                for buf in (x_pad, c_pad):
                    ins = nc.gpsimd.tensor_copy(buf[:, u.par, :, 0:L + 2:L + 1], buf[:, u.par, :, 2:L:L - 3])
                ins.then_inc(padded, 1)

            def rest_of_x(u):
                pool.wait_ge(x_hi, u.u + 1)
                for n, x in enumerate(raw):
                    ins = nc.gpsimd.tensor_tensor(x_part(n, u.par, 1), x[:, u.par, :, :], x_part(n, u.par, 0), ALU.subtract)
                ins.then_inc(x_lo, 1)

            def add_bias(u):
                pool.wait_ge(resid_ld[u.par], 16 * (u.k + 1))
                r = resid[:, u.par, :].rearrange("p (b d) -> p b d", b=TILES)
                nc.gpsimd.tensor_tensor(r, r, bo[:, :].unsqueeze(1).to_broadcast([P, TILES, L]), ALU.add
                                        ).then_inc(resid_ready, 1)

            def scale_pmask(u):
                wait_apart(pool, pmask_ld[u.par], 16 * (u.k + 1), passed["pool"])
                m = pmask[:, u.par, :, :]
                nc.gpsimd.tensor_scalar(m, m, MASKED, None, ALU.mult).then_inc(pmask_ready, 1)

            def first_rest(u, i):
                n = HALVES * u.u + i
                pool.wait_ge(work_out, work_count(u, "project", i))
                rest = yproj[:, i % 2, :]
                nc.gpsimd.tensor_tensor(rest, rest, parts[:, u.par, i, HI, :], ALU.subtract).then_inc(rest_step, 1)

            def low_part(u, i):
                n = HALVES * u.u + i
                rest = yproj[:, i % 2, :]
                pool.wait_ge(mid_done, n + 1)
                nc.gpsimd.tensor_tensor(parts[:, u.par, i, LO, :], rest, parts[:, u.par, i, MID, :], ALU.subtract
                                        ).then_inc(split_done, 1)

            def power(u, j):
                n = TILES * u.u + j
                r = j % 2
                if phase == 2:
                    pool.wait_ge(var_done, n + 1)
                    nc.gpsimd.tensor_tensor(rstd[:, r, :], moments[:, r, 1:2], c["minus_half"][:, :], ALU.pow
                                            ).then_inc(rstd_done, 1)
                    return
                wait_apart(pool, var_done, n + 1, passed["pool"])
                nc.gpsimd.tensor_scalar(shift[:, r, :], moments[:, r, 0:1], -1.0, None, ALU.mult
                                        ).then_inc(rstd_done, 1)
                nc.gpsimd.tensor_tensor(rstd[:, r, :], moments[:, r, 1:2], c["minus_half"][:, :], ALU.pow
                                        ).then_inc(rstd_done, 1)
                pool.wait_ge(rstd_done, 3 * n + 2)
                nc.gpsimd.tensor_tensor(shift[:, r, :], shift[:, r, :], rstd[:, r, :], ALU.mult
                                        ).then_inc(rstd_done, 1)

            def affine(u, j):
                n = TILES * u.u + j
                row = y[:, u.par, j, :]
                if j == 0:
                    wait(pool, stored[u.par], 16 * (2 if conv else 3) * u.k)
                pool.wait_ge(normed, n + 1)
                nc.gpsimd.tensor_tensor(row, z[:, j % 2, :], ln_g[:, 0:W], ALU.mult).then_inc(scaled, 1)
                pool.wait_ge(scaled, n + 1)
                nc.gpsimd.tensor_tensor(row, row, ln_b[:, 0:W], ALU.add).then_inc(y_done, 1)

            def body(t):
                if not conv and exists(t, N):
                    add_bias(t)
                for slot in range(16):
                    for pos in range(3):
                        for u, j, step in vector_in(t, slot, pos):
                            if step == "epsilon":
                                power(u, j)
                    if slot in P_SLOT and exists(t.plus(2), N):
                        first_rest(t.plus(2), P_SLOT.index(slot))
                    if slot - 1 in P_SLOT and exists(t.plus(2), N):
                        low_part(t.plus(2), P_SLOT.index(slot - 1))
                    for at in finish_in(t, slot, "normalise"):
                        affine(*at)
                    if slot == 15 and phase == 2 and exists(t.plus(2), N):
                        scale_pmask(t.plus(2))
                    if conv and slot == SPLIT_SLOT - 1 and exists(t.plus(3), N):
                        pad_edges(t.plus(3))
                    if slot == SPLIT_SLOT and phase != 2 and exists(t.plus(3), N):
                        rest_of_x(t.plus(3))

            iterations(pool, N, 3, 1, body)

        running.close()
        reset(nc, sems)


def feed_forward(nc, top, c, io):
    NB, _, L = io["x"].shape
    F = io["ffn_w1"].shape[1]
    FT = F // P
    N = NB // TILES
    EPS = 1e-6
    with ExitStack() as ctx:
        def sb(n, shape, dt=F32):
            return ctx.enter_context(nc.sbuf_tensor(f"ffn_{n}", shape, dt))

        def sem(n):
            return ctx.enter_context(nc.semaphore(f"ffn_{n}"))

        w1, w2 = sb("w1", [P, 2, F]), sb("w2", [P, FT, L])
        w1_parts, w2_parts = sb("w1_parts", [P, 2, 2, F], F32R), sb("w2_parts", [P, 2, FT, L], F32R)
        xin = sb("xin", [P, 2, 2, TOK])
        x_parts = sb("x_parts", [P, 2, 2, 2, TOK], F32R)
        resid = sb("resid", [P, 2, TILES, L])
        hidden = sb("hidden", [P, 2, TOK])
        hidden_parts = sb("hidden_parts", [P, 2, 2, FT, TOK], F32R)
        z = sb("z", [P, 2, L])
        stats, moments, rstd = sb("stats", [P, 2, 6]), sb("moments", [P, 2, 2]), sb("rstd", [P, 2, 1])
        y = sb("y", [P, 2, TILES, L])
        hbank = [ctx.enter_context(nc.psum_tensor(f"ffn_h{i}", [P, 512], F32)) for i in range(4)]
        obank = [ctx.enter_context(nc.psum_tensor(f"ffn_o{i}", [P, 512], F32)) for i in range(4)]
        w_in = [sem(f"w_in{i}") for i in range(2)]
        weights_hi, weights_lo = sem("weights_hi"), sem("weights_lo")
        xin_ld = [sem(f"xin_ld{i}") for i in range(2)]
        x_hi, x_lo = sem("x_hi"), sem("x_lo")
        resid_ld = [sem(f"resid_ld{i}") for i in range(2)]
        resid_ready = sem("resid_ready")
        h_mm, h_out, h_split = sem("h_mm"), sem("h_out"), sem("h_split")
        o_mm = sem("o_mm")
        z_done, stats_done, moments_done, var_done, rstd_done = (
            sem("z_done"), sem("stats_done"), sem("moments_done"), sem("var_done"), sem("rstd_done"))
        normed, scaled, y_done = sem("normed"), sem("scaled"), sem("y_done")
        passed, passed_sp = sem("passed_dve"), sem("passed_sp")
        stored = [sem(f"stored{i}") for i in range(2)]
        xt_units = io["o2t"].rearrange("(u b) k p s -> u p k b s", b=TILES)
        res_units = io["o2"].rearrange("(u b) s d -> u s b d", b=TILES)
        out_units = io["out"].rearrange("(u b) s d -> u s b d", b=TILES)
        block = ctx.enter_context(nc.Block())

        @block.sync
        def _(sp):
            sp.dma_start(w1[:, :, :], io["ffn_w1"].rearrange("(k p) n -> p k n", p=P)).then_inc(w_in[0], 16)

            def body(t):
                u = t.plus(2)
                if exists(u, N):
                    wait_sp(sp, x_lo, u.u - 1, passed_sp)
                    for kt in range(2):
                        sp.dma_start(xin[:, u.par, kt, :].rearrange("p (b s) -> p b s", b=TILES),
                                     xt_units[u.u][:, kt]).then_inc(xin_ld[u.par], 16)
                if t.number() == -2:
                    sp.dma_start(w2[:, :, :], io["ffn_w2"].rearrange("(k p) n -> p k n", p=P)).then_inc(w_in[1], 16)
                u = t.plus(-2)
                if exists(u, N):
                    wait_sp(sp, y_done, TILES * (u.u + 1), passed_sp)
                    sp.dma_start(out_units[u.u], y[:, u.par, :, :]).then_inc(stored[u.par], 16)
                if exists(t, N):
                    wait_sp(sp, z_done, TILES * (t.u - 1), passed_sp)
                    sp.dma_start(resid[:, t.par, :, :], res_units[t.u]).then_inc(resid_ld[t.par], 16)

            iterations(sp, N, 2, 2, body)
            for p in range(2):
                sp.wait_ge(stored[p], 16 * (N // 2))

        @block.tensor
        def _(pe):
            pe.wait_ge(weights_lo, 1)
            def hidden_tile(u, f):
                if f == 0:
                    pe.wait_ge(x_lo, u.u + 1)
                wait(pe, h_split, FT * u.u + f - 3)
                for i, (kt, (a, b)) in enumerate((kt, ab) for kt in range(2) for ab in PRODUCTS):
                    mm = nc.tensor.matmul(hbank[f % 4][:, :], w1_parts[:, a, kt, f * P:(f + 1) * P],
                                          x_parts[:, u.par, b, kt, :], start=(i == 0), stop=(i == 5))
                mm.then_inc(h_mm, 1)

            def output_tile(u, j):
                if u.number() != 0:
                    pe.wait_ge(z_done, TILES * (u.u - 1) + j + 1)
                elif j == 0:
                    pe.wait_ge(weights_lo, 2)
                if j == 0:
                    pe.wait_ge(h_split, FT * (u.u + 1))
                for f in range(FT):
                    for i, (a, b) in enumerate(PRODUCTS):
                        mm = nc.tensor.matmul(obank[j][:, 0:L], hidden_parts[:, u.par, b, f, j * P:(j + 1) * P],
                                              w2_parts[:, a, f, :], start=(f == 0 and i == 0),
                                              stop=(f == FT - 1 and i == 2))
                mm.then_inc(o_mm, 1)

            def body(t):
                for f in range(FT):
                    if exists(t, N):
                        hidden_tile(t, f)
                    if f % 2 == 1 and exists(t.plus(-1), N):
                        output_tile(t.plus(-1), f // 2)

            iterations(pe, N, 0, 1, body)

        @block.scalar
        def _(act):
            def split_x(u):
                wait(act, h_mm, FT * (u.u - 1))
                act.wait_ge(xin_ld[u.par], 32 * (u.k + 1))
                nc.scalar.activation(x_parts[:, u.par, 0, :, :], xin[:, u.par, :, :], ACT.Copy).then_inc(x_hi, 1)

            def body(t):
                if exists(t.plus(1), N):
                    split_x(t.plus(1))
                if not exists(t, N):
                    round_weights(1)
                    return
                wait(act, o_mm, TILES * (t.u - 1))
                for f in range(FT):
                    n = FT * t.u + f
                    wait(act, h_split, n - 1)
                    act.wait_ge(h_mm, n + 1)
                    for out in (hidden[:, f % 2, :], hidden_parts[:, t.par, 0, f, :]):
                        last = nc.scalar.activation(out, hbank[f % 4][:, :], ACT.Relu, bias=c["ffn_b1_s"][:, f:f + 1])
                    last.then_inc(h_out, 1)

            def round_weights(i):
                w, w_parts = ((w1, w1_parts), (w2, w2_parts))[i]
                act.wait_ge(w_in[i], 16)
                nc.scalar.activation(w_parts[:, 0, :, :], w[:, :, :], ACT.Copy).then_inc(weights_hi, 1)

            round_weights(0)
            iterations(act, N, 1, 0, body)

        @block.vector
        def _(dve):
            def split_x(u):
                dve.wait_ge(x_hi, u.u + 1)
                nc.vector.tensor_tensor(x_parts[:, u.par, 1, :, :], xin[:, u.par, :, :], x_parts[:, u.par, 0, :, :],
                                        ALU.subtract).then_inc(x_lo, 1)

            def split_hidden(u, f):
                dve.wait_ge(h_out, FT * u.u + f + 1)
                nc.vector.tensor_tensor(hidden_parts[:, u.par, 1, f, :], hidden[:, f % 2, :],
                                        hidden_parts[:, u.par, 0, f, :], ALU.subtract).then_inc(h_split, 1)

            def add(u, j):
                n = TILES * u.u + j
                if j == 0:
                    dve.wait_ge(resid_ready, u.u + 1)
                wait(dve, scaled, n - 1)
                dve.wait_ge(o_mm, n + 1)
                nc.vector.tensor_tensor(z[:, j % 2, :], obank[j][:, 0:L], resid[:, u.par, j, :], ALU.add
                                        ).then_inc(z_done, 1)

            def moments_of(u, j):
                n = TILES * u.u + j
                r = j % 2
                dve.wait_ge(z_done, n + 1)
                nc.vector.bn_stats(stats[:, r, :], z[:, r, :]).then_inc(stats_done, 1)
                wait_apart(dve, stats_done, n + 1, passed)
                nc.vector.bn_aggr(moments[:, r, :], stats[:, r, :]).then_inc(moments_done, 1)
                dve.wait_ge(moments_done, n + 1)
                nc.vector.tensor_scalar(moments[:, r, 1:2], moments[:, r, 1:2], EPS, None, ALU.add
                                        ).then_inc(var_done, 1)

            def normalise(u, j):
                r = j % 2
                dve.wait_ge(rstd_done, TILES * u.u + j + 1)
                nc.vector.tensor_scalar(z[:, r, :], z[:, r, :], moments[:, r, 0:1], rstd[:, r, 0:1],
                                        ALU.subtract, ALU.mult).then_inc(normed, 1)

            def body(t):
                if t.number() == 0:
                    rest_of_weights(1)
                for f in range(FT):
                    if exists(t, N):
                        split_hidden(t, f)
                    if f == 1 and exists(t.plus(1), N):
                        split_x(t.plus(1))
                    u, j = (t.plus(-1), f // 2 - 1) if f >= 2 else (t.plus(-2), TILES - 1)
                    if exists(u, N) and f % 2 == 0:
                        add(u, j)
                        moments_of(u, j)
                    elif exists(u, N):
                        normalise(u, j)

            def rest_of_weights(i):
                w, w_parts = ((w1, w1_parts), (w2, w2_parts))[i]
                dve.wait_ge(weights_hi, i + 1)
                nc.vector.tensor_tensor(w_parts[:, 1, :, :], w[:, :, :], w_parts[:, 0, :, :], ALU.subtract
                                        ).then_inc(weights_lo, 1)

            rest_of_weights(0)
            iterations(dve, N, 1, 2, body)

        @block.gpsimd
        def _(pool):
            def add_bias(u):
                pool.wait_ge(resid_ld[u.par], 16 * (u.k + 1))
                nc.gpsimd.tensor_tensor(resid[:, u.par, :, :], resid[:, u.par, :, :],
                                        c["ffn_b2"][:, :].unsqueeze(1).to_broadcast([P, TILES, L]), ALU.add
                                        ).then_inc(resid_ready, 1)

            def body(t):
                for j in range(TILES):
                    if j == 2 and exists(t.plus(1), N):
                        add_bias(t.plus(1))
                    n = TILES * t.u + j
                    r = j % 2
                    row = y[:, t.par, j, :]
                    pool.wait_ge(var_done, n + 1)
                    nc.gpsimd.tensor_tensor(rstd[:, r, :], moments[:, r, 1:2], c["minus_half"][:, :], ALU.pow
                                            ).then_inc(rstd_done, 1)
                    if j == 0:
                        wait(pool, stored[t.par], 16 * t.k)
                    pool.wait_ge(normed, n + 1)
                    nc.gpsimd.tensor_tensor(row, z[:, r, :], c["ln3_g"][:, :], ALU.mult).then_inc(scaled, 1)
                    pool.wait_ge(scaled, n + 1)
                    nc.gpsimd.tensor_tensor(row, row, c["ln3_b"][:, :], ALU.add).then_inc(y_done, 1)

            add_bias(Unit(0, 0))
            iterations(pool, N, 1, 0, lambda t: body(t) if exists(t, N) else None)


def build(nc, io):
    with ExitStack() as top:
        c = {}
        with ExitStack() as l0:
            constants(nc, top, l0, io, c)
            attention(nc, top, c, io, 0)
        attention(nc, top, c, io, 1)
        attention(nc, top, c, io, 2)
        feed_forward(nc, top, c, io)


def _laid_out(inputs):
    import numpy as np

    a = {k: np.asarray(v) for k, v in inputs.items()}
    out = {"x": a["x"], "ctx": a["ctx_1024"], "mask0": a["L0_xattn_mask"], "mask1": a["mask_1x1xSxS2_fk1"],
           "mask2": a["mask_Bx1x1xS2_fk0"], "gamma": a["L0_xattn_gamma"], "beta": a["L0_xattn_beta"]}
    for n in "qkv":
        out[f"conv_{n}"] = a[f"L0_xattn_w{n}"].reshape(8, 16, 16, 3).transpose(0, 2, 3, 1)
    for m in ("mha1", "mha2"):
        for n in "qk":
            out[f"{m}_w{n}"] = a[f"L1_xattn_{m}_w{n}"].reshape(256, 2, 8, 16).transpose(0, 1, 3, 2).reshape(256, 256)
            out[f"{m}_b{n}"] = a[f"L1_xattn_{m}_b{n}"].reshape(2, 8, 16).transpose(2, 1, 0).reshape(128, 2)
        out[f"{m}_wv"], out[f"{m}_wo"] = a[f"L1_xattn_{m}_wv"], a[f"L1_xattn_{m}_wo"]
        out[f"{m}_bv"] = a[f"L1_xattn_{m}_bv"].reshape(2, 128).T
        out[f"{m}_bo"] = a[f"L1_xattn_{m}_bo"]
    out["ffn_w1"], out["ffn_w2"], out["ffn_b2"] = (a[f"L1_xattn_ffn_{n}"] for n in ("w1", "w2", "b2"))
    out["ffn_b1"] = a["L1_xattn_ffn_b1"].reshape(8, 128).T
    for i in (1, 2, 3):
        for n in "gb":
            out[f"ln{i}_{n}"] = a[f"L1_xattn_ln{i}_{n}"]
    for i in (1, 2):
        for n in "gb":
            out[f"ln{i}_{n}c"] = out[f"ln{i}_{n}"].reshape(2, 128).T
    out["g0_col"], out["b0_col"] = out["gamma"].reshape(128, 1), out["beta"].reshape(128, 1)
    return {k: np.ascontiguousarray(v) for k, v in out.items()}


def kernel(**inputs):
    import concourse.bacc as bacc
    from concourse.bass_utils import run_bass_kernel_spmd

    nc = bacc.Bacc("TRN2", target_bir_lowering=False, num_devices=1)
    arrays, io = {}, {}
    for name, a in _laid_out(inputs).items():
        arrays[f"in_{name}"] = a
        io[name] = nc.dram_tensor(f"in_{name}", a.shape, mybir.dt.from_np(a.dtype), kind="ExternalInput").ap()
    NB, S, L = arrays["in_x"].shape
    for name in ("x1", "o1", "o2"):
        io[name] = nc.dram_tensor(f"rows_{name}", (NB, S, L), F32, kind="Internal").ap()
        io[f"{name}t"] = nc.dram_tensor(f"cols_{name}", (NB, 2, P, S), F32, kind="Internal").ap()
    io["out"] = nc.dram_tensor("out_0", (NB, S, L), F32, kind="ExternalOutput").ap()
    build(nc, io)
    r = run_bass_kernel_spmd(nc, [arrays], core_ids=[0])
    return r.results[0]["out_0"]
```
